# Optimizing a Trainium2 kernel written in Bass

```python
import numpy as np
import jax
import jax.numpy as jnp

def _softmax(x, axis=-1):
    return jax.nn.softmax(x, axis=axis)

def _gelu(x):
    return jax.nn.gelu(x, approximate=True)

def _silu(x):
    return jax.nn.silu(x)

def _sigmoid(x):
    return jax.nn.sigmoid(x)

def _layernorm(x, axis=-1, eps=1e-05):
    m = jnp.mean(x, axis=axis, keepdims=True)
    v = jnp.var(x, axis=axis, keepdims=True)
    return (x - m) / jnp.sqrt(v + eps)

def _scatter_add(tgt, idx, src, axis=0):
    return tgt.at[idx].add(src)

def _segment_sum(src, seg, n):
    return jax.ops.segment_sum(src, seg, n)
kernel_name = 'mk_gnn_preln_d4_gnn_r32_03bb12'

def setup_inputs(seed: int=0):
    np.random.seed(seed)
    _w = jnp.asarray

    def _rec_inputs():
        import jax
        import jax.numpy as jnp
        _gk = jax.random.key(seed)
        x = -0.000202 + 1 * jax.random.normal(jax.random.fold_in(_gk, 1), (3125, 128), jnp.float32)
        src = jax.random.randint(jax.random.fold_in(_gk, 2), (50000,), 0, 3125, jnp.int32)
        dst = jax.random.randint(jax.random.fold_in(_gk, 3), (50000,), 0, 3125, jnp.int32)
        _o = jnp.argsort(dst, stable=True)
        src = src[_o]
        dst = dst[_o]
        edge_type_3 = jax.random.randint(jax.random.fold_in(_gk, 12), (50000,), 0, 3, jnp.int32)
        edge_type_5 = jax.random.randint(jax.random.fold_in(_gk, 13), (50000,), 0, 5, jnp.int32)
        return (x, src, dst, edge_type_3, edge_type_5)
    x, src, dst, edge_type_3, edge_type_5 = _rec_inputs()

    def _L0_gnn_setup():
        import jax, jax.numpy as jnp
        import numpy as np
        N_NODES = 50000
        N_EDGES = 50000
        IN_DIM = 128
        HEADS = 4
        HEAD_DIM = 32
        N_REL = 3
        NEG_SLOPE = 0.2
        key = jax.random.key(seed)
        ks = jax.random.split(key, 8)
        x = jax.random.normal(ks[0], (N_NODES, IN_DIM), dtype=jnp.float32)
        edge_index = jax.random.randint(ks[1], (2, N_EDGES), 0, N_NODES, dtype=jnp.int64)
        edge_type = jax.random.randint(ks[2], (N_EDGES,), 0, N_REL, dtype=jnp.int64)
        s = 1.0 / np.sqrt(IN_DIM)
        W = jax.random.normal(ks[3], (N_REL, IN_DIM, HEADS * HEAD_DIM), dtype=jnp.float32) * s
        att_src = jax.random.normal(ks[4], (N_REL, HEADS, HEAD_DIM), dtype=jnp.float32) * s
        att_dst = jax.random.normal(ks[5], (N_REL, HEADS, HEAD_DIM), dtype=jnp.float32) * s
        bias = jnp.zeros((N_REL, HEADS * HEAD_DIM), dtype=jnp.float32)
        rel_w = jnp.ones((N_REL,), dtype=jnp.float32)
        return {'x': x, 'W': W, 'att_src': att_src, 'att_dst': att_dst, 'bias': bias, 'rel_w': rel_w, 'edge_index': edge_index, 'edge_type': edge_type}
    _L0_gnn_all = _L0_gnn_setup()
    _L0_gnn_in = {k: v for k, v in _L0_gnn_all.items() if k in ('W', 'att_src', 'att_dst', 'bias', 'rel_w')}
    del _L0_gnn_all

    def _L1_gnn_setup():
        import jax, jax.numpy as jnp
        import numpy as np
        N_NODES = 50000
        N_EDGES = 18750
        D_IN = 128
        D_OUT = 128
        N_BASES = 4
        N_RATINGS = 5
        key = jax.random.key(seed)
        k1, k2, k3, k4, k5, k6 = jax.random.split(key, 6)
        x = jax.random.normal(k1, (N_NODES, D_IN), dtype=jnp.float32)
        edge_index = jax.random.randint(k2, (2, N_EDGES), 0, N_NODES, dtype=jnp.int64)
        edge_type = jax.random.randint(k3, (N_EDGES,), 0, N_RATINGS, dtype=jnp.int64)
        B = jax.random.normal(k4, (N_BASES, D_OUT, D_IN), dtype=jnp.float32) * 0.05
        A = jax.random.normal(k5, (N_RATINGS, N_BASES), dtype=jnp.float32) * 0.05
        W0 = jax.random.normal(k6, (D_OUT, D_IN), dtype=jnp.float32) * 0.05
        return {'x': x, 'edge_index': edge_index, 'edge_type': edge_type, 'B': B, 'A': A, 'W0': W0}
    _L1_gnn_all = _L1_gnn_setup()
    _L1_gnn_in = {k: v for k, v in _L1_gnn_all.items() if k in ('B', 'A', 'W0')}
    del _L1_gnn_all

    def _L2_gnn_setup():
        import jax, jax.numpy as jnp
        import numpy as np
        N_N = 3125
        N_E = 50000
        IN_DIM = 128
        OUT_DIM = 128
        key = jax.random.key(seed)
        k1, k2, k3, k4 = jax.random.split(key, 4)
        feats_n = jax.random.normal(k1, (N_N, IN_DIM), dtype=jnp.float32)
        hs = jnp.concatenate([jnp.arange(N_N, dtype=jnp.int64), jax.random.randint(k2, (N_E - N_N,), 0, N_N, dtype=jnp.int64)])
        ts = jax.random.randint(k3, (N_E,), 0, N_N, dtype=jnp.int64)
        edges = jnp.stack([hs, ts], axis=0)
        weight = jax.random.normal(k4, (OUT_DIM, IN_DIM), dtype=jnp.float32) / np.sqrt(OUT_DIM)
        return {'feats_n': feats_n, 'edges': edges, 'weight': weight}
    _L2_gnn_all = _L2_gnn_setup()
    _L2_gnn_in = {k: v for k, v in _L2_gnn_all.items() if k in ('weight',)}
    del _L2_gnn_all

    def _L3_gnn_setup():
        import jax, jax.numpy as jnp
        import numpy as np
        HEADS = 4
        CH = 32

        def _transformer_conv(x, src, dst, Wq, bq, Wk, bk, Wv, bv, Ws, bs):
            N = x.shape[0]
            q = (x @ Wq + bq).reshape(N, HEADS, CH)
            k = (x @ Wk + bk).reshape(N, HEADS, CH)
            v = (x @ Wv + bv).reshape(N, HEADS, CH)
            alpha = (q[dst] * k[src]).sum(-1) / jnp.sqrt(jnp.asarray(CH, x.dtype))
            amax = jax.ops.segment_max(alpha, dst, num_segments=N)
            ea = jnp.exp(alpha - amax[dst])
            denom = jax.ops.segment_sum(ea, dst, num_segments=N)
            a = ea / jnp.maximum(denom, 1e-16)[dst]
            out = jax.ops.segment_sum(a[:, :, None] * v[src], dst, num_segments=N)
            out = out.reshape(N, HEADS * CH)
            return out + x @ Ws + bs
        key = jax.random.key(seed)
        ks = jax.random.split(key, 20)
        N, E, D = (50000, 25000, 128)
        inp = {'x': jax.random.normal(ks[0], (N, D), jnp.float32), 'edge_index': jax.random.randint(ks[1], (2, E), 0, N, jnp.int64)}
        i = 2
        for l in range(2):
            for nm in ('Wq', 'Wk', 'Wv', 'Ws'):
                inp[f'{nm}{l}'] = jax.random.normal(ks[i], (D, D), jnp.float32) * 0.05
                i += 1
            for nm in ('bq', 'bk', 'bv', 'bs'):
                inp[f'{nm}{l}'] = jnp.zeros((D,), jnp.float32)
        return inp
    _L3_gnn_all = _L3_gnn_setup()
    _L3_gnn_in = {k: v for k, v in _L3_gnn_all.items() if k in ('Wq0', 'Wk0', 'Wv0', 'Ws0', 'bq0', 'bk0', 'bv0', 'bs0', 'Wq1', 'Wk1', 'Wv1', 'Ws1', 'bq1', 'bk1', 'bv1', 'bs1')}
    del _L3_gnn_all
    return {'x': x, 'src': src, 'dst': dst, 'edge_type_3': edge_type_3, 'edge_type_5': edge_type_5, 'L0_gnn_W': _L0_gnn_in['W'], 'L0_gnn_att_src': _L0_gnn_in['att_src'], 'L0_gnn_att_dst': _L0_gnn_in['att_dst'], 'L0_gnn_bias': _L0_gnn_in['bias'], 'L0_gnn_rel_w': _L0_gnn_in['rel_w'], 'L1_gnn_B': _L1_gnn_in['B'], 'L1_gnn_A': _L1_gnn_in['A'], 'L1_gnn_W0': _L1_gnn_in['W0'], 'L2_gnn_weight': _L2_gnn_in['weight'], 'L3_gnn_Wq0': _L3_gnn_in['Wq0'], 'L3_gnn_Wk0': _L3_gnn_in['Wk0'], 'L3_gnn_Wv0': _L3_gnn_in['Wv0'], 'L3_gnn_Ws0': _L3_gnn_in['Ws0'], 'L3_gnn_bq0': _L3_gnn_in['bq0'], 'L3_gnn_bk0': _L3_gnn_in['bk0'], 'L3_gnn_bv0': _L3_gnn_in['bv0'], 'L3_gnn_bs0': _L3_gnn_in['bs0'], 'L3_gnn_Wq1': _L3_gnn_in['Wq1'], 'L3_gnn_Wk1': _L3_gnn_in['Wk1'], 'L3_gnn_Wv1': _L3_gnn_in['Wv1'], 'L3_gnn_Ws1': _L3_gnn_in['Ws1'], 'L3_gnn_bq1': _L3_gnn_in['bq1'], 'L3_gnn_bk1': _L3_gnn_in['bk1'], 'L3_gnn_bv1': _L3_gnn_in['bv1'], 'L3_gnn_bs1': _L3_gnn_in['bs1']}

def reference(x, src, dst, edge_type_3, edge_type_5, L0_gnn_W, L0_gnn_att_src, L0_gnn_att_dst, L0_gnn_bias, L0_gnn_rel_w, L1_gnn_B, L1_gnn_A, L1_gnn_W0, L2_gnn_weight, L3_gnn_Wq0, L3_gnn_Wk0, L3_gnn_Wv0, L3_gnn_Ws0, L3_gnn_bq0, L3_gnn_bk0, L3_gnn_bv0, L3_gnn_bs0, L3_gnn_Wq1, L3_gnn_Wk1, L3_gnn_Wv1, L3_gnn_Ws1, L3_gnn_bq1, L3_gnn_bk1, L3_gnn_bv1, L3_gnn_bs1):
    import jax
    import jax.numpy as jnp

    def _L0_gnn_ref(x, W, att_src, att_dst, bias, rel_w, edge_index, edge_type):
        import jax, jax.numpy as jnp
        import numpy as np
        N_NODES = 50000
        N_EDGES = 50000
        IN_DIM = 128
        HEADS = 4
        HEAD_DIM = 32
        N_REL = 3
        NEG_SLOPE = 0.2
        N = x.shape[0]
        NEG = jnp.float32(-1000000000.0)
        self_idx = jnp.arange(N, dtype=edge_index.dtype)
        src = jnp.concatenate([edge_index[0], self_idx])
        dst = jnp.concatenate([edge_index[1], self_idx])
        weights = jax.nn.softmax(rel_w)
        out = jnp.zeros((N, HEADS * HEAD_DIM), dtype=x.dtype)
        for r in range(N_REL):
            h = (x @ W[r]).reshape(N, HEADS, HEAD_DIM)
            a_s = jnp.einsum('nhc,hc->nh', h, att_src[r])
            a_d = jnp.einsum('nhc,hc->nh', h, att_dst[r])
            score = jax.nn.leaky_relu(a_s[src] + a_d[dst], NEG_SLOPE)
            mask = jnp.concatenate([edge_type == r, jnp.ones((N,), dtype=bool)])
            score = jnp.where(mask[:, None], score, NEG)
            smax = jax.ops.segment_max(score, dst, num_segments=N)
            ex = jnp.exp(score - smax[dst])
            denom = jax.ops.segment_sum(ex, dst, num_segments=N)
            alpha = ex / denom[dst]
            msg = alpha[:, :, None] * h[src]
            rel_out = jax.ops.segment_sum(msg, dst, num_segments=N).reshape(N, HEADS * HEAD_DIM)
            out = out + weights[r] * (rel_out + bias[r])
        return out

    def _L1_gnn_ref(x, edge_index, edge_type, B, A, W0):
        import jax, jax.numpy as jnp
        import numpy as np
        N_NODES = 50000
        N_EDGES = 18750
        D_IN = 128
        D_OUT = 128
        N_BASES = 4
        N_RATINGS = 5
        n_nodes = x.shape[0]
        src, tgt = (edge_index[0], edge_index[1])
        out = x @ W0.T
        W = jnp.einsum('rk,kod->rod', A, B)
        n_ratings = A.shape[0]
        for r in range(n_ratings):
            h = x @ W[r].T
            msg = jnp.where((edge_type == r)[:, None], h[src], jnp.float32(0))
            out = out + jax.ops.segment_sum(msg, tgt, num_segments=n_nodes)
        return out

    def _L2_gnn_ref(feats_n, edges, weight):
        import jax, jax.numpy as jnp
        import numpy as np
        N_N = 3125
        N_E = 50000
        IN_DIM = 128
        OUT_DIM = 128
        hs, ts = (edges[0], edges[1])
        n = feats_n.shape[0]
        deg = jax.ops.segment_sum(jnp.ones_like(hs, dtype=feats_n.dtype), hs, num_segments=n)
        sqrt_d_inv = deg ** (-0.5)
        scaled = sqrt_d_inv[:, None] * feats_n
        agg = jax.ops.segment_sum(scaled[ts], hs, num_segments=n)
        msg = sqrt_d_inv[:, None] * agg
        out = msg @ weight.T
        return jax.nn.relu(out)

    def _L3_gnn_ref(x, edge_index, Wq0, Wk0, Wv0, Ws0, bq0, bk0, bv0, bs0, Wq1, Wk1, Wv1, Ws1, bq1, bk1, bv1, bs1):
        import jax, jax.numpy as jnp
        import numpy as np
        HEADS = 4
        CH = 32

        def _transformer_conv(x, src, dst, Wq, bq, Wk, bk, Wv, bv, Ws, bs):
            N = x.shape[0]
            q = (x @ Wq + bq).reshape(N, HEADS, CH)
            k = (x @ Wk + bk).reshape(N, HEADS, CH)
            v = (x @ Wv + bv).reshape(N, HEADS, CH)
            alpha = (q[dst] * k[src]).sum(-1) / jnp.sqrt(jnp.asarray(CH, x.dtype))
            amax = jax.ops.segment_max(alpha, dst, num_segments=N)
            ea = jnp.exp(alpha - amax[dst])
            denom = jax.ops.segment_sum(ea, dst, num_segments=N)
            a = ea / jnp.maximum(denom, 1e-16)[dst]
            out = jax.ops.segment_sum(a[:, :, None] * v[src], dst, num_segments=N)
            out = out.reshape(N, HEADS * CH)
            return out + x @ Ws + bs
        src, dst = (edge_index[0], edge_index[1])
        h = jax.nn.relu(_transformer_conv(x, src, dst, Wq0, bq0, Wk0, bk0, Wv0, bv0, Ws0, bs0))
        h = jax.nn.relu(_transformer_conv(h, src, dst, Wq1, bq1, Wk1, bk1, Wv1, bv1, Ws1, bs1))
        return h
    edge_index = jnp.stack([src, dst])
    h = jnp.maximum(_layernorm(x, axis=-1), 0.0)
    x = x + _L0_gnn_ref(h, L0_gnn_W, L0_gnn_att_src, L0_gnn_att_dst, L0_gnn_bias, L0_gnn_rel_w, edge_index, edge_type_3)
    h = jnp.maximum(_layernorm(x, axis=-1), 0.0)
    x = x + _L1_gnn_ref(h, edge_index, edge_type_5, L1_gnn_B, L1_gnn_A, L1_gnn_W0)
    h = jnp.maximum(_layernorm(x, axis=-1), 0.0)
    x = x + _L2_gnn_ref(h, edge_index, L2_gnn_weight)
    h = jnp.maximum(_layernorm(x, axis=-1), 0.0)
    x = x + _L3_gnn_ref(h, edge_index, L3_gnn_Wq0, L3_gnn_Wk0, L3_gnn_Wv0, L3_gnn_Ws0, L3_gnn_bq0, L3_gnn_bk0, L3_gnn_bv0, L3_gnn_bs0, L3_gnn_Wq1, L3_gnn_Wk1, L3_gnn_Wv1, L3_gnn_Ws1, L3_gnn_bq1, L3_gnn_bk1, L3_gnn_bv1, L3_gnn_bs1)
    return x

_drawn_inputs = setup_inputs


def setup_inputs(seed=0):
    import zlib

    import numpy as np

    out = dict(_drawn_inputs(seed))
    spreads = {'L0_gnn_bias': (0.0, 0.1),
     'L0_gnn_rel_w': (1.0, 0.2),
     'L3_gnn_bq0': (0.0, 0.8),
     'L3_gnn_bk0': (0.0, 2.0),
     'L3_gnn_bv0': (0.0, 0.1),
     'L3_gnn_bs0': (0.0, 0.289),
     'L3_gnn_bq1': (0.0, 2.0),
     'L3_gnn_bk1': (0.0, 2.0),
     'L3_gnn_bv1': (0.0, 0.1),
     'L3_gnn_bs1': (0.0, 0.1)}
    factors = {'L0_gnn_att_dst': 20.402,
     'L3_gnn_Wq0': 8.0,
     'L3_gnn_Wk0': 8.0,
     'L3_gnn_Wq1': 8.0,
     'L3_gnn_Wk1': 8.0}
    for name, (base, spread) in spreads.items():
        noise = np.random.default_rng([zlib.crc32(name.encode()), seed]).standard_normal(out[name].shape)
        drawn = base * np.exp(spread * noise) if base else spread * noise
        out[name] = jnp.asarray(drawn.astype(out[name].dtype))
    for name, factor in factors.items():
        out[name] = (out[name] * factor).astype(out[name].dtype)
    return out
```

```python
from contextlib import ExitStack

import concourse.bass as bass
from concourse import mybir

F32 = mybir.dt.float32
BF16 = mybir.dt.bfloat16
I32 = mybir.dt.int32
ALU = mybir.AluOpType
ACT = mybir.ActivationFunctionType
AX = mybir.AxisListType.X
ds = bass.ds

P = 128
N, D = 3125, 128
E = 50000
H, C = 4, 32
NREL, NRAT, NBASE = 3, 5, 4
NT = -(-N // P)
NP = NT * P
FULL = N // P
REST = N - FULL * P
ET = -(-E // P)
EREST = E - (ET - 1) * P
RB = 104
NB = 4
NS = RB * NB
assert NS >= ET + NT - 1
G = 8
NI = NS // (2 * G)
assert NI * 2 * G == NS
XW = H * P
WA0 = D + H
WN0 = D + 2 * H
BIG = 1e37
NEG = 1e9
EPS = 1e-5
NDUMP = NP + P


class Chain:

    def __init__(self, eng, sem):
        self.eng, self.sem, self.n = eng, sem, 0

    def __call__(self, ins):
        self.n += 1
        ins.then_inc(self.sem, 1)
        self.eng.wait_ge(self.sem, self.n)


class Hand:

    def __init__(self, sem):
        self.sem, self.given, self.taken = sem, 0, 0

    def give(self, ins, by=1):
        self.given += by
        ins.then_inc(self.sem, by)

    def take(self, eng, by=1):
        self.taken += by
        eng.wait_ge(self.sem, self.taken)


def bc(ap, shape):
    return ap.to_broadcast(shape)


def build(nc, x_in, src_in, dst_in, t3_in, t5_in, W_in, as_in, ad_in, bias_in, relw_in,
          B_in, A_in, W0_in, W2_in, l3, out):
    ctx = ExitStack()
    with ctx:
        def sb(name, shape, dt=F32):
            return ctx.enter_context(nc.sbuf_tensor(name, shape, dt))

        layer_sems = []

        def sem(name):
            s = nc.alloc_semaphore(name=name)
            layer_sems.append(s)
            return s

        def end_layer():
            nc.clear_and_free_semaphores(layer_sems)
            layer_sems.clear()
            nc.all_engine_barrier()

        def dram(name, shape, dt=F32):
            return nc.dram_tensor(name, shape, dt, kind="Internal").ap()

        edge_tab = dram("edge_tab", [ET, 4 * P], I32)
        dl_dram = dram("dl_dram", [NS * P], BF16)
        srcrow_dram = dram("srcrow_dram", [NS * P])
        tab0 = dram("tab0", [NREL * NP, WA0])
        tab1 = dram("tab1", [NRAT * NP, D])
        tab3 = dram("tab3", [NP, 2 * D])
        spill = dram("spill", [P, NS * D])
        scat = [dram(f"scat{k}", [NDUMP, D]) for k in range(G)]

        iota_row = sb("iota_row", [P, P])
        iota_p = sb("iota_p", [P, 1])
        ident = sb("ident", [P, P])
        ones = sb("ones", [P, P])
        zeros = sb("zeros", [P, 512])
        dlT = sb("dlT", [P, NS])
        srcT = sb("srcT", [P, NS])
        t3T = sb("t3T", [P, NS])
        loT = sb("loT", [P, NS])
        hiT = sb("hiT", [P, NS])
        i0 = sb("i0", [P, NS], I32)
        i1 = sb("i1", [P, NS], I32)
        i3 = sb("i3", [P, NS], I32)
        tnI = sb("tnI", [1, NS], I32)
        Kr = sb("Kr", [RB, NB, P])
        same_f = sb("same_f", [RB, NB, H, P])
        same_b = sb("same_b", [RB, NB, H, P])
        carry_f = sb("carry_f", [RB, NB, P])
        carry_b = sb("carry_b", [RB, NB, P])
        is_last = sb("is_last", [RB, NB, P])
        chain_f = sb("chain_f", [H, NS])
        chain_b = sb("chain_b", [H, NS])
        x = sb("x", [P, NT, D])
        hid = sb("hid", [P, NT, D])
        idx = sb("idx", [P, 2, G], I32)
        A1 = sb("A1", [P, 10240])
        A2 = sb("A2", [P, 16384])
        A3 = sb("A3", [P, 6144])
        SM = sb("SM", [P, 1024])
        SMI = sb("SMI", [P, 256], I32)

        ps = ctx.enter_context(nc.psum_tensor("ps", [P, 8, 512], F32))
        psf = ps[:, :, :].rearrange("p a b -> p (a b)")

        passed = ctx.enter_context(nc.semaphore("passed"))

        def hold(eng, s, value):
            eng.wait_ge(s, value)
            eng.sem_inc(passed, 1)

        cnt_cmp = A2[:, 0:9600].rearrange("p (j e) -> p j e", j=24)
        dst_i = A1[:, 0:400].bitcast(I32)
        dst_f = A1[:, 400:800]
        R = A1[:, 1024:1024 + NB * 512].bitcast(I32).rearrange("p (b q e) -> p b q e", b=NB, q=4)
        Rf = A1[:, 4096:4096 + NB * 512].rearrange("p (b q e) -> p b q e", b=NB, q=4)
        DL = A3[:, 0:512].rearrange("p (b e) -> p b e", b=NB)
        VAL = A3[:, 512:1024].rearrange("p (b e) -> p b e", b=NB)
        I0f = A3[:, 1024:1536].rearrange("p (b e) -> p b e", b=NB)
        I1f = A3[:, 1536:2048].rearrange("p (b e) -> p b e", b=NB)
        TMP = A3[:, 2048:2560].rearrange("p (b e) -> p b e", b=NB)
        DLB = A3[:, 2560:2816].bitcast(BF16).rearrange("p (b e) -> p b e", b=NB)
        KK = A3[:, 2816:2848].rearrange("p (a b h) -> p a b h", a=2, b=NB)
        TJ = A3[:, 2848:2948].rearrange("p (b j) -> p b j", b=NB)
        KL = A3[:, 3072:3072 + NS + 1]
        KF = A3[:, 3520:3520 + NS + 1]
        cnt = SM[:, 0:26]
        Fv = SM[:, 32:58]
        af = SM[:, 64:90]
        lf = SM[:, 96:122]
        nn = SM[:, 128:153]
        Oc = SM[:, 160:185]
        dl_ = SM[:, 192:217]
        sval = SM[:, 224:228]
        tn = SM[:, 232:236]
        tnc = SM[:, 240:244]
        te = SM[:, 248:252]
        tn128 = SM[:, 256:260]
        PL = SM[:, 288:320].rearrange("p (a b h) -> p a b h", a=2, b=NB)
        pad_i = SMI[:, 0:96]
        Fi = SMI[:, 96:122]
        Li = SMI[:, 128:154]
        te_i = SMI[:, 160:164]
        LO = A2[:, 0:NS].bitcast(I32)
        HI = A2[:, 512:512 + NS].bitcast(I32)
        HIf = A2[:, 1024:1024 + NS]
        VT = A2[:, 1536:1536 + NS]

        s_pad, s_tab, s_dst, s_c = sem("s_pad"), sem("s_tab"), sem("s_dst"), sem("s_c")
        s_io, s_io2, s_id, s_cnt, s_F, s_te, s_R = (sem("s_io"), sem("s_io2"), sem("s_id"), sem("s_cnt"),
                                                    sem("s_F"), sem("s_te"), sem("s_R"))
        s_row, s_tr, s_kk, s_kt, s_sh, s_sht, s_dd, s_x = (sem("s_row"), sem("s_tr"), sem("s_kk"), sem("s_kt"),
                                                           sem("s_sh"), sem("s_sht"), sem("s_dd"), sem("s_x"))
        QUANT = [DL, Rf[:, :, 1, :], I0f, I1f, Rf[:, :, 2, :]]

        with nc.Block() as block:
            @block.sync
            def _(sp):
                sp.dma_start(dst_i[0:125, :], dst_in.rearrange("(p e) -> p e", p=125)).then_inc(s_dst, 16)
                for q, arr in enumerate((dst_in, src_in, t3_in, t5_in)):
                    sp.dma_start(edge_tab[0:ET - 1, q * P:(q + 1) * P],
                                 arr[0:(ET - 1) * P].rearrange("(t e) -> t e", e=P)).then_inc(s_tab, 16)
                    sp.dma_start(edge_tab[ET - 1:ET, q * P:q * P + EREST],
                                 arr[(ET - 1) * P:E].rearrange("(a e) -> a e", a=1)).then_inc(s_tab, 16)
                sp.wait_ge(s_pad, 2)
                for q in range(4):
                    sp.dma_start(edge_tab[ET - 1:ET, q * P + EREST:(q + 1) * P],
                                 pad_i[0:1, (48 if q else 0):(48 if q else 0) + P - EREST]).then_inc(s_tab, 16)
                sp.dma_start(x[:, 0:FULL, :], x_in[0:FULL * P, :].rearrange("(t p) d -> p t d", p=P)).then_inc(s_x, 16)
                sp.wait_ge(s_pad, 3)
                sp.dma_start(x[0:REST, FULL, :], x_in[FULL * P:N, :]).then_inc(s_x, 16)
                sp.wait_ge(s_row, 1)
                sp.dma_start(dl_dram.rearrange("(b p e) -> p b e", b=NB, e=P), DLB[0:RB]).then_inc(s_dd, 16)
                sp.dma_start(srcrow_dram.rearrange("(b p e) -> p b e", b=NB, e=P), Rf[0:RB, :, 1, :]).then_inc(s_dd, 16)
                sp.wait_ge(s_dd, 32)
                sp.wait_ge(s_x, 32)

            @block.gpsimd
            def _(g):
                g.memset(ident[:, :], 0.0).then_inc(s_io, 1)
                g.iota(iota_row[:, :], [[1, P]], base=0, channel_multiplier=0,
                       allow_small_or_imprecise_dtypes=True).then_inc(s_io, 1)
                g.iota(iota_p[:, :], [[0, 1]], base=0, channel_multiplier=1,
                       allow_small_or_imprecise_dtypes=True).then_inc(s_io, 1)
                g.iota(sval, [[RB, NB]], base=0, channel_multiplier=1,
                       allow_small_or_imprecise_dtypes=True).then_inc(s_io, 1)
                g.wait_ge(s_io, 1)
                g.affine_select(out=ident[:, :], in_=ident[:, :], compare_op=ALU.not_equal, fill=1.0,
                                base=0, pattern=[[-1, P]], channel_multiplier=1).then_inc(s_id, 1)
                g.wait_ge(s_tab, 16 * 12)
                g.wait_ge(s_te, 1)
                for b in range(NB):
                    g.indirect_dma_start(out=R[0:RB, b].rearrange("p q e -> p (q e)"), out_offset=None, in_=edge_tab[:, :],
                                         in_offset=bass.IndirectOffsetOnAxis(ap=te_i[0:RB, b:b + 1], axis=0)
                                         ).then_inc(s_R, 16)

            @block.tensor
            def _(pe):
                pe.wait_ge(s_cnt, 1)
                pe.matmul(ps[:, 7, 0:26], ones[0:125, :], cnt[0:125, :], start=True, stop=True).then_inc(s_F, 1)
                pe.wait_ge(s_id, 1)
                pe.wait_ge(s_row, 1)
                for q, Q in enumerate(QUANT):
                    for b in range(NB):
                        pe.transpose(ps[:, q, b * RB:(b + 1) * RB], Q[0:RB, b, :], ident[0:RB, 0:RB])
                for b in range(NB):
                    last = pe.transpose(ps[0:1, 5, b * RB:(b + 1) * RB], tnc[0:RB, b:b + 1], ident[0:RB, 0:RB])
                last.then_inc(s_tr, 1)
                pe.wait_ge(s_kk, 1)
                for a in range(2):
                    for b in range(NB):
                        last = pe.transpose(ps[0:H, 6 + a, b * RB:(b + 1) * RB], KK[0:RB, a, b, :], ident[0:RB, 0:RB])
                last.then_inc(s_kt, 1)
                pe.wait_ge(s_sh, 1)
                for b in range(NB):
                    pe.transpose(ps[0:RB, 0, b * H:(b + 1) * H], KL[0:H, b * RB:(b + 1) * RB], ident[0:H, 0:H])
                for b in range(NB):
                    last = pe.transpose(ps[0:RB, 0, 16 + b * H:16 + (b + 1) * H],
                                        KF[0:H, 1 + b * RB:1 + (b + 1) * RB], ident[0:H, 0:H])
                last.then_inc(s_sht, 1)

            @block.vector
            def _(v):
                do = Chain(v, s_c)
                do(v.memset(ones[:, :], 1.0))
                do(v.memset(zeros[:, :], 0.0))
                v.memset(pad_i[:, 0:48], 8192).then_inc(s_pad, 1)
                v.memset(pad_i[:, 48:96], 0).then_inc(s_pad, 1)
                v.memset(x[:, FULL, :], 0.0).then_inc(s_pad, 1)
                do(v.memset(cnt, 0.0))
                do(v.memset(cnt[:, 25:26], E / 125))
                v.wait_ge(s_dst, 16)
                do(v.tensor_copy(dst_f[0:125, :], dst_i[0:125, :]))
                for j in range(1, NT):
                    ins = v.tensor_scalar(cnt_cmp[0:125, j - 1, :], dst_f[0:125, :], float(P * j), None, ALU.is_lt)
                do(ins)
                do(v.tensor_reduce(cnt[0:125, 1:NT], cnt_cmp[0:125], AX, ALU.add))
                v.nop().then_inc(s_cnt, 1)
                v.wait_ge(s_F, 1)
                do(v.tensor_copy(Fv, ps[:, 7, 0:26]))
                do(v.tensor_copy(Fi, Fv))
                do(v.tensor_scalar(Fi, Fi, 7, None, ALU.arith_shift_right))
                do(v.tensor_copy(af, Fi))
                do(v.tensor_scalar(lf, Fv, -1.0, None, ALU.add))
                do(v.tensor_copy(Li, lf))
                do(v.tensor_scalar(Li, Li, 7, None, ALU.arith_shift_right))
                do(v.tensor_copy(lf, Li))
                do(v.tensor_tensor(nn, lf[:, 1:26], af[:, 0:25], ALU.subtract))
                do(v.tensor_scalar(nn, nn, 1.0, None, ALU.add))
                do(v.tensor_tensor(dl_, Fv[:, 1:26], Fv[:, 0:25], ALU.is_gt))
                do(v.tensor_tensor(nn, nn, dl_, ALU.mult))
                do(v.tensor_tensor_scan(Oc, ones[:, 0:25], nn, 0.0, ALU.mult, ALU.add))
                do(v.tensor_tensor(dl_, nn, Oc, ALU.subtract))
                do(v.tensor_tensor(dl_, dl_, af[:, 0:25], ALU.add))
                v.wait_ge(s_io, 4)
                do(v.tensor_tensor(TJ, bc(Oc.unsqueeze(1), [P, NB, NT]), bc(sval.unsqueeze(2), [P, NB, NT]), ALU.is_le))
                do(v.tensor_reduce(tn, TJ, AX, ALU.add))
                do(v.tensor_tensor(TJ, bc(iota_row[:, 0:NT].unsqueeze(1), [P, NB, NT]),
                                   bc(tn.unsqueeze(2), [P, NB, NT]), ALU.is_equal))
                do(v.tensor_tensor(TJ, TJ, bc(dl_.unsqueeze(1), [P, NB, NT]), ALU.mult))
                do(v.tensor_reduce(te, TJ, AX, ALU.add))
                do(v.tensor_tensor(te, te, sval, ALU.add))
                do(v.tensor_scalar(te, te, float(ET - 1), 0.0, ALU.min, ALU.max))
                do(v.tensor_copy(te_i, te))
                v.nop().then_inc(s_te, 1)
                do(v.tensor_scalar(tnc, tn, float(NT - 1), None, ALU.min))
                do(v.tensor_scalar(tn128, tn, float(P), None, ALU.mult))
                v.wait_ge(s_R, 16 * NB)
                do(v.tensor_copy(A1[0:RB, 4096:4096 + NB * 512], A1[0:RB, 1024:1024 + NB * 512].bitcast(I32)))
                dstf, srcf, t3f, t5f = (Rf[0:RB, :, q, :] for q in range(4))
                do(v.tensor_tensor(DL[0:RB], dstf, bc(tn128[0:RB].unsqueeze(2), [RB, NB, P]), ALU.subtract))
                do(v.tensor_scalar(VAL[0:RB], DL[0:RB], 0.0, None, ALU.is_ge))
                do(v.tensor_scalar(TMP[0:RB], DL[0:RB], float(P), None, ALU.is_lt))
                do(v.tensor_tensor(VAL[0:RB], VAL[0:RB], TMP[0:RB], ALU.mult))
                do(v.tensor_scalar(Kr[:, :, :], dstf, 1.0, None, ALU.add))
                do(v.tensor_tensor(Kr[:, :, :], Kr[:, :, :], VAL[0:RB], ALU.mult))
                do(v.tensor_scalar(Kr[:, :, :], Kr[:, :, :], -1.0, None, ALU.add))
                do(v.scalar_tensor_tensor(I0f[0:RB], t3f, float(NP), srcf, ALU.mult, ALU.add))
                do(v.scalar_tensor_tensor(I1f[0:RB], t5f, float(NP), srcf, ALU.mult, ALU.add))
                do(v.tensor_copy(DLB[0:RB], DL[0:RB]))
                v.nop().then_inc(s_row, 1)
                do(v.tensor_copy(KK[0:RB, 0], bc(Kr[:, :, P - 1:P], [RB, NB, H])))
                do(v.tensor_copy(KK[0:RB, 1], bc(Kr[:, :, 0:1], [RB, NB, H])))
                v.nop().then_inc(s_kk, 1)
                v.wait_ge(s_tr, 1)
                do(v.tensor_copy(dlT[:, :], ps[:, 0, 0:NS]))
                do(v.tensor_copy(srcT[:, :], ps[:, 1, 0:NS]))
                do(v.tensor_copy(i3[:, :], ps[:, 1, 0:NS]))
                do(v.tensor_copy(i0[:, :], ps[:, 2, 0:NS]))
                do(v.tensor_copy(i1[:, :], ps[:, 3, 0:NS]))
                do(v.tensor_copy(t3T[:, :], ps[:, 4, 0:NS]))
                do(v.tensor_scalar(tnI[:, :], ps[0:1, 5, 0:NS], float(P), None, ALU.mult))
                do(v.tensor_scalar(LO, i3[:, :], P - 1, None, ALU.bitwise_and))
                do(v.tensor_copy(loT[:, :], LO))
                do(v.tensor_scalar(HI, i3[:, :], 7, None, ALU.arith_shift_right))
                do(v.tensor_copy(HIf, HI))
                do(v.tensor_scalar(VT, dlT[:, :], 0.0, None, ALU.is_ge))
                do(v.scalar_tensor_tensor(VT, dlT[:, :], float(P), VT, ALU.is_lt, ALU.mult))
                do(v.scalar_tensor_tensor(HIf, HIf, 1.0, VT, ALU.add, ALU.mult))
                do(v.tensor_scalar(hiT[:, :], HIf, -1.0, None, ALU.add))
                do(v.memset(same_f[:, :, :, :], 0.0))
                do(v.memset(same_b[:, :, :, :], 0.0))
                for h in range(H):
                    v.tensor_tensor(same_f[:, :, h, 1:P], Kr[:, :, 1:P], Kr[:, :, 0:P - 1], ALU.is_equal)
                    ins = v.tensor_tensor(same_b[:, :, h, 0:P - 1], Kr[:, :, 1:P], Kr[:, :, 0:P - 1], ALU.is_equal)
                do(ins)
                v.wait_ge(s_kt, 1)
                do(v.memset(KL[0:H, 0:1], -5.0))
                do(v.memset(KF[0:H, NS:NS + 1], -6.0))
                do(v.tensor_copy(KL[0:H, 1:NS + 1], ps[0:H, 6, 0:NS]))
                do(v.tensor_copy(KF[0:H, 0:NS], ps[0:H, 7, 0:NS]))
                v.nop().then_inc(s_sh, 1)
                do(v.tensor_tensor(chain_f[:, :], KL[0:H, 1:NS + 1], KL[0:H, 0:NS], ALU.is_equal))
                do(v.tensor_tensor(chain_b[:, :], KF[0:H, 1:NS + 1], KF[0:H, 0:NS], ALU.is_equal))
                v.wait_ge(s_sht, 1)
                do(v.tensor_copy(PL[0:RB].rearrange("p a b h -> p (a b h)"), ps[0:RB, 0, 0:32]))
                do(v.tensor_tensor(carry_f[:, :, :], Kr[:, :, :], bc(PL[0:RB, 0, :, 0:1], [RB, NB, P]), ALU.is_equal))
                do(v.tensor_tensor(carry_b[:, :, :], Kr[:, :, :], bc(PL[0:RB, 1, :, 0:1], [RB, NB, P]), ALU.is_equal))
                do(v.tensor_scalar(is_last[:, :, 0:P - 1], same_b[:, :, 0, 0:P - 1], -1.0, 1.0, ALU.mult, ALU.add))
                do(v.tensor_scalar(is_last[:, :, P - 1:P], carry_b[:, :, P - 1:P], -1.0, 1.0, ALU.mult, ALU.add))
                do(v.tensor_tensor(is_last[:, :, :], is_last[:, :, :], VAL[0:RB], ALU.mult))


        hT = A3[:, 0:NT * P].rearrange("p (t n) -> p t n", t=NT)
        xf = x[:, :, :].rearrange("p t d -> p (t d)")
        hf = hid[:, :, :].rearrange("p t d -> p (t d)")
        xc = A1[:, 0:3200].rearrange("p (t d) -> p t d", t=NT)
        sq = A1[:, 3200:6400].rearrange("p (t d) -> p t d", t=NT)
        mean, var, std, rstd = (SM[:, 32 * k:32 * k + NT] for k in range(4))
        NBK = -(-NT // 4)

        def layer_norm(v, do, s_var, s_std):
            do(v.tensor_reduce(mean, x[:, :, :], AX, ALU.add))
            do(v.tensor_scalar(mean, mean, 1.0 / D, None, ALU.mult))
            do(v.tensor_tensor(xc, x[:, :, :], bc(mean.unsqueeze(2), [P, NT, D]), ALU.subtract))
            do(v.tensor_tensor(sq, xc, xc, ALU.mult))
            do(v.tensor_reduce(var, sq, AX, ALU.add))
            do(v.tensor_scalar(var, var, 1.0 / D, EPS, ALU.mult, ALU.add))
            v.nop().then_inc(s_var, 1)
            v.wait_ge(s_std, 1)
            do(v.reciprocal(rstd, std))
            do(v.tensor_tensor(xc, xc, bc(rstd.unsqueeze(2), [P, NT, D]), ALU.mult))
            do(v.tensor_scalar(hid[:, :, :], xc, 0.0, None, ALU.max))

        def transpose_hidden(pe, s_ht):
            for t in range(NT):
                last = pe.transpose(ps[:, t // 4, (t % 4) * P:(t % 4 + 1) * P], hid[:, t, :], ident[:, :])
            last.then_inc(s_ht, 1)

        def node_stage(tag, prods, norm=True, prep_v=None, prep_pe=None, prep_sp=None, after_sp=None,
                       after_v=None, hidden_v=None):
            s_c, s_var, s_std, s_h, s_ht, s_htc, s_w, s_wd, s_mm, s_st = (
                sem(f"{tag}_{n}") for n in ("c", "var", "std", "h", "ht", "htc", "w", "wd", "mm", "st"))
            s_out = {"v": sem(f"{tag}_ov"), "a": sem(f"{tag}_oa")}
            s_pw, s_pwc = sem(f"{tag}_pw"), sem(f"{tag}_pwc")
            done, total = [], {"v": 0, "a": 0}
            for _, _, _, e, _ in prods:
                total[e] += 1
                done.append((e, total[e]))
            with nc.Block() as block:
                @block.sync
                def _(sp):
                    if prep_sp:
                        prep_sp(sp, s_wd)
                    if after_sp:
                        for e in "va":
                            if total[e]:
                                sp.wait_ge(s_out[e], total[e])
                        after_sp(sp, s_st)

                @block.vector
                def _(v):
                    do = Chain(v, s_c)
                    if norm:
                        layer_norm(v, do, s_var, s_std)
                    if hidden_v:
                        hidden_v(v, do)
                    v.nop().then_inc(s_h, 1)
                    if prep_v:
                        prep_v(v, do, s_wd, s_pw, s_pwc)
                    v.nop().then_inc(s_w, 1)
                    for j, (t, w, n, e, put) in enumerate(prods):
                        if e == "v":
                            v.wait_ge(s_mm, j + 1)
                            put(v, ps[:, j % 8, 0:n]).then_inc(s_out["v"], 1)
                    if after_v:
                        v.wait_ge(s_out["v"], total["v"])
                        after_v(v, do)

                @block.scalar
                def _(a):
                    if norm:
                        a.wait_ge(s_var, 1)
                        a.activation(std, var, ACT.Sqrt).then_inc(s_std, 1)
                    a.wait_ge(s_ht, 1)
                    for k in range(NBK):
                        n = min(4, NT - 4 * k) * P
                        a.activation(A3[:, 512 * k:512 * k + n], ps[:, k, 0:n], ACT.Copy).then_inc(s_htc, 1)
                    for j, (t, w, n, e, put) in enumerate(prods):
                        if e == "a":
                            a.wait_ge(s_mm, j + 1)
                            put(a, ps[:, j % 8, 0:n]).then_inc(s_out["a"], 1)

                @block.tensor
                def _(pe):
                    if prep_pe:
                        prep_pe(pe, s_wd, s_pw)
                        pe.wait_ge(s_pwc, 1)
                    pe.wait_ge(s_h, 1)
                    transpose_hidden(pe, s_ht)
                    pe.wait_ge(s_htc, NBK)
                    pe.wait_ge(s_w, 1)
                    for j, (t, w, n, e, put) in enumerate(prods):
                        if j >= 8:
                            pe.wait_ge(s_out[done[j - 8][0]], done[j - 8][1])
                        pe.matmul(ps[:, j % 8, 0:n], hT[:, t, :], w, start=True, stop=True).then_inc(s_mm, 1)

        def copy_to(dst):
            def put(eng, src):
                if eng.engine == mybir.EngineType.Activation:
                    return eng.activation(dst, src, ACT.Copy)
                return eng.tensor_copy(dst, src)
            return put

        def half(base, n, h):
            return slice(base + h * n, base + (h + 1) * n)

        def gather_loop(g, table, rows, idx_src, s_idx, s_rows, s_free):
            with g.Fori(0, NI) as i:
                for h in range(2):
                    for s in s_free:
                        hold(g, s[h], i + 1)
                    g.tensor_copy(idx[:, h, :], idx_src[:, ds(i * (2 * G) + h * G, G)]).then_inc(s_idx, 1)
                    hold(g, s_idx, 2 * i + (h + 1))
                    for k in range(G):
                        g.indirect_dma_start(out=rows(h, k), out_offset=None, in_=table,
                                             in_offset=bass.IndirectOffsetOnAxis(ap=idx[:, h, k:k + 1], axis=0)
                                             ).then_inc(s_rows[h], 16)

        def broadcast_loop(eng, dst, src, s_in, s_free):
            with eng.Fori(0, NI) as i:
                for h in range(2):
                    hold(eng, s_free[h], i + 1)
                    eng.dma_start(dst(h), src[ds(i * (2 * G * P) + h * (G * P), G * P)].partition_broadcast(P)
                                  ).then_inc(s_in[h], 16)

        def onehot_in(rows8):
            return bc(iota_row[:, :].unsqueeze(1), [P, G, P]), bc(rows8.unsqueeze(2), [P, G, P])

        def clear_acc(pe, banks):
            for b in range(banks):
                pe.matmul(ps[:, b, :], zeros[:, 0:P], zeros[:, :], start=True, stop=False, skip_group_check=True)

        def tile_regs(pe, tag):
            return [pe.alloc_register(f"{tag}_tile{k}") for k in range(G)]

        def load_tiles(pe, regs, s0):
            pe.load(regs, tnI[0:1, ds(s0, G)])
            return [pe.snap(r, min_val=0, max_val=(NT - 1) * P) for r in regs]

        def lookup_stage(tag, table, idx_src, width, vcol, rhs, ncol, use):
            s_idx, s_oht, s_g, s_c = (sem(f"{tag}_{n}") for n in ("idx", "oht", "g", "c"))
            s_rows, s_used, s_sp, s_spf, s_dl, s_dlf = ([sem(f"{tag}_{n}{h}") for h in range(2)]
                                                        for n in ("rows", "used", "sp", "spf", "dl", "dlf"))
            rows = A1[:, 0:2 * G * width].rearrange("p (h k w) -> p h k w", h=2, k=G)
            o = 4096
            OHT = A1[:, o:o + 2048].rearrange("p (h k n) -> p h k n", h=2, k=G)
            dlb = A1[:, o + 2048:o + 3072].bitcast(BF16).rearrange("p (h n) -> p h n", h=2)
            prod = A1[:, o + 3072:o + 5120]
            look = [ps[:, 2 * h:2 * h + 2, :].rearrange("p a (k n) -> p (a k) n", n=P)[:, :, 0:ncol] for h in range(2)]
            with nc.Block() as block:
                @block.gpsimd
                def _(g):
                    gather_loop(g, table, lambda h, k: rows[:, h, k, :], idx_src, s_idx, s_rows,
                                [s_used, s_spf])

                @block.scalar
                def _(a):
                    broadcast_loop(a, lambda h: dlb[:, h, :], dl_dram, s_dl, s_dlf)

                @block.sync
                def _(sp):
                    for h in range(2):
                        sp.sem_inc(s_spf[h], 1)
                    with sp.Fori(0, NI) as i:
                        for h in range(2):
                            hold(sp, s_rows[h], i * (16 * G) + 16 * G)
                            sp.dma_start(spill[:, ds(i * (2 * G * P) + h * (G * P), G * P)].rearrange("p (k d) -> p k d", k=G),
                                         rows[:, h, :, vcol:vcol + D]).then_inc(s_sp[h], 16)
                            hold(sp, s_sp[h], 16 * i + 16)
                            sp.sem_inc(s_spf[h], 1)

                @block.vector
                def _(v):
                    for h in range(2):
                        v.sem_inc(s_used[h], 1)
                        v.sem_inc(s_dlf[h], 1)
                    with v.Fori(0, NI) as i:
                        for h in range(2):
                            hold(v, s_dl[h], 16 * i + 16)
                            v.tensor_scalar(OHT[:, h].rearrange("p k n -> p (k n)"), dlb[:, h, :], iota_p[:, 0:1], None,
                                            ALU.is_equal).then_inc(s_oht, 1)
                            hold(v, s_oht, 2 * i + (h + 1))
                            v.sem_inc(s_dlf[h], 1)
                            hold(v, s_g, 2 * i + (h + 1))
                            hold(v, s_rows[h], i * (16 * G) + 16 * G)
                            use(v, i, h, rows, look[h], prod, s_c)
                            v.sem_inc(s_used[h], 1)

                @block.tensor
                def _(pe):
                    regs = tile_regs(pe, tag)
                    with pe.Fori(0, NI) as i:
                        for h in range(2):
                            hold(pe, s_oht, 2 * i + (h + 1))
                            hold(pe, s_used[h], i + 1)
                            tiles = load_tiles(pe, regs, i * (2 * G) + h * G)
                            for k in range(G):
                                last = pe.matmul(look[h][:, k, :], OHT[:, h, k, :], rhs(tiles[k]), start=True, stop=True)
                            last.then_inc(s_g, 1)

        def sum_stage(tag, wts, extra=None, combine=None, combine_sp=None):
            s_oh, s_msg, s_mm, s_c, s_all, s_e = (sem(f"{tag}_{n}") for n in ("oh", "msg", "mm", "c", "all", "e"))
            s_v = [sem(f"{tag}_v{h}") for h in range(2)]
            s_vf = [sem(f"{tag}_vf{h}") for h in range(2)]
            s_mf = [sem(f"{tag}_mf{h}") for h in range(2)]
            val = A1[:, 0:2048].rearrange("p (h n) -> p h n", h=2)
            OH = A1[:, 2048:4096].rearrange("p (h k n) -> p h k n", h=2, k=G)
            msg = A1[:, 4096:6144].rearrange("p (h k n) -> p h k n", h=2, k=G)
            with nc.Block() as block:
                @block.sync
                def _(sp):
                    with sp.Fori(0, NI) as i:
                        for h in range(2):
                            hold(sp, s_vf[h], i + 1)
                            sp.dma_start(val[:, h, :], spill[:, ds(i * (2 * G * P) + h * (G * P), G * P)]).then_inc(s_v[h], 16)
                    if combine_sp:
                        combine_sp(sp, s_e)

                @block.vector
                def _(v):
                    for h in range(2):
                        v.sem_inc(s_vf[h], 1)
                    with v.Fori(0, NI) as i:
                        for h in range(2):
                            hold(v, s_mf[h], i + 1)
                            a, b = onehot_in(dlT[:, ds(i * (2 * G) + h * G, G)])
                            v.tensor_tensor(OH[:, h], a, b, ALU.is_equal).then_inc(s_oh, 1)
                            hold(v, s_v[h], 16 * i + 16)
                            w = wts[:, ds(i * (2 * G * H) + h * (G * H), G * H)]
                            v.tensor_tensor(msg[:, h].rearrange("p k (h c) -> p (k h) c", h=H),
                                            val[:, h, :].rearrange("p (q c) -> p q c", c=C),
                                            bc(w.unsqueeze(2), [P, G * H, C]), ALU.mult).then_inc(s_msg, 1)
                            hold(v, s_msg, 2 * i + (h + 1))
                            v.sem_inc(s_vf[h], 1)
                    v.wait_ge(s_all, 1)
                    combine(v, Chain(v, s_c), s_e)

                @block.tensor
                def _(pe):
                    for h in range(2):
                        pe.sem_inc(s_mf[h], 1)
                    clear_acc(pe, 8 if extra is not None else 7)
                    regs = tile_regs(pe, tag + "s")
                    with pe.Fori(0, NI) as i:
                        for h in range(2):
                            hold(pe, s_oh, 2 * i + (h + 1))
                            hold(pe, s_msg, 2 * i + (h + 1))
                            tiles = load_tiles(pe, regs, i * (2 * G) + h * G)
                            for k in range(G):
                                s = i * (2 * G) + (h * G + k)
                                r = tiles[k]
                                last = pe.matmul(psf[:, ds(r, P)], OH[:, h, k, :], msg[:, h, k, :],
                                                 start=False, stop=False, skip_group_check=True)
                                if extra is not None:
                                    last = pe.matmul(psf[:, ds((r >> 3) + 7 * 512, XC)], OH[:, h, k, :],
                                                     extra[:, ds(s * XC, XC)],
                                                     start=False, stop=False, skip_group_check=True)
                            last.then_inc(s_mf[h], 1)
                    for h in range(2):
                        pe.wait_ge(s_mf[h], NI + 1)
                    pe.nop().then_inc(s_all, 1)
        XN = NREL * H
        XC = XN + 1
        XP = 16

        def row4(ap):
            return ap.rearrange("p (b h e) -> p b h e", b=NB, h=H)

        CC = SM[0:H, 0:NS + 1]
        CI = SM[0:RB, 424:440]
        T2 = SM[0:RB, 448:960].rearrange("p (b e) -> p b e", b=NB)
        PC = A3[0:H, 5696:5696 + NS]

        def scan_v(v, do, to_pe, from_pe, Xin, Y, T, kind, back):
            is_max = kind == "max"
            same, carry, chain = (same_b, carry_b, chain_b) if back else (same_f, carry_f, chain_f)
            samef = same[:, :, :, :].rearrange("p b h e -> p (b h e)")
            st = -1 if back else 1
            ini = -BIG if is_max else 0.0
            if is_max:
                do(v.tensor_scalar(T, samef, -1.0, BIG, ALU.add, ALU.mult))
                do(v.tensor_scalar(PC, chain[:, :], -1.0, BIG, ALU.add, ALU.mult))
                do(v.tensor_tensor_scan(Y[:, ::st], T[:, ::st], Xin[:, ::st], ini, ALU.add, ALU.max))
            else:
                do(v.tensor_tensor_scan(Y[:, ::st], samef[:, ::st], Xin[:, ::st], ini, ALU.mult, ALU.add))
            to_pe.give(v.nop())
            o = 0 if back else 1
            do(v.memset(CC[:, NS:NS + 1] if back else CC[:, 0:1], ini))
            from_pe.take(v)
            d0 = PC if is_max else chain[:, :]
            do(v.tensor_tensor_scan(CC[:, o:o + NS][:, ::st], d0[:, ::st], ps[0:H, 0, 0:NS][:, ::st], ini,
                                    ALU.add if is_max else ALU.mult, ALU.max if is_max else ALU.add))
            to_pe.give(v.nop())
            if is_max:
                do(v.tensor_scalar(T2, carry[:, :, :], -1.0, BIG, ALU.add, ALU.mult))
            from_pe.take(v)
            do(v.tensor_copy(CI, ps[0:RB, 1, 0:NB * H]))
            ci = CI.rearrange("p (b h) -> p b h", b=NB)
            cm = T2 if is_max else carry[:, :, :]
            do(v.tensor_tensor(row4(T), bc(cm.unsqueeze(2), [RB, NB, H, P]), bc(ci.unsqueeze(3), [RB, NB, H, P]),
                               ALU.add if is_max else ALU.mult))
            do(v.tensor_tensor(Y, Y, T, ALU.max if is_max else ALU.add))

        def scan_pe(pe, from_v, to_v, Y, back):
            from_v.take(pe)
            e = 0 if back else P - 1
            for b in range(NB):
                last = pe.transpose(ps[0:H, 0, b * RB:(b + 1) * RB], row4(Y)[:, b, :, e], ident[0:RB, 0:RB])
            to_v.give(last)
            from_v.take(pe)
            o = 1 if back else 0
            for b in range(NB):
                last = pe.transpose(ps[0:RB, 1, b * H:(b + 1) * H], CC[:, o + b * RB:o + (b + 1) * RB], ident[0:H, 0:H])
            to_v.give(last)

        def total_v(v, do, to_pe, from_pe, Xin, Y, M, T, kind):
            scan_v(v, do, to_pe, from_pe, Xin, Y, T, kind, False)
            scan_v(v, do, to_pe, from_pe, Y, M, T, "max", True)

        def total_pe(pe, from_v, to_v, Y, M):
            scan_pe(pe, from_v, to_v, Y, False)
            scan_pe(pe, from_v, to_v, M, True)

        def to_rows_pe(pe, src, bank):
            for b in range(NB):
                for h in range(H):
                    last = pe.transpose(ps[0:RB, bank + b, h * P:(h + 1) * P], src[:, b * RB:(b + 1) * RB, h], ident[:, :])
            return last

        def to_edges_pe(pe, X, bank):
            for h in range(H):
                for b in range(NB):
                    last = pe.transpose(ps[:, bank + h, b * RB:(b + 1) * RB], row4(X)[:, b, h, :], ident[0:RB, 0:RB])
            return last

        NC0 = NREL * WN0
        HN = A1[:, 0:NT * NC0].rearrange("p (t r w) -> p t r w", t=NT, r=NREL)
        HNf = A1[:, 0:NT * NC0].rearrange("p (t w) -> p t w", t=NT)
        W0c = A2[:, 0:NC0].rearrange("p (r w) -> p r w", r=NREL)
        ATT = A2[:, 512:512 + 2 * NREL * P].rearrange("p (a r w) -> p a r w", a=2, r=NREL)
        WAT = A2[:, 1536:1536 + NREL * P].rearrange("p (r w) -> p r w", r=NREL)
        wrel = sb("wrel", [P, NREL])
        rl = SM[:, 130:130 + NREL]
        rmax, rsum = SM[:, 134:135], SM[:, 135:136]
        NDA = sb("NDA", [P, NT * 32])
        nda = NDA[:, :].rearrange("p (t w) -> p t w", t=NT)

        def l0_prep_sp(sp, s_wd):
            sp.dma_start(W0c[:, :, 0:D], W_in.rearrange("r i o -> i r o")).then_inc(s_wd, 16)
            sp.dma_start(ATT[:, 0].rearrange("p r w -> p (r w)"),
                         as_in.rearrange("r h c -> (r h c)").partition_broadcast(P)).then_inc(s_wd, 16)
            sp.dma_start(ATT[:, 1].rearrange("p r w -> p (r w)"),
                         ad_in.rearrange("r h c -> (r h c)").partition_broadcast(P)).then_inc(s_wd, 16)
            sp.dma_start(rl, relw_in.partition_broadcast(P)).then_inc(s_wd, 16)

        def l0_prep_v(v, do, s_wd, s_pw, s_pwc):
            v.wait_ge(s_wd, 64)
            for a in range(2):
                do(v.tensor_tensor(WAT, W0c[:, :, 0:D], ATT[:, a], ALU.mult))
                for r in range(NREL):
                    ins = v.tensor_reduce(W0c[:, r, D + a * H:D + (a + 1) * H],
                                          WAT[:, r].rearrange("p (h c) -> p h c", h=H), AX, ALU.add)
                do(ins)
            do(v.tensor_reduce(rmax, rl, AX, ALU.max))
            do(v.tensor_scalar(wrel[:, :], rl, rmax, None, ALU.subtract))

        def l0_after_v(v, do):
            a_s = HN[:, :, :, D:D + H]
            a_d = HN[:, :, :, D + H:D + 2 * H]
            od = nda[:, :, 0:NREL * H]
            os_ = nda[:, :, NREL * H:2 * NREL * H]
            for r in range(NREL):
                v.tensor_copy(od[:, :, r * H:(r + 1) * H], a_d[:, :, r, :])
                ins = v.tensor_tensor(os_[:, :, r * H:(r + 1) * H], a_s[:, :, r, :], a_d[:, :, r, :], ALU.add)
            do(ins)
            do(v.scalar_tensor_tensor(os_, os_, 0.2, os_, ALU.mult, ALU.max))

        def l0_after_sp(sp, s_st):
            for r in range(NREL):
                sp.dma_start(tab0[r * NP:(r + 1) * NP, :].rearrange("(t p) w -> p t w", p=P),
                             HN[:, :, r, 0:WA0]).then_inc(s_st, 16)
            sp.wait_ge(s_st, 16 * NREL)

        AS = A3[:, 0:NS * H].rearrange("p (s h) -> p s h", h=H)
        ADS = A2[:, 0:NS * 24].rearrange("p (s w) -> p s w", w=24)
        ADSf = A2[:, 0:NS * 24]
        CS = A2[:, NS * 24:NS * 24 + NS * XC].rearrange("p (s w) -> p s w", w=XC)
        CSf = A2[:, NS * 24:NS * 24 + NS * XC]
        SCR = A3[:, 1664:3328].rearrange("p (s h) -> p s h", h=H)
        WT = A3[:, 3328:4992]
        WTv = WT.rearrange("p (s h) -> p s h", h=H)
        MK = SM[:, 0:NS]
        R_ = [A1[0:RB, 2048 * k:2048 * (k + 1)] for k in range(5)]
        ACC = hf[0:RB, 0:2048]
        ADS_N = 24

        def l0_use(v, i, h, rows, look, prod, s_c):
            v.tensor_copy(AS[:, ds(i * (2 * G) + h * G, G), :], rows[:, h, :, D:D + H])
            v.tensor_copy(ADS[:, ds(i * (2 * G) + h * G, G), :], look).then_inc(s_c, 1)
            hold(v, s_c, 2 * i + (h + 1))

        def l0_softmax():
            s_c, s_x1, s_x2, s_e1 = sem("l0s_c"), sem("l0s_x1"), sem("l0s_x2"), sem("l0s_e1")
            s_vp, s_pv, s_w = sem("l0s_vp"), sem("l0s_pv"), sem("l0s_w")
            X, S, Y, M, T = R_
            with nc.Block() as block:
                @block.scalar
                def _(a):
                    a.wait_ge(s_w, 1)
                    a.activation(wrel[:, :], wrel[:, :], ACT.Exp, accum_out=rsum).then_inc(s_w, 1)
                    for r in range(NREL):
                        a.wait_ge(s_x1, r + 1)
                        a.activation(X, X, ACT.Exp).then_inc(s_e1, 1)
                        a.activation(S, S, ACT.Exp).then_inc(s_e1, 1)

                @block.tensor
                def _(pe):
                    vp, pv = Hand(s_vp), Hand(s_pv)
                    for r in range(NREL):
                        vp.take(pe)
                        to_rows_pe(pe, SCR, 0)
                        pv.give(to_rows_pe(pe, ADS[:, :, NREL * H + r * H:NREL * H + (r + 1) * H], 4))
                        total_pe(pe, vp, pv, Y, M)
                        total_pe(pe, vp, pv, Y, M)
                        vp.take(pe)
                        pv.give(to_edges_pe(pe, S, 2))
                    vp.take(pe)
                    to_edges_pe(pe, ACC, 0)
                    for b in range(NB):
                        last = pe.transpose(ps[:, 4, b * RB:(b + 1) * RB], is_last[:, b, :], ident[0:RB, 0:RB])
                    pv.give(last)

                @block.vector
                def _(v):
                    do = Chain(v, s_c)
                    vp, pv = Hand(s_vp), Hand(s_pv)
                    v.nop().then_inc(s_w, 1)
                    v.wait_ge(s_w, 2)
                    do(v.reciprocal(rmax, rsum))
                    do(v.tensor_scalar(wrel[:, :], wrel[:, :], rmax, None, ALU.mult))
                    for r in range(NREL):
                        do(v.tensor_scalar(MK, t3T[:, :], float(r), None, ALU.is_equal))
                        do(v.tensor_tensor(SCR, AS, ADS[:, :, r * H:(r + 1) * H], ALU.add))
                        sf = A3[:, 1664:3328]
                        do(v.scalar_tensor_tensor(sf, sf, 0.2, sf, ALU.mult, ALU.max))
                        do(v.tensor_tensor(SCR, SCR, bc(MK.unsqueeze(2), [P, NS, H]), ALU.mult))
                        do(v.tensor_scalar(MK, MK, -1.0, NEG, ALU.add, ALU.mult))
                        do(v.tensor_tensor(SCR, SCR, bc(MK.unsqueeze(2), [P, NS, H]), ALU.add))
                        vp.give(v.nop())
                        pv.take(v)
                        do(v.tensor_copy(X, psf[0:RB, 0:2048]))
                        do(v.tensor_copy(S, psf[0:RB, 2048:4096]))
                        total_v(v, do, vp, pv, X, Y, M, T, "max")
                        do(v.tensor_tensor(M, M, S, ALU.max))
                        do(v.tensor_tensor(X, X, M, ALU.subtract))
                        do(v.tensor_tensor(S, S, M, ALU.subtract))
                        v.nop().then_inc(s_x1, 1)
                        v.wait_ge(s_e1, 2 * (r + 1))
                        total_v(v, do, vp, pv, X, Y, M, T, "sum")
                        do(v.tensor_tensor(M, M, S, ALU.add))
                        do(v.reciprocal(M, M))
                        do(v.tensor_scalar(M, M, wrel[0:RB, r:r + 1], None, ALU.mult))
                        do(v.tensor_tensor(X, X, M, ALU.mult))
                        do(v.tensor_tensor(ACC, ACC, X, ALU.add) if r else v.tensor_copy(ACC, X))
                        do(v.tensor_tensor(S, S, M, ALU.mult))
                        do(v.tensor_tensor(row4(S), row4(S), bc(is_last[:, :, :].unsqueeze(2), [RB, NB, H, P]), ALU.mult))
                        vp.give(v.nop())
                        pv.take(v)
                        for h in range(H):
                            ins = v.tensor_copy(CS[:, :, r * H + h], ps[:, 2 + h, 0:NS])
                        do(ins)
                    vp.give(v.nop())
                    pv.take(v)
                    for h in range(H):
                        ins = v.tensor_copy(WTv[:, :, h], ps[:, h, 0:NS])
                    do(ins)
                    do(v.tensor_copy(CS[:, :, XN], ps[:, 4, 0:NS]))

        CO = A3[:, 0:NT * XP].rearrange("p (t w) -> p t w", w=XP)
        HB = [A2[:, 3200 * k:3200 * (k + 1)].rearrange("p (t d) -> p t d", t=NT) for k in range(4)]
        BIA = A3[:, 512:512 + NREL * D].rearrange("p (r d) -> p r d", r=NREL)
        CF = A3[:, 1024:1024 + NT * H].rearrange("p (t h) -> p t h", h=H)
        ABS = A3[:, 1152:1152 + NT]

        def l0_combine_sp(sp, s_e):
            sp.wait_ge(s_e, 1)
            for r in range(NREL):
                sp.dma_start(HB[r], tab0[r * NP:(r + 1) * NP, 0:D].rearrange("(t p) w -> p t w", p=P)).then_inc(s_e, 16)
            sp.dma_start(BIA.rearrange("p r d -> p (r d)"), bias_in.rearrange("r d -> (r d)").partition_broadcast(P)).then_inc(s_e, 16)
            sp.wait_ge(s_e, 65)

        def l0_combine(v, do, s_e):
            v.nop().then_inc(s_e, 1)
            do(v.tensor_tensor(xf, xf, psf[:, 0:NT * P], ALU.add))
            do(v.tensor_copy(CO[:, :, 0:XC], ps[:, 7, 0:NT * XP].rearrange("p (t w) -> p t w", w=XP)[:, :, 0:XC]))
            do(v.tensor_scalar(ABS, CO[:, :, XN], -1.0, 1.0, ALU.mult, ALU.add))
            v.wait_ge(s_e, 65)
            for r in range(NREL):
                do(v.tensor_scalar(CF, bc(ABS.unsqueeze(2), [P, NT, H]), wrel[:, r:r + 1], None, ALU.mult))
                do(v.tensor_tensor(CF, CF, CO[:, :, r * H:(r + 1) * H], ALU.add))
                t4 = HB[3].rearrange("p t (h c) -> p t h c", h=H)
                do(v.tensor_tensor(t4, HB[r].rearrange("p t (h c) -> p t h c", h=H),
                                   bc(CF.unsqueeze(3), [P, NT, H, C]), ALU.mult))
                do(v.tensor_tensor(x[:, :, :], x[:, :, :], HB[3], ALU.add))
                do(v.tensor_scalar(BIA[:, r, :], BIA[:, r, :], wrel[:, r:r + 1], None, ALU.mult))
                do(v.tensor_tensor(x[:, :, :], x[:, :, :], bc(BIA[:, r:r + 1, :], [P, NT, D]), ALU.add))

        node_stage("n0", [(t, W0c.rearrange("p r w -> p (r w)"), NC0, "va"[t % 2], copy_to(HNf[:, t, :])) for t in range(NT)],
                   prep_v=l0_prep_v, prep_sp=l0_prep_sp, after_sp=l0_after_sp, after_v=None)
        s_n0 = sem("n0_self")
        with nc.Block() as block:
            @block.vector
            def _(v):
                l0_after_v(v, Chain(v, s_n0))
        lookup_stage("k0", tab0, i0, WA0, 0, lambda r: NDA[:, ds(r >> 2, ADS_N)], ADS_N, l0_use)
        l0_softmax()
        sum_stage("m0", WT, extra=CSf, combine=l0_combine, combine_sp=l0_combine_sp)

        def finish():
            s_fin = sem("s_fin")
            with nc.Block() as block:
                @block.sync
                def _(sp):
                    sp.dma_start(out[0:FULL * P, :].rearrange("(t p) d -> p t d", p=P), x[:, 0:FULL, :]).then_inc(s_fin, 16)
                    sp.dma_start(out[FULL * P:N, :], x[0:REST, FULL, :]).then_inc(s_fin, 16)
                    sp.wait_ge(s_fin, 32)

        end_layer()

        Bo = A1[:, 6400:6912].rearrange("p (k d) -> p k d", k=NBASE)
        BT = A1[:, 6912:7424].rearrange("p (k d) -> p k d", k=NBASE)
        W0o = A1[:, 7424:7552]
        WT1 = A1[:, 7552:7552 + (NRAT + 1) * D]
        Abc = A1[:, 8320:8320 + NRAT * NBASE]
        T1 = A2[:, 0:NT * NRAT * D].rearrange("p (t w) -> p t w", t=NT)
        dinv = sb("dinv", [P, NT])

        def l1_prep_sp(sp, s_wd):
            sp.dma_start(Bo, B_in.rearrange("k o i -> o k i")).then_inc(s_wd, 16)
            sp.dma_start(W0o, W0_in).then_inc(s_wd, 16)
            sp.dma_start(Abc, A_in.rearrange("r k -> (r k)").partition_broadcast(P)).then_inc(s_wd, 16)

        def l1_prep_pe(pe, s_wd, s_pw):
            pe.wait_ge(s_wd, 48)
            for k in range(NBASE):
                pe.transpose(ps[:, 7, k * P:(k + 1) * P], Bo[:, k, :], ident[:, :])
            pe.transpose(ps[:, 6, 0:P], W0o, ident[:, :]).then_inc(s_pw, 1)

        def l1_prep_v(v, do, s_wd, s_pw, s_pwc):
            v.wait_ge(s_wd, 48)
            v.wait_ge(s_pw, 1)
            do(v.tensor_copy(BT.rearrange("p k d -> p (k d)"), ps[:, 7, :]))
            do(v.tensor_copy(WT1[:, NRAT * D:], ps[:, 6, 0:P]))
            v.nop().then_inc(s_pwc, 1)
            for k in range(NBASE):
                for r in range(NRAT):
                    w, a = WT1[:, r * D:(r + 1) * D], Abc[:, r * NBASE + k:r * NBASE + k + 1]
                    ins = (v.scalar_tensor_tensor(w, BT[:, k, :], a, w, ALU.mult, ALU.add) if k
                           else v.tensor_scalar(w, BT[:, k, :], a, None, ALU.mult))
                do(ins)

        def l1_after_sp(sp, s_st):
            for r in range(NRAT):
                sp.dma_start(tab1[r * NP:(r + 1) * NP, :].rearrange("(t p) w -> p t w", p=P),
                             T1[:, :, r * D:(r + 1) * D]).then_inc(s_st, 16)
            sp.wait_ge(s_st, 16 * NRAT)

        def add_to_x(t):
            return lambda eng, src: eng.tensor_tensor(x[:, t, :], x[:, t, :], src, ALU.add)

        l1_prods = []
        for t in range(NT):
            l1_prods += [(t, WT1[:, 0:512], 512, "a", copy_to(T1[:, t, 0:512])),
                         (t, WT1[:, 512:640], 128, "v", copy_to(T1[:, t, 512:640])),
                         (t, WT1[:, 640:768], 128, "v", add_to_x(t))]
        node_stage("n1", l1_prods, prep_v=l1_prep_v, prep_pe=l1_prep_pe, prep_sp=l1_prep_sp, after_sp=l1_after_sp)

        def l1_edges():
            s_idx, s_oh, s_c, s_all, s_z, s_zd, s_v, s_sq = (
                sem(f"e1_{n}") for n in ("idx", "oh", "c", "all", "z", "zd", "v", "sq"))
            s_rows, s_mf = ([sem(f"e1_{n}{h}") for h in range(2)] for n in ("rows", "mf"))
            rows = A1[:, 0:2048].rearrange("p (h k w) -> p h k w", h=2, k=G)
            OH = A1[:, 2048:4096].rearrange("p (h k n) -> p h k n", h=2, k=G)
            LO_ = A1[:, 4096:5120].bitcast(BF16).rearrange("p (h k n) -> p h k n", h=2, k=G)
            HI_ = A1[:, 5120:5120 + G * NT].bitcast(BF16).rearrange("p (h k n) -> p h k n", h=2, k=G)
            ZR = A3[:, 0:NT * D]
            deg = SM[:, 0:NT]
            with nc.Block() as block:
                @block.gpsimd
                def _(g):
                    gather_loop(g, tab1, lambda h, k: rows[:, h, k, :], i1, s_idx, s_rows, [s_mf])

                @block.sync
                def _(sp):
                    sp.wait_ge(s_z, 1)
                    for k in range(G):
                        sp.dma_start(scat[k][0:NP, :].rearrange("(p a) d -> p (a d)", p=P), ZR).then_inc(s_zd, 16)
                    sp.wait_ge(s_zd, 16 * G)

                @block.scalar
                def _(a):
                    a.wait_ge(s_v, 1)
                    a.activation(deg, deg, ACT.Sqrt).then_inc(s_sq, 1)

                @block.vector
                def _(v):
                    do = Chain(v, s_c)
                    v.memset(ZR, 0.0).then_inc(s_z, 1)
                    with v.Fori(0, NI) as i:
                        for h in range(2):
                            s0 = i * (2 * G) + h * G
                            hold(v, s_mf[h], i + 1)
                            a, b = onehot_in(dlT[:, ds(s0, G)])
                            v.tensor_tensor(OH[:, h], a, b, ALU.is_equal)
                            a, b = onehot_in(loT[:, ds(s0, G)])
                            v.tensor_tensor(LO_[:, h], a, b, ALU.is_equal)
                            v.tensor_tensor(HI_[:, h], bc(iota_row[:, 0:NT].unsqueeze(1), [P, G, NT]),
                                            bc(hiT[:, ds(s0, G)].unsqueeze(2), [P, G, NT]), ALU.is_equal).then_inc(s_oh, 1)
                    v.wait_ge(s_all, 1)
                    do(v.tensor_tensor(xf, xf, psf[:, 0:NT * P], ALU.add))
                    do(v.tensor_copy(deg, ps[:, 7, 0:NT]))
                    do(v.scalar_tensor_tensor(deg[:, FULL:NT], iota_p[:, :], float(REST), deg[:, FULL:NT], ALU.is_ge, ALU.add))
                    v.nop().then_inc(s_v, 1)
                    v.wait_ge(s_sq, 1)
                    do(v.reciprocal(dinv[:, :], deg))

                @block.tensor
                def _(pe):
                    for h in range(2):
                        pe.sem_inc(s_mf[h], 1)
                    clear_acc(pe, 8)
                    regs = tile_regs(pe, "e1")
                    with pe.Fori(0, NI) as i:
                        for h in range(2):
                            hold(pe, s_oh, 2 * i + (h + 1))
                            hold(pe, s_rows[h], i * (16 * G) + 16 * G)
                            tiles = load_tiles(pe, regs, i * (2 * G) + h * G)
                            for k in range(G):
                                pe.matmul(psf[:, ds(tiles[k], P)], OH[:, h, k, :], rows[:, h, k, :],
                                          start=False, stop=False, skip_group_check=True)
                                last = pe.matmul(ps[:, 7, 0:NT], LO_[:, h, k, :], HI_[:, h, k, :],
                                                 start=False, stop=False, skip_group_check=True)
                            last.then_inc(s_mf[h], 1)
                    for h in range(2):
                        pe.wait_ge(s_mf[h], NI + 1)
                    pe.nop().then_inc(s_all, 1)

        l1_edges()
        end_layer()

        def l2_edges():
            s_c, s_var, s_std, s_lo = sem("e2_c"), sem("e2_var"), sem("e2_std"), sem("e2_lo")
            s_oht, s_seq, s_g, s_val, s_sum, s_gs, s_ix, s_prev, s_cc = (
                sem(f"e2_{n}") for n in ("oht", "seq", "g", "val", "sum", "gs", "ix", "prev", "cc"))
            s_dl, s_dlf, s_sr = ([sem(f"e2_{n}{h}") for h in range(2)] for n in ("dl", "dlf", "sr"))
            s_t = [sem(f"e2_t{k}") for k in range(G)]
            s_in, s_hid = sem("e2_in"), sem("e2_hid")
            OHT = A1[:, 0:2048].rearrange("p (h k n) -> p h k n", h=2, k=G)
            dlb = A1[:, 2048:3072].bitcast(BF16).rearrange("p (h n) -> p h n", h=2)
            srcb = A1[:, 3072:5120].rearrange("p (h n) -> p h n", h=2)
            SEQ = A1[:, 5120:7168].rearrange("p (h k n) -> p h k n", h=2, k=G)
            val = A1[:, 7168:9216].rearrange("p (h k n) -> p h k n", h=2, k=G)
            gs = A3[:, 0:2048].rearrange("p (h k n) -> p h k n", h=2, k=G)
            tmp = A3[:, 2048:3072].rearrange("p (k n) -> p k n", k=G)
            LOW = A3[:, 3072:3200]
            spare = SM[:, 192:193]
            cnt8, first8, d8 = SM[:, 200:208], SM[:, 208:216], SM[:, 216:224]
            SIX = SMI[:, 0:2 * G].rearrange("p (h k) -> p h k", h=2)
            look = [ps[:, 2 * h:2 * h + 2, :].rearrange("p a n -> p (a n)") for h in range(2)]
            tot = [ps[:, 4 + 2 * h:6 + 2 * h, :].rearrange("p a n -> p (a n)") for h in range(2)]
            with nc.Block() as block:
                @block.vector
                def _(v):
                    do = Chain(v, s_c)
                    layer_norm(v, do, s_var, s_std)
                    do(v.tensor_tensor(hid[:, :, :], hid[:, :, :], bc(dinv[:, :].unsqueeze(2), [P, NT, D]), ALU.mult))
                    do(v.tensor_scalar(LOW, iota_row[:, :], iota_p[:, 0:1], None, ALU.is_lt))
                    do(v.tensor_scalar(spare, iota_p[:, 0:1], float(NP), None, ALU.add))

                @block.scalar
                def _(a):
                    a.wait_ge(s_var, 1)
                    a.activation(std, var, ACT.Sqrt).then_inc(s_std, 1)

            with nc.Block() as block:
                @block.sync
                def _(sp):
                    with sp.Fori(0, NI) as i:
                        for h in range(2):
                            hold(sp, s_dlf[h], i + 1)
                            c0 = i * (2 * G * P) + h * (G * P)
                            sp.dma_start(dlb[:, h, :], dl_dram[ds(c0, G * P)].partition_broadcast(P)).then_inc(s_dl[h], 16)
                            sp.dma_start(srcb[:, h, :], srcrow_dram[ds(c0, G * P)].partition_broadcast(P)).then_inc(s_sr[h], 16)

                @block.vector
                def _(v):
                    for h in range(2):
                        v.sem_inc(s_dlf[h], 1)
                    with v.Fori(0, NI) as i:
                        for h in range(2):
                            s0 = i * (2 * G) + h * G
                            hold(v, s_dl[h], 16 * i + 16)
                            hold(v, s_g, 2 * i + (h + 1))
                            v.tensor_scalar(OHT[:, h].rearrange("p k n -> p (k n)"), dlb[:, h, :], iota_p[:, 0:1], None,
                                            ALU.is_equal).then_inc(s_oht, 1)
                            hold(v, s_sr[h], 16 * i + 16)
                            hold(v, s_sum, 2 * i + (h + 1))
                            v.tensor_tensor(SEQ[:, h], srcb[:, h, :].rearrange("p (k n) -> p k n", k=G),
                                            bc(srcT[:, ds(s0, G)].unsqueeze(2), [P, G, P]), ALU.is_equal).then_inc(s_seq, 1)
                            hold(v, s_seq, 2 * i + (h + 1))
                            hold(v, s_oht, 2 * i + (h + 1))
                            v.sem_inc(s_dlf[h], 1)
                            n0 = i * 8 + 4 * h

                            def step(ins, k):
                                ins.then_inc(s_cc, 1)
                                hold(v, s_cc, i * 10 + (5 * h + k))
                            step(v.tensor_tensor(tmp, SEQ[:, h], bc(LOW.unsqueeze(1), [P, G, P]), ALU.mult), 1)
                            step(v.tensor_reduce(cnt8, tmp, AX, ALU.add), 2)
                            step(v.tensor_scalar(d8, srcT[:, ds(s0, G)], spare, None, ALU.subtract), 3)
                            step(v.scalar_tensor_tensor(first8, cnt8, 0.0, d8, ALU.is_equal, ALU.mult), 4)
                            step(v.tensor_scalar(first8, first8, spare, None, ALU.add), 5)
                            hold(v, s_prev, 2 * i + (h + 1))
                            v.tensor_copy(SIX[:, h, :], first8).then_inc(s_ix, 1)
                            hold(v, s_ix, 2 * i + (h + 1))

                @block.tensor
                def _(pe):
                    pe.sem_inc(s_g, 2)
                    pe.sem_inc(s_sum, 2)
                    regs = tile_regs(pe, "e2")
                    with pe.Fori(0, NI) as i:
                        for h in range(2):
                            hold(pe, s_oht, 2 * i + (h + 1))
                            hold(pe, s_val, 2 * i + (h + 1))
                            tiles = load_tiles(pe, regs, i * (2 * G) + h * G)
                            for k in range(G):
                                last = pe.matmul(look[h][:, k * P:(k + 1) * P], OHT[:, h, k, :], hf[:, ds(tiles[k], P)],
                                                 start=True, stop=True)
                            last.then_inc(s_g, 1)
                            hold(pe, s_seq, 2 * i + (h + 1))
                            hold(pe, s_val, 2 * i + (h + 3))
                            hold(pe, s_gs, 2 * i + (h + 1))
                            for k in range(G):
                                last = pe.matmul(tot[h][:, k * P:(k + 1) * P], SEQ[:, h, k, :], val[:, h, k, :],
                                                 start=True, stop=True)
                            last.then_inc(s_sum, 1)

                @block.scalar
                def _(a):
                    a.sem_inc(s_val, 2)
                    a.sem_inc(s_gs, 2)
                    with a.Fori(0, NI) as i:
                        for h in range(2):
                            hold(a, s_g, 2 * i + (h + 3))
                            hold(a, s_sum, 2 * i + (h + 1))
                            a.activation(val[:, h].rearrange("p k n -> p (k n)"), look[h], ACT.Copy).then_inc(s_val, 1)
                            hold(a, s_sum, 2 * i + (h + 3))
                            hold(a, s_prev, 2 * i + (h + 1))
                            a.activation(gs[:, h].rearrange("p k n -> p (k n)"), tot[h], ACT.Copy).then_inc(s_gs, 1)

                @block.gpsimd
                def _(g):
                    g.sem_inc(s_prev, 1)
                    for k in range(G):
                        g.dma_start(scat[k][NP:NDUMP, :], zeros[:, 0:D]).then_inc(s_t[k], 16)
                    with g.Fori(0, NI) as i:
                        for h in range(2):
                            hold(g, s_gs, 2 * i + (h + 3))
                            hold(g, s_ix, 2 * i + (h + 1))
                            for k in range(G):
                                hold(g, s_t[k], i * 32 + (16 * h + 16))
                                g.indirect_dma_start(out=scat[k], out_offset=bass.IndirectOffsetOnAxis(ap=SIX[:, h, k:k + 1], axis=0),
                                                     in_=gs[:, h, k, :], in_offset=None,
                                                     compute_op=ALU.add).then_inc(s_t[k], 16)
                            g.sem_inc(s_prev, 1)
                    for k in range(G):
                        g.wait_ge(s_t[k], 16 + 32 * NI)

            TB = [A2[:, 3200 * k:3200 * (k + 1)] for k in range(5)] + [A1[:, 3200 * k:3200 * (k + 1)] for k in range(3)]
            with nc.Block() as block:
                @block.sync
                def _(sp):
                    for k in range(G):
                        sp.dma_start(TB[k].rearrange("p (t d) -> p t d", t=NT),
                                     scat[k][0:NP, :].rearrange("(t p) d -> p t d", p=P)).then_inc(s_t2[k], 16)
                    for k in range(G):
                        sp.wait_ge(s_t2[k], 16)

                @block.vector
                def _(v):
                    do = Chain(v, s_in)
                    v.wait_ge(s_t2[0], 16)
                    for k in range(1, G):
                        v.wait_ge(s_t2[k], 16)
                        do(v.tensor_tensor(TB[0], TB[0], TB[k], ALU.add))
                    do(v.tensor_tensor(hid[:, :, :], TB[0].rearrange("p (t d) -> p t d", t=NT),
                                       bc(dinv[:, :].unsqueeze(2), [P, NT, D]), ALU.mult))

        s_t2 = [sem(f"e2_l{k}") for k in range(G)]
        l2_edges()
        W2o, W2T = A1[:, 0:P], A1[:, P:2 * P]

        def l2_prep_sp(sp, s_wd):
            sp.dma_start(W2o, W2_in).then_inc(s_wd, 16)

        def l2_prep_pe(pe, s_wd, s_pw):
            pe.wait_ge(s_wd, 16)
            pe.transpose(ps[:, 7, 0:P], W2o, ident[:, :]).then_inc(s_pw, 1)

        def l2_prep_v(v, do, s_wd, s_pw, s_pwc):
            v.wait_ge(s_pw, 1)
            do(v.tensor_copy(W2T, ps[:, 7, 0:P]))
            v.nop().then_inc(s_pwc, 1)

        def add_relu(t):
            return lambda eng, src: eng.scalar_tensor_tensor(x[:, t, :], src, 0.0, x[:, t, :], ALU.max, ALU.add)

        node_stage("n2", [(t, W2T, D, "v", add_relu(t)) for t in range(NT)], norm=False,
                   prep_v=l2_prep_v, prep_pe=l2_prep_pe, prep_sp=l2_prep_sp)
        end_layer()

        KV = A2[:, 0:NT * 4 * D].rearrange("p (t w) -> p t w", t=NT)
        WALL = A2[:, 12800:13312]
        BALL = A2[:, 13312:13824]
        ALf = A3[:, 0:NS * H]

        def l3_layer(l):
            Wq, Wk, Wv, Ws, bq, bk, bv, bs = l3[8 * l:8 * l + 8]
            tag = f"t{l}"

            def prep_sp(sp, s_wd):
                for k, (w, b) in enumerate(((Wk, bk), (Wv, bv), (Wq, bq), (Ws, bs))):
                    sp.dma_start(WALL[:, k * D:(k + 1) * D], w).then_inc(s_wd, 16)
                    sp.dma_start(BALL[:, k * D:(k + 1) * D], b.partition_broadcast(P)).then_inc(s_wd, 16)

            def prep_v(v, do, s_wd, s_pw, s_pwc):
                v.wait_ge(s_wd, 128)

            def put(t):
                return lambda eng, src: eng.tensor_tensor(KV[:, t, :], src, BALL, ALU.add)

            def after_sp(sp, s_st):
                sp.dma_start(tab3.rearrange("(t p) w -> p t w", p=P), KV[:, :, 0:2 * D]).then_inc(s_st, 16)
                sp.wait_ge(s_st, 16)

            node_stage(tag + "n", [(t, WALL, 4 * D, "v", put(t)) for t in range(NT)], norm=(l == 0),
                       prep_v=prep_v, prep_sp=prep_sp, after_sp=after_sp)

            def use(v, i, h, rows, look, prod, s_c):
                pk = prod[:, h * 1024:(h + 1) * 1024]
                v.tensor_tensor(pk.rearrange("p (k d) -> p k d", k=G), rows[:, h, :, 0:D], look, ALU.mult).then_inc(s_c, 1)
                hold(v, s_c, 4 * i + (2 * h + 1))
                v.tensor_reduce(ALf[:, ds(i * (2 * G * H) + h * (G * H), G * H)],
                                pk.rearrange("p (q c) -> p q c", c=C), AX, ALU.add).then_inc(s_c, 1)
                hold(v, s_c, 4 * i + (2 * h + 2))

            lookup_stage(tag + "k", tab3, i3, 2 * D, D, lambda r: A2[:, ds(r * 4 + 2 * D, D)], D, use)

            s_c, s_x1, s_e1, s_vp, s_pv = (sem(f"{tag}s_{n}") for n in ("c", "x1", "e1", "vp", "pv"))
            X, Y, M, T = R_[0:4]
            with nc.Block() as block:
                @block.scalar
                def _(a):
                    a.wait_ge(s_x1, 1)
                    a.activation(X, X, ACT.Exp, scale=float(C) ** -0.5).then_inc(s_e1, 1)

                @block.tensor
                def _(pe):
                    vp, pv = Hand(s_vp), Hand(s_pv)
                    pv.give(to_rows_pe(pe, AS, 0))
                    total_pe(pe, vp, pv, Y, M)
                    total_pe(pe, vp, pv, Y, M)
                    vp.take(pe)
                    pv.give(to_edges_pe(pe, X, 2))

                @block.vector
                def _(v):
                    do = Chain(v, s_c)
                    vp, pv = Hand(s_vp), Hand(s_pv)
                    pv.take(v)
                    do(v.tensor_copy(X, psf[0:RB, 0:2048]))
                    total_v(v, do, vp, pv, X, Y, M, T, "max")
                    do(v.tensor_tensor(X, X, M, ALU.subtract))
                    v.nop().then_inc(s_x1, 1)
                    v.wait_ge(s_e1, 1)
                    total_v(v, do, vp, pv, X, Y, M, T, "sum")
                    do(v.tensor_scalar(M, M, 1e-16, None, ALU.max))
                    do(v.reciprocal(M, M))
                    do(v.tensor_tensor(X, X, M, ALU.mult))
                    vp.give(v.nop())
                    pv.take(v)
                    for h in range(H):
                        ins = v.tensor_copy(WTv[:, :, h], ps[:, 2 + h, 0:NS])
                    do(ins)

            def combine(v, do, s_e):
                do(v.tensor_tensor(hid[:, :, :], psf[:, 0:NT * P].rearrange("p (t d) -> p t d", t=NT),
                                   KV[:, :, 3 * D:4 * D], ALU.add))
                do(v.tensor_scalar(hid[:, :, :], hid[:, :, :], 0.0, None, ALU.max))
                if l == 1:
                    do(v.tensor_tensor(xf, xf, hf, ALU.add))

            sum_stage(tag + "m", WT, combine=combine)

        l3_layer(0)
        end_layer()
        l3_layer(1)
        finish()


_L3 = [f"L3_gnn_{k}{l}" for l in range(2) for k in ("Wq", "Wk", "Wv", "Ws", "bq", "bk", "bv", "bs")]
_INS = ["x", "src", "dst", "edge_type_3", "edge_type_5", "L0_gnn_W", "L0_gnn_att_src", "L0_gnn_att_dst",
        "L0_gnn_bias", "L0_gnn_rel_w", "L1_gnn_B", "L1_gnn_A", "L1_gnn_W0", "L2_gnn_weight"] + _L3


def kernel(**inputs):
    import numpy as _np
    import concourse.bacc as _bacc
    from concourse import mybir as _mybir
    from concourse.bass_utils import run_bass_kernel_spmd as _run

    nc = _bacc.Bacc("TRN2", target_bir_lowering=False, num_devices=1)
    arrays, args = {}, {}
    for name in _INS:
        a = _np.ascontiguousarray(inputs[name])
        arrays[f"in_{name}_dram"] = a
        args[name] = nc.dram_tensor(f"in_{name}_dram", a.shape, _mybir.dt.from_np(a.dtype), kind="ExternalInput").ap()
    out = nc.dram_tensor("out_0_dram", (N, D), F32, kind="ExternalOutput").ap()
    A = [args[n] for n in _INS]
    build(nc, A[0], A[1], A[2], A[3], A[4], A[5], A[6], A[7], A[8], A[9], A[10], A[11], A[12], A[13], A[14:], out)
    r = _run(nc, [arrays], core_ids=[0])
    return r.results[0]["out_0_dram"]
```

```python
from contextlib import ExitStack

import concourse.bass as bass
from concourse import mybir

F32 = mybir.dt.float32
BF16 = mybir.dt.bfloat16
F16 = mybir.dt.float16
I32 = mybir.dt.int32
ALU = mybir.AluOpType
ACT = mybir.ActivationFunctionType
AX = mybir.AxisListType.X
ds = bass.ds

P = 128
N, D = 3125, 128
E = 50000
H, C = 4, 32
NREL, NRAT, NBASE = 3, 5, 4
NT = -(-N // P)
NP = NT * P
FULL = N // P
REST = N - FULL * P
ET = -(-E // P)
EREST = E - (ET - 1) * P
RB = 104
NB = 4
NS = RB * NB
assert NS >= ET + NT - 1
G = 8
NI = NS // (2 * G)
assert NI * 2 * G == NS
XW = H * P
WA0 = D + H
WN0 = D + 2 * H
BIG = 1e37
NEG = 1e9
EPS = 1e-5
NDUMP = NP + P


class Chain:

    def __init__(self, eng, sem):
        self.eng, self.sem, self.n = eng, sem, 0

    def __call__(self, ins):
        self.n += 1
        ins.then_inc(self.sem, 1)
        self.eng.wait_ge(self.sem, self.n)


class Hand:

    def __init__(self, sem):
        self.sem, self.given, self.taken = sem, 0, 0

    def give(self, ins, by=1):
        self.given += by
        ins.then_inc(self.sem, by)

    def take(self, eng, by=1):
        self.taken += by
        eng.wait_ge(self.sem, self.taken)


def bc(ap, shape):
    return ap.to_broadcast(shape)


def build(nc, x_in, src_in, dst_in, t3_in, t5_in, W_in, as_in, ad_in, bias_in, relw_in,
          B_in, A_in, W0_in, W2_in, l3, out):
    ctx = ExitStack()
    with ctx:
        def sb(name, shape, dt=F32):
            return ctx.enter_context(nc.sbuf_tensor(name, shape, dt))

        layer_sems = []

        def sem(name):
            s = nc.alloc_semaphore(name=name)
            layer_sems.append(s)
            return s

        def end_layer():
            nc.clear_and_free_semaphores(layer_sems)
            layer_sems.clear()
            nc.all_engine_barrier()

        def dram(name, shape, dt=F32):
            return nc.dram_tensor(name, shape, dt, kind="Internal").ap()

        edge_tab = dram("edge_tab", [ET, 4 * P], I32)
        dl_dram = dram("dl_dram", [NS * P], BF16)
        srcrow_dram = dram("srcrow_dram", [NS * P])
        tab0 = dram("tab0", [NREL * NP, WA0])
        tab1 = dram("tab1", [NRAT * NP, D])
        tab3 = dram("tab3", [NP, 2 * D])
        spill = dram("spill", [P, NS * D])
        scat = [dram(f"scat{k}", [NDUMP, D]) for k in range(G)]

        iota_row = sb("iota_row", [P, P])
        iota16 = sb("iota16", [P, P], F16)
        iota_p = sb("iota_p", [P, 1])
        ident = sb("ident", [P, P])
        ones = sb("ones", [P, P])
        zeros = sb("zeros", [P, 512])
        dlT = sb("dlT", [P, NS])
        dl16 = sb("dl16", [P, NS], F16)
        srcT = sb("srcT", [P, NS])
        t3T = sb("t3T", [P, NS])
        loT = sb("loT", [P, NS])
        hiT = sb("hiT", [P, NS])
        i0 = sb("i0", [P, NS], I32)
        i1 = sb("i1", [P, NS], I32)
        i3 = sb("i3", [P, NS], I32)
        tnI = sb("tnI", [1, NS], I32)
        Kr = sb("Kr", [RB, NB, P])
        same_f = sb("same_f", [RB, NB, H, P])
        same_b = sb("same_b", [RB, NB, H, P])
        carry_f = sb("carry_f", [RB, NB, P])
        carry_b = sb("carry_b", [RB, NB, P])
        is_last = sb("is_last", [RB, NB, P])
        chain_f = sb("chain_f", [H, NS])
        chain_b = sb("chain_b", [H, NS])
        x = sb("x", [P, NT, D])
        hid = sb("hid", [P, NT, D])
        idx = sb("idx", [P, 2, G], I32)
        A1 = sb("A1", [P, 10240])
        A2 = sb("A2", [P, 16384])
        A3 = sb("A3", [P, 6144])
        SM = sb("SM", [P, 1024])
        SMI = sb("SMI", [P, 256], I32)

        ps = ctx.enter_context(nc.psum_tensor("ps", [P, 8, 512], F32))
        psf = ps[:, :, :].rearrange("p a b -> p (a b)")

        passed = ctx.enter_context(nc.semaphore("passed"))

        def hold(eng, s, value):
            eng.wait_ge(s, value)
            eng.sem_inc(passed, 1)

        cnt_cmp = A2[:, 0:9600].rearrange("p (j e) -> p j e", j=24)
        dst_i = A1[:, 0:400].bitcast(I32)
        dst_f = A1[:, 400:800]
        R = A1[:, 1024:1024 + NB * 512].bitcast(I32).rearrange("p (b q e) -> p b q e", b=NB, q=4)
        Rf = A1[:, 4096:4096 + NB * 512].rearrange("p (b q e) -> p b q e", b=NB, q=4)
        DL = A3[:, 0:512].rearrange("p (b e) -> p b e", b=NB)
        VAL = A3[:, 512:1024].rearrange("p (b e) -> p b e", b=NB)
        I0f = A3[:, 1024:1536].rearrange("p (b e) -> p b e", b=NB)
        I1f = A3[:, 1536:2048].rearrange("p (b e) -> p b e", b=NB)
        TMP = A3[:, 2048:2560].rearrange("p (b e) -> p b e", b=NB)
        DLB = A3[:, 2560:2816].bitcast(BF16).rearrange("p (b e) -> p b e", b=NB)
        KK = A3[:, 2816:2848].rearrange("p (a b h) -> p a b h", a=2, b=NB)
        TJ = A3[:, 2848:2948].rearrange("p (b j) -> p b j", b=NB)
        KL = A3[:, 3072:3072 + NS + 1]
        KF = A3[:, 3520:3520 + NS + 1]
        cnt = SM[:, 0:26]
        Fv = SM[:, 32:58]
        af = SM[:, 64:90]
        lf = SM[:, 96:122]
        nn = SM[:, 128:153]
        Oc = SM[:, 160:185]
        dl_ = SM[:, 192:217]
        sval = SM[:, 224:228]
        tn = SM[:, 232:236]
        tnc = SM[:, 240:244]
        te = SM[:, 248:252]
        tn128 = SM[:, 256:260]
        PL = SM[:, 288:320].rearrange("p (a b h) -> p a b h", a=2, b=NB)
        pad_i = SMI[:, 0:96]
        Fi = SMI[:, 96:122]
        Li = SMI[:, 128:154]
        te_i = SMI[:, 160:164]
        LO = A2[:, 0:NS].bitcast(I32)
        HI = A2[:, 512:512 + NS].bitcast(I32)
        HIf = A2[:, 1024:1024 + NS]
        VT = A2[:, 1536:1536 + NS]

        s_pad, s_tab, s_dst, s_c = sem("s_pad"), sem("s_tab"), sem("s_dst"), sem("s_c")
        s_io, s_io2, s_id, s_cnt, s_F, s_te, s_R = (sem("s_io"), sem("s_io2"), sem("s_id"), sem("s_cnt"),
                                                    sem("s_F"), sem("s_te"), sem("s_R"))
        s_row, s_tr, s_kk, s_kt, s_sh, s_sht, s_dd, s_x = (sem("s_row"), sem("s_tr"), sem("s_kk"), sem("s_kt"),
                                                           sem("s_sh"), sem("s_sht"), sem("s_dd"), sem("s_x"))
        QUANT = [DL, Rf[:, :, 1, :], I0f, I1f, Rf[:, :, 2, :]]

        with nc.Block() as block:
            @block.sync
            def _(sp):
                sp.dma_start(dst_i[0:125, :], dst_in.rearrange("(p e) -> p e", p=125)).then_inc(s_dst, 16)
                for q, arr in enumerate((dst_in, src_in, t3_in, t5_in)):
                    sp.dma_start(edge_tab[0:ET - 1, q * P:(q + 1) * P],
                                 arr[0:(ET - 1) * P].rearrange("(t e) -> t e", e=P)).then_inc(s_tab, 16)
                    sp.dma_start(edge_tab[ET - 1:ET, q * P:q * P + EREST],
                                 arr[(ET - 1) * P:E].rearrange("(a e) -> a e", a=1)).then_inc(s_tab, 16)
                sp.wait_ge(s_pad, 2)
                for q in range(4):
                    sp.dma_start(edge_tab[ET - 1:ET, q * P + EREST:(q + 1) * P],
                                 pad_i[0:1, (48 if q else 0):(48 if q else 0) + P - EREST]).then_inc(s_tab, 16)
                sp.dma_start(x[:, 0:FULL, :], x_in[0:FULL * P, :].rearrange("(t p) d -> p t d", p=P)).then_inc(s_x, 16)
                sp.wait_ge(s_pad, 3)
                sp.dma_start(x[0:REST, FULL, :], x_in[FULL * P:N, :]).then_inc(s_x, 16)
                sp.wait_ge(s_row, 1)
                sp.dma_start(dl_dram.rearrange("(b p e) -> p b e", b=NB, e=P), DLB[0:RB]).then_inc(s_dd, 16)
                sp.dma_start(srcrow_dram.rearrange("(b p e) -> p b e", b=NB, e=P), Rf[0:RB, :, 1, :]).then_inc(s_dd, 16)
                sp.wait_ge(s_dd, 32)
                sp.wait_ge(s_x, 32)

            @block.gpsimd
            def _(g):
                g.memset(ident[:, :], 0.0).then_inc(s_io, 1)
                g.iota(iota_row[:, :], [[1, P]], base=0, channel_multiplier=0,
                       allow_small_or_imprecise_dtypes=True).then_inc(s_io, 1)
                g.iota(iota_p[:, :], [[0, 1]], base=0, channel_multiplier=1,
                       allow_small_or_imprecise_dtypes=True).then_inc(s_io, 1)
                g.iota(sval, [[RB, NB]], base=0, channel_multiplier=1,
                       allow_small_or_imprecise_dtypes=True).then_inc(s_io, 1)
                g.wait_ge(s_io, 1)
                g.affine_select(out=ident[:, :], in_=ident[:, :], compare_op=ALU.not_equal, fill=1.0,
                                base=0, pattern=[[-1, P]], channel_multiplier=1).then_inc(s_id, 1)
                g.wait_ge(s_tab, 16 * 12)
                g.wait_ge(s_te, 1)
                for b in range(NB):
                    g.indirect_dma_start(out=R[0:RB, b].rearrange("p q e -> p (q e)"), out_offset=None, in_=edge_tab[:, :],
                                         in_offset=bass.IndirectOffsetOnAxis(ap=te_i[0:RB, b:b + 1], axis=0)
                                         ).then_inc(s_R, 16)

            @block.tensor
            def _(pe):
                pe.wait_ge(s_cnt, 1)
                pe.matmul(ps[:, 7, 0:26], ones[0:125, :], cnt[0:125, :], start=True, stop=True).then_inc(s_F, 1)
                pe.wait_ge(s_id, 1)
                pe.wait_ge(s_row, 1)
                for q, Q in enumerate(QUANT):
                    for b in range(NB):
                        pe.transpose(ps[:, q, b * RB:(b + 1) * RB], Q[0:RB, b, :], ident[0:RB, 0:RB])
                for b in range(NB):
                    last = pe.transpose(ps[0:1, 5, b * RB:(b + 1) * RB], tnc[0:RB, b:b + 1], ident[0:RB, 0:RB])
                last.then_inc(s_tr, 1)
                pe.wait_ge(s_kk, 1)
                for a in range(2):
                    for b in range(NB):
                        last = pe.transpose(ps[0:H, 6 + a, b * RB:(b + 1) * RB], KK[0:RB, a, b, :], ident[0:RB, 0:RB])
                last.then_inc(s_kt, 1)
                pe.wait_ge(s_sh, 1)
                for b in range(NB):
                    pe.transpose(ps[0:RB, 0, b * H:(b + 1) * H], KL[0:H, b * RB:(b + 1) * RB], ident[0:H, 0:H])
                for b in range(NB):
                    last = pe.transpose(ps[0:RB, 0, 16 + b * H:16 + (b + 1) * H],
                                        KF[0:H, 1 + b * RB:1 + (b + 1) * RB], ident[0:H, 0:H])
                last.then_inc(s_sht, 1)

            @block.vector
            def _(v):
                do = Chain(v, s_c)
                do(v.memset(ones[:, :], 1.0))
                do(v.memset(zeros[:, :], 0.0))
                v.memset(pad_i[:, 0:48], 8192).then_inc(s_pad, 1)
                v.memset(pad_i[:, 48:96], 0).then_inc(s_pad, 1)
                v.memset(x[:, FULL, :], 0.0).then_inc(s_pad, 1)
                do(v.memset(cnt, 0.0))
                do(v.memset(cnt[:, 25:26], E / 125))
                v.wait_ge(s_dst, 16)
                do(v.tensor_copy(dst_f[0:125, :], dst_i[0:125, :]))
                for j in range(1, NT):
                    ins = v.tensor_scalar(cnt_cmp[0:125, j - 1, :], dst_f[0:125, :], float(P * j), None, ALU.is_lt)
                do(ins)
                do(v.tensor_reduce(cnt[0:125, 1:NT], cnt_cmp[0:125], AX, ALU.add))
                v.nop().then_inc(s_cnt, 1)
                v.wait_ge(s_F, 1)
                do(v.tensor_copy(Fv, ps[:, 7, 0:26]))
                do(v.tensor_copy(Fi, Fv))
                do(v.tensor_scalar(Fi, Fi, 7, None, ALU.arith_shift_right))
                do(v.tensor_copy(af, Fi))
                do(v.tensor_scalar(lf, Fv, -1.0, None, ALU.add))
                do(v.tensor_copy(Li, lf))
                do(v.tensor_scalar(Li, Li, 7, None, ALU.arith_shift_right))
                do(v.tensor_copy(lf, Li))
                do(v.tensor_tensor(nn, lf[:, 1:26], af[:, 0:25], ALU.subtract))
                do(v.tensor_scalar(nn, nn, 1.0, None, ALU.add))
                do(v.tensor_tensor(dl_, Fv[:, 1:26], Fv[:, 0:25], ALU.is_gt))
                do(v.tensor_tensor(nn, nn, dl_, ALU.mult))
                do(v.tensor_tensor_scan(Oc, ones[:, 0:25], nn, 0.0, ALU.mult, ALU.add))
                do(v.tensor_tensor(dl_, nn, Oc, ALU.subtract))
                do(v.tensor_tensor(dl_, dl_, af[:, 0:25], ALU.add))
                v.wait_ge(s_io, 4)
                do(v.tensor_tensor(TJ, bc(Oc.unsqueeze(1), [P, NB, NT]), bc(sval.unsqueeze(2), [P, NB, NT]), ALU.is_le))
                do(v.tensor_reduce(tn, TJ, AX, ALU.add))
                do(v.tensor_tensor(TJ, bc(iota_row[:, 0:NT].unsqueeze(1), [P, NB, NT]),
                                   bc(tn.unsqueeze(2), [P, NB, NT]), ALU.is_equal))
                do(v.tensor_tensor(TJ, TJ, bc(dl_.unsqueeze(1), [P, NB, NT]), ALU.mult))
                do(v.tensor_reduce(te, TJ, AX, ALU.add))
                do(v.tensor_tensor(te, te, sval, ALU.add))
                do(v.tensor_scalar(te, te, float(ET - 1), 0.0, ALU.min, ALU.max))
                do(v.tensor_copy(te_i, te))
                v.nop().then_inc(s_te, 1)
                do(v.tensor_scalar(tnc, tn, float(NT - 1), None, ALU.min))
                do(v.tensor_scalar(tn128, tn, float(P), None, ALU.mult))
                v.wait_ge(s_R, 16 * NB)
                do(v.tensor_copy(A1[0:RB, 4096:4096 + NB * 512], A1[0:RB, 1024:1024 + NB * 512].bitcast(I32)))
                dstf, srcf, t3f, t5f = (Rf[0:RB, :, q, :] for q in range(4))
                do(v.tensor_tensor(DL[0:RB], dstf, bc(tn128[0:RB].unsqueeze(2), [RB, NB, P]), ALU.subtract))
                do(v.tensor_scalar(VAL[0:RB], DL[0:RB], 0.0, None, ALU.is_ge))
                do(v.tensor_scalar(TMP[0:RB], DL[0:RB], float(P), None, ALU.is_lt))
                do(v.tensor_tensor(VAL[0:RB], VAL[0:RB], TMP[0:RB], ALU.mult))
                do(v.tensor_scalar(Kr[:, :, :], dstf, 1.0, None, ALU.add))
                do(v.tensor_tensor(Kr[:, :, :], Kr[:, :, :], VAL[0:RB], ALU.mult))
                do(v.tensor_scalar(Kr[:, :, :], Kr[:, :, :], -1.0, None, ALU.add))
                do(v.scalar_tensor_tensor(I0f[0:RB], t3f, float(NP), srcf, ALU.mult, ALU.add))
                do(v.scalar_tensor_tensor(I1f[0:RB], t5f, float(NP), srcf, ALU.mult, ALU.add))
                do(v.tensor_copy(DLB[0:RB], DL[0:RB]))
                v.nop().then_inc(s_row, 1)
                do(v.tensor_copy(KK[0:RB, 0], bc(Kr[:, :, P - 1:P], [RB, NB, H])))
                do(v.tensor_copy(KK[0:RB, 1], bc(Kr[:, :, 0:1], [RB, NB, H])))
                v.nop().then_inc(s_kk, 1)
                v.wait_ge(s_tr, 1)
                do(v.tensor_copy(dlT[:, :], ps[:, 0, 0:NS]))
                do(v.tensor_copy(dl16[:, :], ps[:, 0, 0:NS]))
                v.wait_ge(s_io, 2)
                do(v.tensor_copy(iota16[:, :], iota_row[:, :]))
                do(v.tensor_copy(srcT[:, :], ps[:, 1, 0:NS]))
                do(v.tensor_copy(i3[:, :], ps[:, 1, 0:NS]))
                do(v.tensor_copy(i0[:, :], ps[:, 2, 0:NS]))
                do(v.tensor_copy(i1[:, :], ps[:, 3, 0:NS]))
                do(v.tensor_copy(t3T[:, :], ps[:, 4, 0:NS]))
                do(v.tensor_scalar(tnI[:, :], ps[0:1, 5, 0:NS], float(P), None, ALU.mult))
                do(v.tensor_scalar(LO, i3[:, :], P - 1, None, ALU.bitwise_and))
                do(v.tensor_copy(loT[:, :], LO))
                do(v.tensor_scalar(HI, i3[:, :], 7, None, ALU.arith_shift_right))
                do(v.tensor_copy(HIf, HI))
                do(v.tensor_scalar(VT, dlT[:, :], 0.0, None, ALU.is_ge))
                do(v.scalar_tensor_tensor(VT, dlT[:, :], float(P), VT, ALU.is_lt, ALU.mult))
                do(v.scalar_tensor_tensor(HIf, HIf, 1.0, VT, ALU.add, ALU.mult))
                do(v.tensor_scalar(hiT[:, :], HIf, -1.0, None, ALU.add))
                do(v.memset(same_f[:, :, :, :], 0.0))
                do(v.memset(same_b[:, :, :, :], 0.0))
                for h in range(H):
                    v.tensor_tensor(same_f[:, :, h, 1:P], Kr[:, :, 1:P], Kr[:, :, 0:P - 1], ALU.is_equal)
                    ins = v.tensor_tensor(same_b[:, :, h, 0:P - 1], Kr[:, :, 1:P], Kr[:, :, 0:P - 1], ALU.is_equal)
                do(ins)
                v.wait_ge(s_kt, 1)
                do(v.memset(KL[0:H, 0:1], -5.0))
                do(v.memset(KF[0:H, NS:NS + 1], -6.0))
                do(v.tensor_copy(KL[0:H, 1:NS + 1], ps[0:H, 6, 0:NS]))
                do(v.tensor_copy(KF[0:H, 0:NS], ps[0:H, 7, 0:NS]))
                v.nop().then_inc(s_sh, 1)
                do(v.tensor_tensor(chain_f[:, :], KL[0:H, 1:NS + 1], KL[0:H, 0:NS], ALU.is_equal))
                do(v.tensor_tensor(chain_b[:, :], KF[0:H, 1:NS + 1], KF[0:H, 0:NS], ALU.is_equal))
                v.wait_ge(s_sht, 1)
                do(v.tensor_copy(PL[0:RB].rearrange("p a b h -> p (a b h)"), ps[0:RB, 0, 0:32]))
                do(v.tensor_tensor(carry_f[:, :, :], Kr[:, :, :], bc(PL[0:RB, 0, :, 0:1], [RB, NB, P]), ALU.is_equal))
                do(v.tensor_tensor(carry_b[:, :, :], Kr[:, :, :], bc(PL[0:RB, 1, :, 0:1], [RB, NB, P]), ALU.is_equal))
                do(v.tensor_scalar(is_last[:, :, 0:P - 1], same_b[:, :, 0, 0:P - 1], -1.0, 1.0, ALU.mult, ALU.add))
                do(v.tensor_scalar(is_last[:, :, P - 1:P], carry_b[:, :, P - 1:P], -1.0, 1.0, ALU.mult, ALU.add))
                do(v.tensor_tensor(is_last[:, :, :], is_last[:, :, :], VAL[0:RB], ALU.mult))


        hT = A3[:, 0:NT * P].rearrange("p (t n) -> p t n", t=NT)
        xf = x[:, :, :].rearrange("p t d -> p (t d)")
        hf = hid[:, :, :].rearrange("p t d -> p (t d)")
        stats = SM[:, 0:NT * 6].rearrange("p (t w) -> p t w", t=NT)
        mean, var, std, rstd, nmr, dm = (SM[:, 160 + 32 * k:160 + 32 * k + NT] for k in range(6))
        QUADS = [range(4 * q, min(4 * q + 4, NT)) for q in range(-(-NT // 4))]

        def norm_stats_v(v, do, s_var, s_std, scale=None):
            for t in range(NT):
                ins = v.bn_stats(stats[:, t, :], x[:, t, :])
            do(ins)
            do(v.tensor_tensor(mean, stats[:, :, 1], stats[:, :, 4], ALU.add))
            do(v.tensor_tensor(dm, stats[:, :, 1], stats[:, :, 4], ALU.subtract))
            do(v.tensor_tensor(dm, dm, dm, ALU.mult))
            do(v.tensor_tensor(var, stats[:, :, 2], stats[:, :, 5], ALU.add))
            do(v.tensor_scalar(var, var, 1.0 / D, EPS, ALU.mult, ALU.add))
            do(v.scalar_tensor_tensor(var, dm, 0.25, var, ALU.mult, ALU.add))
            v.nop().then_inc(s_var, 1)
            v.wait_ge(s_std, 1)
            do(v.reciprocal(rstd, std))
            if scale is not None:
                do(v.tensor_tensor(rstd, rstd, scale, ALU.mult))
            do(v.scalar_tensor_tensor(nmr, mean, -0.5, rstd, ALU.mult, ALU.mult))
            v.nop().then_inc(s_var, 1)

        def norm_relu_a(a, t):
            return a.activation(hid[:, t, :], x[:, t, :], ACT.Relu, bias=nmr[:, t:t + 1], scale=rstd[:, t:t + 1])

        def node_stage(tag, prods, norm=True, prep_v=None, prep_pe=None, prep_sp=None, table_sp=None,
                       hidden_v=None):
            s_c, s_var, s_std, s_h, s_ht, s_htc, s_w, s_wd, s_mm, s_st, s_pw, s_pwc = (
                sem(f"{tag}_{n}") for n in ("c", "var", "std", "h", "ht", "htc", "w", "wd", "mm", "st", "pw", "pwc"))
            s_out = {"v": sem(f"{tag}_ov"), "a": sem(f"{tag}_oa")}
            BANKS = (0, 1, 2, 3, 7)
            flat, total, after = [], {"v": 0, "a": 0}, []
            for q in QUADS:
                for t in q:
                    for w, n, e, put in prods[t]:
                        total[e] += 1
                        flat.append((t, w, n, e, put, total[e]))
                after.append((len(flat), dict(total)))
            quad_prods = [range(a, b) for a, b in zip([0] + [x_[0] for x_ in after], [x_[0] for x_ in after])]

            def evacuate(eng, e, q):
                for j in quad_prods[q]:
                    t, w, n, ee, put, _ = flat[j]
                    if ee == e:
                        eng.wait_ge(s_mm, j + 1)
                        put(eng, ps[:, BANKS[j % 5], 0:n]).then_inc(s_out[e], 1)

            with nc.Block() as block:
                @block.sync
                def _(sp):
                    if prep_sp:
                        prep_sp(sp, s_wd)
                    if table_sp:
                        cut = len(QUADS) // 2
                        for q0, q1 in ((0, cut), (cut, len(QUADS))):
                            for e in "va":
                                if after[q1 - 1][1][e]:
                                    sp.wait_ge(s_out[e], after[q1 - 1][1][e])
                            table_sp(sp, s_st, range(QUADS[q0][0], QUADS[q1 - 1][-1] + 1))

                @block.vector
                def _(v):
                    do = Chain(v, s_c)
                    if norm:
                        norm_stats_v(v, do, s_var, s_std)
                    if hidden_v:
                        hidden_v(v, do)
                    if not norm:
                        v.nop().then_inc(s_h, len(QUADS))
                    if prep_v:
                        prep_v(v, do, s_wd, s_pw, s_pwc)
                    v.nop().then_inc(s_w, 1)
                    for q, tiles in enumerate(QUADS):
                        v.wait_ge(s_ht, q + 1)
                        v.tensor_copy(A3[:, 512 * q:512 * q + P * len(tiles)], ps[:, 4 + q % 3, 0:P * len(tiles)]).then_inc(s_htc, 1)
                        if q:
                            evacuate(v, "v", q - 1)
                    evacuate(v, "v", len(QUADS) - 1)

                @block.scalar
                def _(a):
                    if norm:
                        a.wait_ge(s_var, 1)
                        a.activation(std, var, ACT.Sqrt).then_inc(s_std, 1)
                        a.wait_ge(s_var, 2)
                    for q, tiles in enumerate(QUADS):
                        if norm:
                            for t in tiles:
                                ins = norm_relu_a(a, t)
                            ins.then_inc(s_h, 1)
                        if q:
                            evacuate(a, "a", q - 1)
                    evacuate(a, "a", len(QUADS) - 1)

                @block.tensor
                def _(pe):
                    if prep_pe:
                        prep_pe(pe, s_wd, s_pw)
                        pe.wait_ge(s_pwc, 1)

                    def products(q):
                        for j in quad_prods[q]:
                            t, w, n, e, put, _ = flat[j]
                            if j >= 5:
                                pe.wait_ge(s_out[flat[j - 5][3]], flat[j - 5][5])
                            pe.matmul(ps[:, BANKS[j % 5], 0:n], hT[:, t, :], w, start=True, stop=True).then_inc(s_mm, 1)

                    for q, tiles in enumerate(QUADS):
                        pe.wait_ge(s_h, q + 1)
                        if q >= 3:
                            pe.wait_ge(s_htc, q - 2)
                        for k, t in enumerate(tiles):
                            last = pe.transpose(ps[:, 4 + q % 3, k * P:(k + 1) * P], hid[:, t, :], ident[:, :])
                        last.then_inc(s_ht, 1)
                        if q == 0:
                            pe.wait_ge(s_w, 1)
                        if q:
                            pe.wait_ge(s_htc, q)
                            products(q - 1)
                    pe.wait_ge(s_htc, len(QUADS))
                    products(len(QUADS) - 1)

        def copy_to(dst):
            def put(eng, src):
                if eng.engine == mybir.EngineType.Activation:
                    return eng.activation(dst, src, ACT.Copy)
                return eng.tensor_copy(dst, src)
            return put

        def half(base, n, h):
            return slice(base + h * n, base + (h + 1) * n)

        def gather_loop(g, table, rows, idx_src, s_idx, s_rows, s_free):
            with g.Fori(0, NI) as i:
                for h in range(2):
                    for s in s_free:
                        hold(g, s[h], i + 1)
                    g.tensor_copy(idx[:, h, :], idx_src[:, ds(i * (2 * G) + h * G, G)]).then_inc(s_idx, 1)
                    hold(g, s_idx, 2 * i + (h + 1))
                    for k in range(G):
                        g.indirect_dma_start(out=rows(h, k), out_offset=None, in_=table,
                                             in_offset=bass.IndirectOffsetOnAxis(ap=idx[:, h, k:k + 1], axis=0)
                                             ).then_inc(s_rows[h], 16)

        def broadcast_loop(eng, dst, src, s_in, s_free):
            with eng.Fori(0, NI) as i:
                for h in range(2):
                    hold(eng, s_free[h], i + 1)
                    eng.dma_start(dst(h), src[ds(i * (2 * G * P) + h * (G * P), G * P)].partition_broadcast(P)
                                  ).then_inc(s_in[h], 16)

        def onehot_in(rows8):
            return bc(iota_row[:, :].unsqueeze(1), [P, G, P]), bc(rows8.unsqueeze(2), [P, G, P])

        def clear_acc(pe, banks):
            for b in range(banks):
                pe.matmul(ps[:, b, :], zeros[:, 0:P], zeros[:, :], start=True, stop=False, skip_group_check=True)

        def tile_regs(pe, tag):
            return [pe.alloc_register(f"{tag}_tile{k}") for k in range(G)]

        def load_tiles(pe, regs, s0):
            pe.load(regs, tnI[0:1, ds(s0, G)])
            return [pe.snap(r, min_val=0, max_val=(NT - 1) * P) for r in regs]

        def lookup_stage(tag, table, idx_src, width, vcol, rhs, ncol, use):
            s_idx, s_oht, s_g, s_c = (sem(f"{tag}_{n}") for n in ("idx", "oht", "g", "c"))
            s_rows, s_used, s_sp, s_spf, s_dl, s_dlf = ([sem(f"{tag}_{n}{h}") for h in range(2)]
                                                        for n in ("rows", "used", "sp", "spf", "dl", "dlf"))
            rows = A1[:, 0:2 * G * width].rearrange("p (h k w) -> p h k w", h=2, k=G)
            o = 4096
            OHT = A1[:, o:o + 2048].rearrange("p (h k n) -> p h k n", h=2, k=G)
            dlb = A1[:, o + 2048:o + 3072].bitcast(BF16).rearrange("p (h n) -> p h n", h=2)
            prod = A1[:, o + 3072:o + 5120]
            look = [ps[:, 2 * h:2 * h + 2, :].rearrange("p a (k n) -> p (a k) n", n=P)[:, :, 0:ncol] for h in range(2)]
            with nc.Block() as block:
                @block.gpsimd
                def _(g):
                    gather_loop(g, table, lambda h, k: rows[:, h, k, :], idx_src, s_idx, s_rows,
                                [s_used, s_spf])

                @block.scalar
                def _(a):
                    broadcast_loop(a, lambda h: dlb[:, h, :], dl_dram, s_dl, s_dlf)

                @block.sync
                def _(sp):
                    for h in range(2):
                        sp.sem_inc(s_spf[h], 1)
                    with sp.Fori(0, NI) as i:
                        for h in range(2):
                            hold(sp, s_rows[h], i * (16 * G) + 16 * G)
                            sp.dma_start(spill[:, ds(i * (2 * G * P) + h * (G * P), G * P)].rearrange("p (k d) -> p k d", k=G),
                                         rows[:, h, :, vcol:vcol + D]).then_inc(s_sp[h], 16)
                            hold(sp, s_sp[h], 16 * i + 16)
                            sp.sem_inc(s_spf[h], 1)

                @block.vector
                def _(v):
                    for h in range(2):
                        v.sem_inc(s_used[h], 1)
                        v.sem_inc(s_dlf[h], 1)
                    with v.Fori(0, NI) as i:
                        for h in range(2):
                            hold(v, s_dl[h], 16 * i + 16)
                            v.tensor_scalar(OHT[:, h].rearrange("p k n -> p (k n)"), dlb[:, h, :], iota_p[:, 0:1], None,
                                            ALU.is_equal).then_inc(s_oht, 1)
                            hold(v, s_oht, 2 * i + (h + 1))
                            v.sem_inc(s_dlf[h], 1)
                            hold(v, s_g, 2 * i + (h + 1))
                            hold(v, s_rows[h], i * (16 * G) + 16 * G)
                            use(v, i, h, rows, look[h], prod, s_c)
                            v.sem_inc(s_used[h], 1)

                @block.tensor
                def _(pe):
                    regs = tile_regs(pe, tag)
                    with pe.Fori(0, NI) as i:
                        for h in range(2):
                            hold(pe, s_oht, 2 * i + (h + 1))
                            hold(pe, s_used[h], i + 1)
                            tiles = load_tiles(pe, regs, i * (2 * G) + h * G)
                            for k in range(G):
                                last = pe.matmul(look[h][:, k, :], OHT[:, h, k, :], rhs(tiles[k]), start=True, stop=True)
                            last.then_inc(s_g, 1)

        NBUF = 4
        NIB = NS // (NBUF * G)
        assert NIB * NBUF * G == NS

        PARTS = 2.0 ** 11
        EXO, EXW = NT * P, 32

        def sum_stage(tag, wts, table, w, combine, combine_sp=None):
            s_oh, s_ohb, s_ex, s_ec, s_msg, s_c, s_all, s_e = (
                sem(f"{tag}_{n}") for n in ("oh", "ohb", "ex", "ec", "msg", "c", "all", "e"))
            s_v, s_mf = ([sem(f"{tag}_{n}{h}") for h in range(NBUF)] for n in ("v", "mf"))
            val = A1[:, 0:NBUF * 1024].rearrange("p (h n) -> p h n", h=NBUF)
            OH = A1[:, NBUF * 1024:2 * NBUF * 1024].rearrange("p (h k n) -> p h k n", h=NBUF, k=G)
            OHB = A1[:, 2 * NBUF * 1024:5 * NBUF * 512].bitcast(F16).rearrange("p (h k n) -> p h k n", h=NBUF, k=G)
            EX = SM[:, 128:128 + NBUF * G * w].bitcast(F16).rearrange("p (h k w) -> p h k w", h=NBUF, k=G)
            RES = SM[:, 560:560 + G * w].rearrange("p (k w) -> p k w", k=G)
            with nc.Block() as block:
                @block.sync
                def _(sp):
                    with sp.Fori(0, NIB) as i:
                        for h in range(NBUF):
                            hold(sp, s_mf[h], i + 1)
                            sp.dma_start(val[:, h, :], spill[:, ds(i * (NBUF * G * P) + h * (G * P), G * P)]).then_inc(s_v[h], 16)
                    if combine_sp:
                        combine_sp(sp, s_e)

                @block.scalar
                def _(a):
                    with a.Fori(0, NIB) as i:
                        for h in range(NBUF):
                            hold(a, s_ohb, NBUF * i + (h + 1))
                            a.activation(OH[:, h].rearrange("p k n -> p (k n)"), OHB[:, h].rearrange("p k n -> p (k n)"),
                                         ACT.Copy).then_inc(s_oh, 1)

                @block.gpsimd
                def _(g):
                    with g.Fori(0, NIB) as i:
                        for h in range(NBUF):
                            n0 = i * (2 * NBUF) + 2 * h
                            src = table[:, ds(i * (NBUF * G * w) + h * (G * w), G * w)].rearrange("p (k w) -> p k w", k=G)
                            hold(g, s_mf[h], i + 1)
                            g.tensor_copy(EX[:, h, :, 0:w], src).then_inc(s_ec, 1)
                            hold(g, s_ec, n0 + 1)
                            g.tensor_tensor(RES, src, EX[:, h, :, 0:w], ALU.subtract).then_inc(s_ec, 1)
                            hold(g, s_ec, n0 + 2)
                            g.tensor_scalar(EX[:, h, :, w:2 * w], RES, PARTS, None, ALU.mult).then_inc(s_ex, 1)
                            hold(g, s_ex, NBUF * i + (h + 1))

                @block.vector
                def _(v):
                    with v.Fori(0, NIB) as i:
                        for h in range(NBUF):
                            hold(v, s_mf[h], i + 1)
                            v.tensor_tensor(OHB[:, h], bc(iota16[:, :].unsqueeze(1), [P, G, P]),
                                            bc(dl16[:, ds(i * (NBUF * G) + h * G, G)].unsqueeze(2), [P, G, P]),
                                            ALU.is_equal).then_inc(s_ohb, 1)
                            hold(v, s_v[h], 16 * i + 16)
                            wt = wts[:, ds(i * (NBUF * G * H) + h * (G * H), G * H)]
                            vq = val[:, h, :].rearrange("p (q c) -> p q c", c=C)
                            v.tensor_tensor(vq, vq, bc(wt.unsqueeze(2), [P, G * H, C]), ALU.mult).then_inc(s_msg, 1)
                    v.wait_ge(s_all, 1)
                    combine(v, Chain(v, s_c), s_e)

                @block.tensor
                def _(pe):
                    for h in range(NBUF):
                        pe.sem_inc(s_mf[h], 1)
                    clear_acc(pe, 8)
                    regs = tile_regs(pe, tag + "s")
                    with pe.Fori(0, NIB) as i:
                        for h in range(NBUF):
                            tiles = load_tiles(pe, regs, i * (NBUF * G) + h * G)
                            hold(pe, s_oh, NBUF * i + (h + 1))
                            hold(pe, s_msg, NBUF * i + (h + 1))
                            hold(pe, s_ohb, NBUF * i + (h + 1))
                            hold(pe, s_ex, NBUF * i + (h + 1))
                            for k in range(G):
                                pe.matmul(psf[:, ds(tiles[k], P)], OH[:, h, k, :], val[:, h, k * P:(k + 1) * P],
                                          start=False, stop=False, skip_group_check=True)
                                last = pe.matmul(psf[:, ds((tiles[k] >> 2) + EXO, 2 * w)], OHB[:, h, k, :], EX[:, h, k, :],
                                                 start=False, stop=False, skip_group_check=True)
                            last.then_inc(s_mf[h], 1)
                    for h in range(NBUF):
                        pe.wait_ge(s_mf[h], NIB + 1)
                    pe.nop().then_inc(s_all, 1)

        def small_sums(v, dst, w):
            ex = psf[:, EXO:EXO + NT * EXW].rearrange("p (t w) -> p t w", w=EXW)
            v_low = SM[:, 128:128 + NT * w].rearrange("p (t w) -> p t w", w=w)
            return [lambda: v.tensor_scalar(v_low, ex[:, :, w:2 * w], 1.0 / PARTS, None, ALU.mult),
                    lambda: v.tensor_tensor(dst, v_low, ex[:, :, 0:w], ALU.add)]

        XN = NREL * H
        XC = XN + 1
        XP = 16

        def row4(ap):
            return ap.rearrange("p (b h e) -> p b h e", b=NB, h=H)

        CC = SM[0:H, 0:NS + 1]
        CI = SM[0:RB, 424:440]
        T2 = SM[0:RB, 448:960].rearrange("p (b e) -> p b e", b=NB)
        PC = A3[0:H, 5696:5696 + NS]

        def scan_v(v, do, to_pe, from_pe, Xin, Y, T, kind, back):
            is_max = kind == "max"
            same, carry, chain = (same_b, carry_b, chain_b) if back else (same_f, carry_f, chain_f)
            samef = same[:, :, :, :].rearrange("p b h e -> p (b h e)")
            st = -1 if back else 1
            ini = -BIG if is_max else 0.0
            if is_max:
                do(v.tensor_scalar(T, samef, -1.0, BIG, ALU.add, ALU.mult))
                do(v.tensor_scalar(PC, chain[:, :], -1.0, BIG, ALU.add, ALU.mult))
                do(v.tensor_tensor_scan(Y[:, ::st], T[:, ::st], Xin[:, ::st], ini, ALU.add, ALU.max))
            else:
                do(v.tensor_tensor_scan(Y[:, ::st], samef[:, ::st], Xin[:, ::st], ini, ALU.mult,
                                        ALU.max if back else ALU.add))
            to_pe.give(v.nop())
            o = 0 if back else 1
            do(v.memset(CC[:, NS:NS + 1] if back else CC[:, 0:1], ini))
            from_pe.take(v)
            d0 = PC if is_max else chain[:, :]
            do(v.tensor_tensor_scan(CC[:, o:o + NS][:, ::st], d0[:, ::st], ps[0:H, 0, 0:NS][:, ::st], ini,
                                    ALU.add if is_max else ALU.mult, ALU.max if is_max or back else ALU.add))
            to_pe.give(v.nop())
            if is_max:
                do(v.tensor_scalar(T2, carry[:, :, :], -1.0, BIG, ALU.add, ALU.mult))
            from_pe.take(v)
            do(v.tensor_copy(CI, ps[0:RB, 1, 0:NB * H]))
            cm = T2 if is_max else carry[:, :, :]
            for b in range(NB):
                for h in range(H):
                    ins = v.scalar_tensor_tensor(row4(Y)[:, b, h, :], cm[:, b, :], CI[:, b * H + h:b * H + h + 1],
                                                 row4(Y)[:, b, h, :], ALU.add if is_max else ALU.mult,
                                                 ALU.max if is_max or back else ALU.add)
            do(ins)

        def scan_pe(pe, from_v, to_v, Y, back):
            from_v.take(pe)
            e = 0 if back else P - 1
            for b in range(NB):
                last = pe.transpose(ps[0:H, 0, b * RB:(b + 1) * RB], row4(Y)[:, b, :, e], ident[0:RB, 0:RB])
            to_v.give(last)
            from_v.take(pe)
            o = 1 if back else 0
            for b in range(NB):
                last = pe.transpose(ps[0:RB, 1, b * H:(b + 1) * H], CC[:, o + b * RB:o + (b + 1) * RB], ident[0:H, 0:H])
            to_v.give(last)

        def total_v(v, do, to_pe, from_pe, Xin, Y, M, T, kind):
            scan_v(v, do, to_pe, from_pe, Xin, Y, T, kind, False)
            scan_v(v, do, to_pe, from_pe, Y, M, T, kind, True)

        def total_pe(pe, from_v, to_v, Y, M):
            scan_pe(pe, from_v, to_v, Y, False)
            scan_pe(pe, from_v, to_v, M, True)

        def to_rows_pe(pe, src, bank):
            for b in range(NB):
                for h in range(H):
                    last = pe.transpose(ps[0:RB, bank + b, h * P:(h + 1) * P], src[:, b * RB:(b + 1) * RB, h], ident[:, :])
            return last

        def to_edges_pe(pe, X, bank):
            for h in range(H):
                for b in range(NB):
                    last = pe.transpose(ps[:, bank + h, b * RB:(b + 1) * RB], row4(X)[:, b, h, :], ident[0:RB, 0:RB])
            return last

        NC0 = NREL * WN0
        HN = A1[:, 0:NT * NC0].rearrange("p (t r w) -> p t r w", t=NT, r=NREL)
        HNf = A1[:, 0:NT * NC0].rearrange("p (t w) -> p t w", t=NT)
        W0c = A2[:, 0:NC0].rearrange("p (r w) -> p r w", r=NREL)
        ATT = A2[:, 512:512 + 2 * NREL * P].rearrange("p (a r w) -> p a r w", a=2, r=NREL)
        WAT = A2[:, 1536:1536 + NREL * P].rearrange("p (r w) -> p r w", r=NREL)
        wrel = sb("wrel", [P, NREL])
        rl = SM[:, 384:384 + NREL]
        rmax, rsum = SM[:, 390:391], SM[:, 391:392]
        NDA = sb("NDA", [P, NT * 32])
        nda = NDA[:, :].rearrange("p (t w) -> p t w", t=NT)

        def l0_prep_sp(sp, s_wd):
            sp.dma_start(W0c[:, :, 0:D], W_in.rearrange("r i o -> i r o")).then_inc(s_wd, 16)
            sp.dma_start(ATT[:, 0].rearrange("p r w -> p (r w)"),
                         as_in.rearrange("r h c -> (r h c)").partition_broadcast(P)).then_inc(s_wd, 16)
            sp.dma_start(ATT[:, 1].rearrange("p r w -> p (r w)"),
                         ad_in.rearrange("r h c -> (r h c)").partition_broadcast(P)).then_inc(s_wd, 16)
            sp.dma_start(rl, relw_in.partition_broadcast(P)).then_inc(s_wd, 16)

        def l0_prep_v(v, do, s_wd, s_pw, s_pwc):
            v.wait_ge(s_wd, 64)
            for a in range(2):
                do(v.tensor_tensor(WAT, W0c[:, :, 0:D], ATT[:, a], ALU.mult))
                for r in range(NREL):
                    ins = v.tensor_reduce(W0c[:, r, D + a * H:D + (a + 1) * H],
                                          WAT[:, r].rearrange("p (h c) -> p h c", h=H), AX, ALU.add)
                do(ins)
            do(v.tensor_reduce(rmax, rl, AX, ALU.max))
            do(v.tensor_scalar(wrel[:, :], rl, rmax, None, ALU.subtract))

        def l0_after_v(v, do):
            a_s = HN[:, :, :, D:D + H]
            a_d = HN[:, :, :, D + H:D + 2 * H]
            od = nda[:, :, 0:NREL * H]
            os_ = nda[:, :, NREL * H:2 * NREL * H]
            for r in range(NREL):
                v.tensor_copy(od[:, :, r * H:(r + 1) * H], a_d[:, :, r, :])
                ins = v.tensor_tensor(os_[:, :, r * H:(r + 1) * H], a_s[:, :, r, :], a_d[:, :, r, :], ALU.add)
            do(ins)
            do(v.scalar_tensor_tensor(os_, os_, 0.2, os_, ALU.mult, ALU.max))

        def store_rows(sp, s_st, table, src, tiles, width):
            a, b = tiles[0], tiles[-1] + 1
            sp.dma_start(table[a * P:b * P, :].rearrange("(t p) w -> p t w", p=P), src[:, a:b, 0:width]).then_inc(s_st, 16)

        def l0_table_sp(sp, s_st, tiles):
            for r in range(NREL):
                store_rows(sp, s_st, tab0[r * NP:(r + 1) * NP, :], HN[:, :, r, :], tiles, WA0)
            if tiles[-1] == NT - 1:
                sp.wait_ge(s_st, 32 * NREL)

        AS = A3[:, 0:NS * H].rearrange("p (s h) -> p s h", h=H)
        LIM = A3[:, 0:NS * NREL].rearrange("p (s r) -> p s r", r=NREL)
        SC8 = SM[:, 0:G * NREL * H].rearrange("p (k r h) -> p k r h", k=G, r=NREL)
        ADS = A2[:, 0:NS * 24].rearrange("p (s w) -> p s w", w=24)
        ADSf = A2[:, 0:NS * 24]
        CS = A2[:, NS * 24:NS * 24 + NS * XC].rearrange("p (s w) -> p s w", w=XC)
        CSf = A2[:, NS * 24:NS * 24 + NS * XC]
        WT = A3[:, 3328:4992]
        WTv = WT.rearrange("p (s h) -> p s h", h=H)
        R_ = [A1[0:RB, 2048 * k:2048 * (k + 1)] for k in range(5)]
        ACC = hf[0:RB, 0:2048]
        ADS_N = 24

        def l0_use(v, i, h, rows, look, prod, s_c):
            s0, n0 = i * (2 * G) + h * G, i * 6 + 3 * h
            out = ADS[:, ds(s0, G), :]
            v.tensor_copy(out[:, :, NREL * H:], look[:, :, NREL * H:])
            v.tensor_tensor(SC8, look[:, :, 0:NREL * H].rearrange("p k (r h) -> p k r h", r=NREL),
                            bc(rows[:, h, :, D:D + H].unsqueeze(2), [P, G, NREL, H]), ALU.add).then_inc(s_c, 1)
            hold(v, s_c, n0 + 1)
            v.scalar_tensor_tensor(SC8, SC8, 0.2, SC8, ALU.mult, ALU.max).then_inc(s_c, 1)
            hold(v, s_c, n0 + 2)
            v.tensor_tensor(out[:, :, 0:NREL * H].rearrange("p k (r h) -> p k r h", r=NREL), SC8,
                            bc(LIM[:, ds(s0, G), :].unsqueeze(3), [P, G, NREL, H]), ALU.min).then_inc(s_c, 1)
            hold(v, s_c, n0 + 3)

        def l0_softmax():
            s_c, s_x1, s_x2, s_e1 = sem("l0s_c"), sem("l0s_x1"), sem("l0s_x2"), sem("l0s_e1")
            s_vp, s_pv, s_w, s_zd = sem("l0s_vp"), sem("l0s_pv"), sem("l0s_w"), sem("l0s_zd")
            s_in, s_cp = sem("l0s_in"), sem("l0s_cp")
            S, Y, M, T = R_[1:5]
            XS = (R_[0], A3[0:RB, 0:2048], R_[0])
            fills = ["X0"] + [f"{n}{q}" for r in range(NREL) for n, q in (("S", r), ("X", r + 1), ("O", r)) if (n, q) != ("X", NREL)]
            nth = {name: k + 1 for k, name in enumerate(fills)}
            with nc.Block() as block:
                @block.sync
                def _(sp):
                    for k in range(G):
                        sp.dma_start(scat[k][0:NP, :].rearrange("(p a) d -> p a d", p=P),
                                     bc(zeros[:, 0:D].unsqueeze(1), [P, NT, D])).then_inc(s_zd, 16)
                    sp.wait_ge(s_zd, 16 * G)

                @block.scalar
                def _(a):
                    a.wait_ge(s_w, 1)
                    a.activation(wrel[:, :], wrel[:, :], ACT.Exp, accum_out=rsum).then_inc(s_w, 1)

                    def rows_in(name, dst):
                        a.wait_ge(s_in, nth[name])
                        a.activation(dst, psf[0:RB, 2048:4096], ACT.Copy).then_inc(s_cp, 1)

                    rows_in("X0", XS[0])
                    for r in range(NREL):
                        rows_in(f"S{r}", S)
                        a.wait_ge(s_x1, r + 1)
                        a.activation(XS[r], XS[r], ACT.Exp).then_inc(s_e1, 1)
                        a.activation(S, S, ACT.Exp).then_inc(s_e1, 1)
                        if r + 1 < NREL:
                            rows_in(f"X{r + 1}", XS[r + 1])
                        a.wait_ge(s_in, nth[f"O{r}"])
                        for h in range(H):
                            ins = a.activation(CS[:, :, r * H + h], ps[:, 4 + h, 0:NS], ACT.Copy)
                        ins.then_inc(s_cp, 1)

                @block.tensor
                def _(pe):
                    vp, pv = Hand(s_vp), Hand(s_pv)

                    def rows_out(name, col):
                        if nth[name] > 1:
                            pe.wait_ge(s_cp, nth[name] - 1)
                        to_rows_pe(pe, ADS[:, :, col:col + H], 4).then_inc(s_in, 1)

                    rows_out("X0", 0)
                    for r in range(NREL):
                        rows_out(f"S{r}", NREL * H + r * H)
                        total_pe(pe, vp, pv, Y, M)
                        if r + 1 < NREL:
                            rows_out(f"X{r + 1}", (r + 1) * H)
                        total_pe(pe, vp, pv, Y, M)
                        vp.take(pe)
                        pe.wait_ge(s_cp, nth[f"O{r}"] - 1)
                        to_edges_pe(pe, S, 4).then_inc(s_in, 1)
                    vp.take(pe)
                    pe.wait_ge(s_cp, len(fills))
                    to_edges_pe(pe, ACC, 0)
                    for b in range(NB):
                        last = pe.transpose(ps[:, 4, b * RB:(b + 1) * RB], is_last[:, b, :], ident[0:RB, 0:RB])
                    pv.give(last)

                @block.vector
                def _(v):
                    do = Chain(v, s_c)
                    vp, pv = Hand(s_vp), Hand(s_pv)
                    v.nop().then_inc(s_w, 1)
                    v.wait_ge(s_w, 2)
                    do(v.reciprocal(rmax, rsum))
                    do(v.tensor_scalar(wrel[:, :], wrel[:, :], rmax, None, ALU.mult))
                    for r in range(NREL):
                        X = XS[r]
                        v.wait_ge(s_cp, nth[f"X{r}"])
                        total_v(v, do, vp, pv, X, Y, M, T, "max")
                        v.wait_ge(s_cp, nth[f"S{r}"])
                        do(v.tensor_tensor(M, M, S, ALU.max))
                        do(v.tensor_tensor(X, X, M, ALU.subtract))
                        do(v.tensor_tensor(S, S, M, ALU.subtract))
                        v.nop().then_inc(s_x1, 1)
                        v.wait_ge(s_e1, 2 * (r + 1))
                        total_v(v, do, vp, pv, X, Y, M, T, "sum")
                        do(v.tensor_tensor(M, M, S, ALU.add))
                        do(v.reciprocal(M, M))
                        do(v.tensor_scalar(M, M, wrel[0:RB, r:r + 1], None, ALU.mult))
                        do(v.tensor_tensor(S, S, M, ALU.mult))
                        do(v.tensor_tensor(row4(S), row4(S), bc(is_last[:, :, :].unsqueeze(2), [RB, NB, H, P]), ALU.mult))
                        vp.give(v.nop())
                        if r:
                            do(v.tensor_tensor(X, X, M, ALU.mult))
                            do(v.tensor_tensor(ACC, ACC, X, ALU.add))
                        else:
                            do(v.tensor_tensor(ACC, X, M, ALU.mult))
                    vp.give(v.nop())
                    pv.take(v)
                    for h in range(H):
                        ins = v.tensor_copy(WTv[:, :, h], ps[:, h, 0:NS])
                    do(ins)
                    do(v.tensor_copy(CS[:, :, XN], ps[:, 4, 0:NS]))

        CO = A3[:, 0:NT * XP].rearrange("p (t w) -> p t w", w=XP)
        HB = [A2[:, 3200 * k:3200 * (k + 1)].rearrange("p (t d) -> p t d", t=NT) for k in range(4)]
        BIA = A3[:, 512:512 + NREL * D].rearrange("p (r d) -> p r d", r=NREL)
        CF = A3[:, 1024:1024 + NT * H].rearrange("p (t h) -> p t h", h=H)
        ABS = A3[:, 1152:1152 + NT]

        def l0_combine_sp(sp, s_e):
            sp.wait_ge(s_e, 1)
            for r in range(NREL):
                sp.dma_start(HB[r], tab0[r * NP:(r + 1) * NP, 0:D].rearrange("(t p) w -> p t w", p=P)).then_inc(s_e, 16)
            sp.dma_start(BIA.rearrange("p r d -> p (r d)"), bias_in.rearrange("r d -> (r d)").partition_broadcast(P)).then_inc(s_e, 16)
            sp.wait_ge(s_e, 65)

        def l0_combine(v, do, s_e):
            v.nop().then_inc(s_e, 1)
            do(v.tensor_tensor(xf, xf, psf[:, 0:NT * P], ALU.add))
            for step in small_sums(v, CO[:, :, 0:XC], XC):
                do(step())
            do(v.tensor_scalar(ABS, CO[:, :, XN], -1.0, 1.0, ALU.mult, ALU.add))
            v.wait_ge(s_e, 65)
            for r in range(NREL):
                do(v.tensor_scalar(CF, bc(ABS.unsqueeze(2), [P, NT, H]), wrel[:, r:r + 1], None, ALU.mult))
                do(v.tensor_tensor(CF, CF, CO[:, :, r * H:(r + 1) * H], ALU.add))
                t4 = HB[3].rearrange("p t (h c) -> p t h c", h=H)
                do(v.tensor_tensor(t4, HB[r].rearrange("p t (h c) -> p t h c", h=H),
                                   bc(CF.unsqueeze(3), [P, NT, H, C]), ALU.mult))
                do(v.tensor_tensor(x[:, :, :], x[:, :, :], HB[3], ALU.add))
                b0, br = BIA[:, 0, :], BIA[:, r, :]
                do(v.scalar_tensor_tensor(b0, br, wrel[:, r:r + 1], b0, ALU.mult, ALU.add) if r
                   else v.tensor_scalar(b0, b0, wrel[:, 0:1], None, ALU.mult))
            do(v.tensor_tensor(x[:, :, :], x[:, :, :], bc(BIA[:, 0:1, :], [P, NT, D]), ALU.add))

        node_stage("n0", [[(W0c.rearrange("p r w -> p (r w)"), NC0, "va"[t % 2], copy_to(HNf[:, t, :]))] for t in range(NT)],
                   prep_v=l0_prep_v, prep_sp=l0_prep_sp, table_sp=l0_table_sp)
        s_n0 = sem("n0_self")
        with nc.Block() as block:
            @block.vector
            def _(v):
                do = Chain(v, s_n0)
                l0_after_v(v, do)
                for r in range(NREL):
                    ins = v.tensor_scalar(LIM[:, :, r], t3T[:, :], float(r), None, ALU.is_equal)
                do(ins)
                do(v.tensor_scalar(A3[:, 0:NS * NREL], A3[:, 0:NS * NREL], 1e30, -NEG, ALU.mult, ALU.add))
        lookup_stage("k0", tab0, i0, WA0, 0, lambda r: NDA[:, ds(r >> 2, ADS_N)], ADS_N, l0_use)
        l0_softmax()
        sum_stage("m0", WT, CSf, XC, l0_combine, combine_sp=l0_combine_sp)

        def finish():
            s_fin = sem("s_fin")
            with nc.Block() as block:
                @block.sync
                def _(sp):
                    sp.dma_start(out[0:FULL * P, :].rearrange("(t p) d -> p t d", p=P), x[:, 0:FULL, :]).then_inc(s_fin, 16)
                    sp.dma_start(out[FULL * P:N, :], x[0:REST, FULL, :]).then_inc(s_fin, 16)
                    sp.wait_ge(s_fin, 32)

        end_layer()

        Bo = A1[:, 6400:6912].rearrange("p (k d) -> p k d", k=NBASE)
        BT = A1[:, 6912:7424].rearrange("p (k d) -> p k d", k=NBASE)
        W0o = A1[:, 7424:7552]
        WT1 = A1[:, 7552:7552 + (NRAT + 1) * D]
        Abc = A1[:, 8320:8320 + NRAT * NBASE]
        T1 = A2[:, 0:NT * NRAT * D].rearrange("p (t w) -> p t w", t=NT)
        dinv = sb("dinv", [P, NT])

        def l1_prep_sp(sp, s_wd):
            sp.dma_start(Bo, B_in.rearrange("k o i -> o k i")).then_inc(s_wd, 16)
            sp.dma_start(W0o, W0_in).then_inc(s_wd, 16)
            sp.dma_start(Abc, A_in.rearrange("r k -> (r k)").partition_broadcast(P)).then_inc(s_wd, 16)

        def l1_prep_pe(pe, s_wd, s_pw):
            pe.wait_ge(s_wd, 48)
            for k in range(NBASE):
                pe.transpose(ps[:, 7, k * P:(k + 1) * P], Bo[:, k, :], ident[:, :])
            pe.transpose(ps[:, 6, 0:P], W0o, ident[:, :]).then_inc(s_pw, 1)

        def l1_prep_v(v, do, s_wd, s_pw, s_pwc):
            v.wait_ge(s_wd, 48)
            v.wait_ge(s_pw, 1)
            do(v.tensor_copy(BT.rearrange("p k d -> p (k d)"), ps[:, 7, :]))
            do(v.tensor_copy(WT1[:, NRAT * D:], ps[:, 6, 0:P]))
            v.nop().then_inc(s_pwc, 1)
            for k in range(NBASE):
                for r in range(NRAT):
                    w, a = WT1[:, r * D:(r + 1) * D], Abc[:, r * NBASE + k:r * NBASE + k + 1]
                    ins = (v.scalar_tensor_tensor(w, BT[:, k, :], a, w, ALU.mult, ALU.add) if k
                           else v.tensor_scalar(w, BT[:, k, :], a, None, ALU.mult))
                do(ins)

        def l1_table_sp(sp, s_st, tiles):
            for r in range(NRAT):
                store_rows(sp, s_st, tab1[r * NP:(r + 1) * NP, :], T1[:, :, r * D:(r + 1) * D], tiles, D)
            if tiles[-1] == NT - 1:
                sp.wait_ge(s_st, 32 * NRAT)

        def add_to_x(t):
            return lambda eng, src: eng.tensor_tensor(x[:, t, :], x[:, t, :], src, ALU.add)

        node_stage("n1", [[(WT1[:, 0:512], 512, "a", copy_to(T1[:, t, 0:512])),
                           (WT1[:, 512:640], 128, "v", copy_to(T1[:, t, 512:640])),
                           (WT1[:, 640:768], 128, "v", add_to_x(t))] for t in range(NT)],
                   prep_v=l1_prep_v, prep_pe=l1_prep_pe, prep_sp=l1_prep_sp, table_sp=l1_table_sp)

        def l1_edges():
            s_idx, s_oh, s_c, s_all, s_v, s_sq = (sem(f"e1_{n}") for n in ("idx", "oh", "c", "all", "v", "sq"))
            s_rows, s_mf = ([sem(f"e1_{n}{h}") for h in range(2)] for n in ("rows", "mf"))
            rows = A1[:, 0:2048].rearrange("p (h k w) -> p h k w", h=2, k=G)
            OH = A1[:, 2048:4096].rearrange("p (h k n) -> p h k n", h=2, k=G)
            LO_ = A1[:, 4096:5120].bitcast(BF16).rearrange("p (h k n) -> p h k n", h=2, k=G)
            HI_ = A1[:, 5120:5120 + G * NT].bitcast(BF16).rearrange("p (h k n) -> p h k n", h=2, k=G)
            deg = SM[:, 0:NT]
            with nc.Block() as block:
                @block.gpsimd
                def _(g):
                    gather_loop(g, tab1, lambda h, k: rows[:, h, k, :], i1, s_idx, s_rows, [s_mf])

                @block.scalar
                def _(a):
                    a.wait_ge(s_v, 1)
                    a.activation(deg, deg, ACT.Sqrt).then_inc(s_sq, 1)

                @block.vector
                def _(v):
                    do = Chain(v, s_c)
                    with v.Fori(0, NI) as i:
                        for h in range(2):
                            s0 = i * (2 * G) + h * G
                            hold(v, s_mf[h], i + 1)
                            a, b = onehot_in(dlT[:, ds(s0, G)])
                            v.tensor_tensor(OH[:, h], a, b, ALU.is_equal)
                            a, b = onehot_in(loT[:, ds(s0, G)])
                            v.tensor_tensor(LO_[:, h], a, b, ALU.is_equal)
                            v.tensor_tensor(HI_[:, h], bc(iota_row[:, 0:NT].unsqueeze(1), [P, G, NT]),
                                            bc(hiT[:, ds(s0, G)].unsqueeze(2), [P, G, NT]), ALU.is_equal).then_inc(s_oh, 1)
                    v.wait_ge(s_all, 1)
                    do(v.tensor_tensor(xf, xf, psf[:, 0:NT * P], ALU.add))
                    do(v.tensor_copy(deg, ps[:, 7, 0:NT]))
                    do(v.scalar_tensor_tensor(deg[:, FULL:NT], iota_p[:, :], float(REST), deg[:, FULL:NT], ALU.is_ge, ALU.add))
                    v.nop().then_inc(s_v, 1)
                    v.wait_ge(s_sq, 1)
                    do(v.reciprocal(dinv[:, :], deg))

                @block.tensor
                def _(pe):
                    for h in range(2):
                        pe.sem_inc(s_mf[h], 1)
                    clear_acc(pe, 8)
                    regs = tile_regs(pe, "e1")
                    with pe.Fori(0, NI) as i:
                        for h in range(2):
                            hold(pe, s_oh, 2 * i + (h + 1))
                            hold(pe, s_rows[h], i * (16 * G) + 16 * G)
                            tiles = load_tiles(pe, regs, i * (2 * G) + h * G)
                            for k in range(G):
                                pe.matmul(psf[:, ds(tiles[k], P)], OH[:, h, k, :], rows[:, h, k, :],
                                          start=False, stop=False, skip_group_check=True)
                                last = pe.matmul(ps[:, 7, 0:NT], LO_[:, h, k, :], HI_[:, h, k, :],
                                                 start=False, stop=False, skip_group_check=True)
                            last.then_inc(s_mf[h], 1)
                    for h in range(2):
                        pe.wait_ge(s_mf[h], NI + 1)
                    pe.nop().then_inc(s_all, 1)

        l1_edges()
        end_layer()

        def l2_edges():
            s_c, s_var, s_std, s_lo = sem("e2_c"), sem("e2_var"), sem("e2_std"), sem("e2_lo")
            s_oht, s_seq, s_g, s_val, s_sum, s_gs, s_ix, s_prev, s_cc = (
                sem(f"e2_{n}") for n in ("oht", "seq", "g", "val", "sum", "gs", "ix", "prev", "cc"))
            s_dl, s_dlf, s_sr = ([sem(f"e2_{n}{h}") for h in range(2)] for n in ("dl", "dlf", "sr"))
            s_t = [sem(f"e2_t{k}") for k in range(G)]
            s_in, s_hid = sem("e2_in"), sem("e2_hid")
            OHT = A1[:, 0:2048].rearrange("p (h k n) -> p h k n", h=2, k=G)
            dlb = A1[:, 2048:3072].bitcast(BF16).rearrange("p (h n) -> p h n", h=2)
            srcb = A1[:, 3072:5120].rearrange("p (h n) -> p h n", h=2)
            SEQ = A1[:, 5120:7168].rearrange("p (h k n) -> p h k n", h=2, k=G)
            val = A1[:, 7168:9216].rearrange("p (h k n) -> p h k n", h=2, k=G)
            gs = A3[:, 0:2048].rearrange("p (h k n) -> p h k n", h=2, k=G)
            tmp = A3[:, 2048:3072].rearrange("p (k n) -> p k n", k=G)
            LOW = A3[:, 3072:3200]
            spare = SM[:, 512:513]
            cnt8, first8, d8 = SM[:, 520:528], SM[:, 528:536], SM[:, 536:544]
            SIX = SMI[:, 0:2 * G].rearrange("p (h k) -> p h k", h=2)
            look = [ps[:, 2 * h:2 * h + 2, :].rearrange("p a n -> p (a n)") for h in range(2)]
            tot = [ps[:, 4 + 2 * h:6 + 2 * h, :].rearrange("p a n -> p (a n)") for h in range(2)]
            with nc.Block() as block:
                @block.vector
                def _(v):
                    do = Chain(v, s_c)
                    norm_stats_v(v, do, s_var, s_std, scale=dinv[:, :])
                    do(v.tensor_scalar(LOW, iota_row[:, :], iota_p[:, 0:1], None, ALU.is_lt))
                    do(v.tensor_scalar(spare, iota_p[:, 0:1], float(NP), None, ALU.add))

                @block.scalar
                def _(a):
                    a.wait_ge(s_var, 1)
                    a.activation(std, var, ACT.Sqrt).then_inc(s_std, 1)
                    a.wait_ge(s_var, 2)
                    for t in range(NT):
                        norm_relu_a(a, t)

            with nc.Block() as block:
                @block.sync
                def _(sp):
                    with sp.Fori(0, NI) as i:
                        for h in range(2):
                            hold(sp, s_dlf[h], i + 1)
                            c0 = i * (2 * G * P) + h * (G * P)
                            sp.dma_start(dlb[:, h, :], dl_dram[ds(c0, G * P)].partition_broadcast(P)).then_inc(s_dl[h], 16)
                            sp.dma_start(srcb[:, h, :], srcrow_dram[ds(c0, G * P)].partition_broadcast(P)).then_inc(s_sr[h], 16)

                @block.vector
                def _(v):
                    for h in range(2):
                        v.sem_inc(s_dlf[h], 1)
                    with v.Fori(0, NI) as i:
                        for h in range(2):
                            s0 = i * (2 * G) + h * G
                            hold(v, s_dl[h], 16 * i + 16)
                            hold(v, s_g, 2 * i + (h + 1))
                            v.tensor_scalar(OHT[:, h].rearrange("p k n -> p (k n)"), dlb[:, h, :], iota_p[:, 0:1], None,
                                            ALU.is_equal).then_inc(s_oht, 1)
                            hold(v, s_sr[h], 16 * i + 16)
                            hold(v, s_sum, 2 * i + (h + 1))
                            v.tensor_tensor(SEQ[:, h], srcb[:, h, :].rearrange("p (k n) -> p k n", k=G),
                                            bc(srcT[:, ds(s0, G)].unsqueeze(2), [P, G, P]), ALU.is_equal).then_inc(s_seq, 1)
                            hold(v, s_seq, 2 * i + (h + 1))
                            hold(v, s_oht, 2 * i + (h + 1))
                            v.sem_inc(s_dlf[h], 1)
                            n0 = i * 8 + 4 * h

                            def step(ins, k):
                                ins.then_inc(s_cc, 1)
                                hold(v, s_cc, i * 10 + (5 * h + k))
                            step(v.tensor_tensor(tmp, SEQ[:, h], bc(LOW.unsqueeze(1), [P, G, P]), ALU.mult), 1)
                            step(v.tensor_reduce(cnt8, tmp, AX, ALU.add), 2)
                            step(v.tensor_scalar(d8, srcT[:, ds(s0, G)], spare, None, ALU.subtract), 3)
                            step(v.scalar_tensor_tensor(first8, cnt8, 0.0, d8, ALU.is_equal, ALU.mult), 4)
                            step(v.tensor_scalar(first8, first8, spare, None, ALU.add), 5)
                            hold(v, s_prev, 2 * i + (h + 1))
                            v.tensor_copy(SIX[:, h, :], first8).then_inc(s_ix, 1)
                            hold(v, s_ix, 2 * i + (h + 1))

                @block.tensor
                def _(pe):
                    pe.sem_inc(s_g, 2)
                    pe.sem_inc(s_sum, 2)
                    regs = tile_regs(pe, "e2")
                    with pe.Fori(0, NI) as i:
                        for h in range(2):
                            hold(pe, s_oht, 2 * i + (h + 1))
                            hold(pe, s_val, 2 * i + (h + 1))
                            tiles = load_tiles(pe, regs, i * (2 * G) + h * G)
                            for k in range(G):
                                last = pe.matmul(look[h][:, k * P:(k + 1) * P], OHT[:, h, k, :], hf[:, ds(tiles[k], P)],
                                                 start=True, stop=True)
                            last.then_inc(s_g, 1)
                            hold(pe, s_seq, 2 * i + (h + 1))
                            hold(pe, s_val, 2 * i + (h + 3))
                            hold(pe, s_gs, 2 * i + (h + 1))
                            for k in range(G):
                                last = pe.matmul(tot[h][:, k * P:(k + 1) * P], SEQ[:, h, k, :], val[:, h, k, :],
                                                 start=True, stop=True)
                            last.then_inc(s_sum, 1)

                @block.scalar
                def _(a):
                    a.sem_inc(s_val, 2)
                    a.sem_inc(s_gs, 2)
                    with a.Fori(0, NI) as i:
                        for h in range(2):
                            hold(a, s_g, 2 * i + (h + 3))
                            hold(a, s_sum, 2 * i + (h + 1))
                            a.activation(val[:, h].rearrange("p k n -> p (k n)"), look[h], ACT.Copy).then_inc(s_val, 1)
                            hold(a, s_sum, 2 * i + (h + 3))
                            hold(a, s_prev, 2 * i + (h + 1))
                            a.activation(gs[:, h].rearrange("p k n -> p (k n)"), tot[h], ACT.Copy).then_inc(s_gs, 1)

                @block.gpsimd
                def _(g):
                    g.sem_inc(s_prev, 1)
                    for k in range(G):
                        g.dma_start(scat[k][NP:NDUMP, :], zeros[:, 0:D]).then_inc(s_t[k], 16)
                    with g.Fori(0, NI) as i:
                        for h in range(2):
                            hold(g, s_gs, 2 * i + (h + 3))
                            hold(g, s_ix, 2 * i + (h + 1))
                            for k in range(G):
                                hold(g, s_t[k], i * 32 + (16 * h + 16))
                                g.indirect_dma_start(out=scat[k], out_offset=bass.IndirectOffsetOnAxis(ap=SIX[:, h, k:k + 1], axis=0),
                                                     in_=gs[:, h, k, :], in_offset=None,
                                                     compute_op=ALU.add).then_inc(s_t[k], 16)
                            g.sem_inc(s_prev, 1)
                    for k in range(G):
                        g.wait_ge(s_t[k], 16 + 32 * NI)

            TB = [A2[:, 3200 * k:3200 * (k + 1)] for k in range(5)] + [A1[:, 3200 * k:3200 * (k + 1)] for k in range(3)]
            with nc.Block() as block:
                @block.sync
                def _(sp):
                    for k in range(G):
                        sp.dma_start(TB[k].rearrange("p (t d) -> p t d", t=NT),
                                     scat[k][0:NP, :].rearrange("(t p) d -> p t d", p=P)).then_inc(s_t2[k], 16)
                    for k in range(G):
                        sp.wait_ge(s_t2[k], 16)

                @block.vector
                def _(v):
                    do = Chain(v, s_in)
                    v.wait_ge(s_t2[0], 16)
                    for k in range(1, G):
                        v.wait_ge(s_t2[k], 16)
                        do(v.tensor_tensor(TB[0], TB[0], TB[k], ALU.add))
                    do(v.tensor_tensor(hid[:, :, :], TB[0].rearrange("p (t d) -> p t d", t=NT),
                                       bc(dinv[:, :].unsqueeze(2), [P, NT, D]), ALU.mult))

        s_t2 = [sem(f"e2_l{k}") for k in range(G)]
        l2_edges()
        W2o, W2T = A1[:, 0:P], A1[:, P:2 * P]

        def l2_prep_sp(sp, s_wd):
            sp.dma_start(W2o, W2_in).then_inc(s_wd, 16)

        def l2_prep_pe(pe, s_wd, s_pw):
            pe.wait_ge(s_wd, 16)
            pe.transpose(ps[:, 7, 0:P], W2o, ident[:, :]).then_inc(s_pw, 1)

        def l2_prep_v(v, do, s_wd, s_pw, s_pwc):
            v.wait_ge(s_pw, 1)
            do(v.tensor_copy(W2T, ps[:, 7, 0:P]))
            v.nop().then_inc(s_pwc, 1)

        def add_relu(t):
            return lambda eng, src: eng.scalar_tensor_tensor(x[:, t, :], src, 0.0, x[:, t, :], ALU.max, ALU.add)

        node_stage("n2", [[(W2T, D, "v", add_relu(t))] for t in range(NT)], norm=False,
                   prep_v=l2_prep_v, prep_pe=l2_prep_pe, prep_sp=l2_prep_sp)
        end_layer()

        KV = A2[:, 0:NT * 4 * D].rearrange("p (t w) -> p t w", t=NT)
        WALL = A2[:, 12800:13312]
        BALL = A2[:, 13312:13824]
        ALf = A3[:, 0:NS * H]

        def l3_layer(l):
            Wq, Wk, Wv, Ws, bq, bk, bv, bs = l3[8 * l:8 * l + 8]
            tag = f"t{l}"

            def prep_sp(sp, s_wd):
                for k, (w, b) in enumerate(((Wk, bk), (Wv, bv), (Wq, bq), (Ws, bs))):
                    sp.dma_start(WALL[:, k * D:(k + 1) * D], w).then_inc(s_wd, 16)
                    sp.dma_start(BALL[:, k * D:(k + 1) * D], b.partition_broadcast(P)).then_inc(s_wd, 16)

            def prep_v(v, do, s_wd, s_pw, s_pwc):
                v.wait_ge(s_wd, 128)

            def put(t):
                return lambda eng, src: eng.tensor_tensor(KV[:, t, :], src, BALL, ALU.add)

            def table_sp(sp, s_st, tiles):
                store_rows(sp, s_st, tab3, KV, tiles, 2 * D)
                if tiles[-1] == NT - 1:
                    sp.wait_ge(s_st, 32)

            node_stage(tag + "n", [[(WALL, 4 * D, "v", put(t))] for t in range(NT)], norm=(l == 0),
                       prep_v=prep_v, prep_sp=prep_sp, table_sp=table_sp)

            def use(v, i, h, rows, look, prod, s_c):
                pk = prod[:, h * 1024:(h + 1) * 1024]
                v.tensor_tensor(pk.rearrange("p (k d) -> p k d", k=G), rows[:, h, :, 0:D], look, ALU.mult).then_inc(s_c, 1)
                hold(v, s_c, 4 * i + (2 * h + 1))
                v.tensor_reduce(ALf[:, ds(i * (2 * G * H) + h * (G * H), G * H)],
                                pk.rearrange("p (q c) -> p q c", c=C), AX, ALU.add).then_inc(s_c, 1)
                hold(v, s_c, 4 * i + (2 * h + 2))

            lookup_stage(tag + "k", tab3, i3, 2 * D, D, lambda r: A2[:, ds(r * 4 + 2 * D, D)], D, use)

            s_c, s_x1, s_e1, s_vp, s_pv = (sem(f"{tag}s_{n}") for n in ("c", "x1", "e1", "vp", "pv"))
            X, Y, M, T = R_[0:4]
            with nc.Block() as block:
                @block.scalar
                def _(a):
                    a.wait_ge(s_x1, 1)
                    a.activation(X, X, ACT.Exp, scale=float(C) ** -0.5).then_inc(s_e1, 1)

                @block.tensor
                def _(pe):
                    vp, pv = Hand(s_vp), Hand(s_pv)
                    pv.give(to_rows_pe(pe, AS, 0))
                    total_pe(pe, vp, pv, Y, M)
                    vp.take(pe)
                    pv.give(to_edges_pe(pe, X, 2))

                @block.vector
                def _(v):
                    do = Chain(v, s_c)
                    vp, pv = Hand(s_vp), Hand(s_pv)
                    pv.take(v)
                    do(v.tensor_copy(X, psf[0:RB, 0:2048]))
                    total_v(v, do, vp, pv, X, Y, M, T, "max")
                    do(v.tensor_tensor(X, X, M, ALU.subtract))
                    v.nop().then_inc(s_x1, 1)
                    v.wait_ge(s_e1, 1)
                    vp.give(v.nop())
                    pv.take(v)
                    for h in range(H):
                        ins = v.tensor_copy(WTv[:, :, h], ps[:, 2 + h, 0:NS])
                    do(ins)

            DEN = SM[:, 0:NT * H]

            def combine(v, do, s_e):
                for step in small_sums(v, DEN.rearrange("p (t h) -> p t h", h=H), H):
                    do(step())
                do(v.tensor_scalar(DEN, DEN, 1e-16, None, ALU.max))
                do(v.reciprocal(DEN, DEN))
                do(v.tensor_tensor(hf.rearrange("p (q c) -> p q c", c=C),
                                   psf[:, 0:NT * P].rearrange("p (q c) -> p q c", c=C),
                                   bc(DEN.unsqueeze(2), [P, NT * H, C]), ALU.mult))
                do(v.tensor_tensor(hid[:, :, :], hid[:, :, :], KV[:, :, 3 * D:4 * D], ALU.add))
                do(v.tensor_scalar(hid[:, :, :], hid[:, :, :], 0.0, None, ALU.max))
                if l == 1:
                    do(v.tensor_tensor(xf, xf, hf, ALU.add))

            sum_stage(tag + "m", WT, WT, H, combine)

        l3_layer(0)
        end_layer()
        l3_layer(1)
        finish()


_L3 = [f"L3_gnn_{k}{l}" for l in range(2) for k in ("Wq", "Wk", "Wv", "Ws", "bq", "bk", "bv", "bs")]
_INS = ["x", "src", "dst", "edge_type_3", "edge_type_5", "L0_gnn_W", "L0_gnn_att_src", "L0_gnn_att_dst",
        "L0_gnn_bias", "L0_gnn_rel_w", "L1_gnn_B", "L1_gnn_A", "L1_gnn_W0", "L2_gnn_weight"] + _L3


def kernel(**inputs):
    import numpy as _np
    import concourse.bacc as _bacc
    from concourse import mybir as _mybir
    from concourse.bass_utils import run_bass_kernel_spmd as _run

    nc = _bacc.Bacc("TRN2", target_bir_lowering=False, num_devices=1)
    arrays, args = {}, {}
    for name in _INS:
        a = _np.ascontiguousarray(inputs[name])
        arrays[f"in_{name}_dram"] = a
        args[name] = nc.dram_tensor(f"in_{name}_dram", a.shape, _mybir.dt.from_np(a.dtype), kind="ExternalInput").ap()
    out = nc.dram_tensor("out_0_dram", (N, D), F32, kind="ExternalOutput").ap()
    A = [args[n] for n in _INS]
    build(nc, A[0], A[1], A[2], A[3], A[4], A[5], A[6], A[7], A[8], A[9], A[10], A[11], A[12], A[13], A[14:], out)
    r = _run(nc, [arrays], core_ids=[0])
    return r.results[0]["out_0_dram"]
```

```python
from contextlib import ExitStack

import concourse.bass as bass
from concourse import mybir

F32 = mybir.dt.float32
BF16 = mybir.dt.bfloat16
F16 = mybir.dt.float16
I32 = mybir.dt.int32
ALU = mybir.AluOpType
ACT = mybir.ActivationFunctionType
AX = mybir.AxisListType.X
ds = bass.ds

P = 128
N, D = 3125, 128
E = 50000
H, C = 4, 32
NREL, NRAT, NBASE = 3, 5, 4
NT = -(-N // P)
NP = NT * P
FULL = N // P
REST = N - FULL * P
ET = -(-E // P)
EREST = E - (ET - 1) * P
RB = 104
NB = 4
NS = RB * NB
assert NS >= ET + NT - 1
G = 8
NI = NS // (2 * G)
assert NI * 2 * G == NS
WA0 = D + H
WN0 = D + 2 * H
BIG = 1e37
NEG = 1e9
EPS = 1e-5
NDUMP = NP + P


class Chain:

    def __init__(self, eng, sem):
        self.eng, self.sem, self.n = eng, sem, 0

    def __call__(self, ins):
        self.n += 1
        ins.then_inc(self.sem, 1)
        self.eng.wait_ge(self.sem, self.n)


class Hand:

    def __init__(self, sem):
        self.sem, self.given, self.taken = sem, 0, 0

    def give(self, ins, by=1):
        self.given += by
        ins.then_inc(self.sem, by)

    def take(self, eng, by=1):
        self.taken += by
        eng.wait_ge(self.sem, self.taken)


def bc(ap, shape):
    return ap.to_broadcast(shape)


def build(nc, x_in, src_in, dst_in, t3_in, t5_in, W_in, as_in, ad_in, bias_in, relw_in,
          B_in, A_in, W0_in, W2_in, l3, out):
    ctx = ExitStack()
    with ctx:
        def sb(name, shape, dt=F32):
            return ctx.enter_context(nc.sbuf_tensor(name, shape, dt))

        layer_sems = []

        def sem(name):
            s = nc.alloc_semaphore(name=name)
            layer_sems.append(s)
            return s

        def end_layer():
            nc.clear_and_free_semaphores(layer_sems)
            layer_sems.clear()
            nc.all_engine_barrier()

        def dram(name, shape, dt=F32):
            return nc.dram_tensor(name, shape, dt, kind="Internal").ap()

        edge_tab = dram("edge_tab", [ET, 4 * P], I32)
        dl_dram = dram("dl_dram", [NS * P], BF16)
        srcrow_dram = dram("srcrow_dram", [NS * P])
        tab0 = dram("tab0", [NREL * NP, WA0])
        tab1 = dram("tab1", [NRAT * NP, D])
        tab3 = dram("tab3", [NP, 2 * D])
        spill = dram("spill", [P, NS * D])
        scat = [dram(f"scat{k}", [NDUMP, D]) for k in range(G)]

        iota_row = sb("iota_row", [P, P])
        iota16 = sb("iota16", [P, P], F16)
        iota_p = sb("iota_p", [P, 1])
        ident = sb("ident", [P, P])
        ones = sb("ones", [P, P])
        zeros = sb("zeros", [P, 512])
        dlT = sb("dlT", [P, NS])
        dl16 = sb("dl16", [P, NS], F16)
        srcT = sb("srcT", [P, NS])
        loT = sb("loT", [P, NS])
        hiT = sb("hiT", [P, NS])
        i0 = sb("i0", [P, NS + 2 * G], I32)
        i1 = sb("i1", [P, NS + 2 * G], I32)
        i3 = sb("i3", [P, NS + 2 * G], I32)
        tnI = sb("tnI", [1, NS], I32)
        same_f = sb("same_f", [RB, NB, H, P], BF16)
        same_b = sb("same_b", [RB, NB, H, P], BF16)
        carry_f = sb("carry_f", [RB, NB, 1])
        carry_b = sb("carry_b", [RB, NB, 1])
        is_last = sb("is_last", [RB, NB, P])
        chain_f = sb("chain_f", [H, NS])
        chain_b = sb("chain_b", [H, NS])
        pen_f = sb("pen_f", [RB, NB, H, P], BF16)
        pen_b = sb("pen_b", [RB, NB, H, P], BF16)
        pcar_f = sb("pcar_f", [RB, NB, 1])
        pcar_b = sb("pcar_b", [RB, NB, 1])
        pch_f = sb("pch_f", [H, NS])
        pch_b = sb("pch_b", [H, NS])
        x = sb("x", [P, NT, D])
        hid = sb("hid", [P, NT, D])
        idx = sb("idx", [P, 2, G], I32)
        A1 = sb("A1", [P, 10240])
        A2 = sb("A2", [P, 16000])
        A3 = sb("A3", [P, 4992])
        SM = sb("SM", [P, 1024])
        SMI = sb("SMI", [P, 256], I32)

        ps = ctx.enter_context(nc.psum_tensor("ps", [P, 8, 512], F32))
        psf = ps[:, :, :].rearrange("p a b -> p (a b)")

        passed = ctx.enter_context(nc.semaphore("passed"))

        def hold(eng, s, value):
            eng.wait_ge(s, value)
            eng.sem_inc(passed, 1)

        cnt_cmp = A2[:, 0:9600].rearrange("p (j e) -> p j e", j=24)
        dst_i = A1[:, 0:400].bitcast(I32)
        dst_f = A1[:, 400:800]
        R = A1[:, 1024:1024 + NB * 512].bitcast(I32).rearrange("p (b q e) -> p b q e", b=NB, q=4)
        Rf = A1[:, 4096:4096 + NB * 512].rearrange("p (b q e) -> p b q e", b=NB, q=4)
        DL = A3[:, 0:512].rearrange("p (b e) -> p b e", b=NB)
        VAL = A3[:, 512:1024].rearrange("p (b e) -> p b e", b=NB)
        I0f = A3[:, 1024:1536].rearrange("p (b e) -> p b e", b=NB)
        I1f = A3[:, 1536:2048].rearrange("p (b e) -> p b e", b=NB)
        TMP = A3[:, 2048:2560].rearrange("p (b e) -> p b e", b=NB)
        Kr = A3[0:RB, 3968:4480].rearrange("p (b e) -> p b e", b=NB)
        t3T = A2[:, 4096:4096 + NS]
        DLB = A3[:, 2560:2816].bitcast(BF16).rearrange("p (b e) -> p b e", b=NB)
        KK = A3[:, 2816:2848].rearrange("p (a b h) -> p a b h", a=2, b=NB)
        TJ = A3[:, 2848:2948].rearrange("p (b j) -> p b j", b=NB)
        KL = A3[:, 3072:3072 + NS + 1]
        KF = A3[:, 3520:3520 + NS + 1]
        cnt = SM[:, 0:26]
        Fv = SM[:, 32:58]
        af = SM[:, 64:90]
        lf = SM[:, 96:122]
        nn = SM[:, 128:153]
        Oc = SM[:, 160:185]
        dl_ = SM[:, 192:217]
        sval = SM[:, 224:228]
        tn = SM[:, 232:236]
        tnc = SM[:, 240:244]
        te = SM[:, 248:252]
        tn128 = SM[:, 256:260]
        PL = SM[:, 288:320].rearrange("p (a b h) -> p a b h", a=2, b=NB)
        pad_i = SMI[:, 0:96]
        Fi = SMI[:, 96:122]
        Li = SMI[:, 128:154]
        te_i = SMI[:, 160:164]
        LO = A2[:, 0:NS].bitcast(I32)
        HI = A2[:, 512:512 + NS].bitcast(I32)
        HIf = A2[:, 1024:1024 + NS]
        VT = A2[:, 1536:1536 + NS]

        s_pad, s_tab, s_dst, s_c = sem("s_pad"), sem("s_tab"), sem("s_dst"), sem("s_c")
        s_io, s_io2, s_id, s_cnt, s_F, s_te, s_R = (sem("s_io"), sem("s_io2"), sem("s_id"), sem("s_cnt"),
                                                    sem("s_F"), sem("s_te"), sem("s_R"))
        s_row, s_tr, s_kk, s_kt, s_sh, s_sht, s_dd, s_x = (sem("s_row"), sem("s_tr"), sem("s_kk"), sem("s_kt"),
                                                           sem("s_sh"), sem("s_sht"), sem("s_dd"), sem("s_x"))
        QUANT = [DL, Rf[:, :, 1, :], I0f, I1f, Rf[:, :, 2, :]]

        with nc.Block() as block:
            @block.sync
            def _(sp):
                sp.dma_start(dst_i[0:125, :], dst_in.rearrange("(p e) -> p e", p=125)).then_inc(s_dst, 16)
                for q, arr in enumerate((dst_in, src_in, t3_in, t5_in)):
                    sp.dma_start(edge_tab[0:ET - 1, q * P:(q + 1) * P],
                                 arr[0:(ET - 1) * P].rearrange("(t e) -> t e", e=P)).then_inc(s_tab, 16)
                    sp.dma_start(edge_tab[ET - 1:ET, q * P:q * P + EREST],
                                 arr[(ET - 1) * P:E].rearrange("(a e) -> a e", a=1)).then_inc(s_tab, 16)
                sp.wait_ge(s_pad, 2)
                for q in range(4):
                    sp.dma_start(edge_tab[ET - 1:ET, q * P + EREST:(q + 1) * P],
                                 pad_i[0:1, (48 if q else 0):(48 if q else 0) + P - EREST]).then_inc(s_tab, 16)
                sp.dma_start(x[:, 0:FULL, :], x_in[0:FULL * P, :].rearrange("(t p) d -> p t d", p=P)).then_inc(s_x, 16)
                sp.wait_ge(s_pad, 3)
                sp.dma_start(x[0:REST, FULL, :], x_in[FULL * P:N, :]).then_inc(s_x, 16)
                sp.wait_ge(s_row, 1)
                sp.dma_start(dl_dram.rearrange("(b p e) -> p b e", b=NB, e=P), DLB[0:RB]).then_inc(s_dd, 16)
                sp.dma_start(srcrow_dram.rearrange("(b p e) -> p b e", b=NB, e=P), Rf[0:RB, :, 1, :]).then_inc(s_dd, 16)
                sp.wait_ge(s_dd, 32)
                sp.wait_ge(s_x, 32)

            @block.gpsimd
            def _(g):
                g.memset(ident[:, :], 0.0).then_inc(s_io, 1)
                g.iota(iota_row[:, :], [[1, P]], base=0, channel_multiplier=0,
                       allow_small_or_imprecise_dtypes=True).then_inc(s_io, 1)
                g.iota(iota_p[:, :], [[0, 1]], base=0, channel_multiplier=1,
                       allow_small_or_imprecise_dtypes=True).then_inc(s_io, 1)
                g.iota(sval, [[RB, NB]], base=0, channel_multiplier=1,
                       allow_small_or_imprecise_dtypes=True).then_inc(s_io, 1)
                g.wait_ge(s_io, 1)
                g.affine_select(out=ident[:, :], in_=ident[:, :], compare_op=ALU.not_equal, fill=1.0,
                                base=0, pattern=[[-1, P]], channel_multiplier=1).then_inc(s_id, 1)
                g.wait_ge(s_tab, 16 * 12)
                g.wait_ge(s_te, 1)
                for b in range(NB):
                    g.indirect_dma_start(out=R[0:RB, b].rearrange("p q e -> p (q e)"), out_offset=None, in_=edge_tab[:, :],
                                         in_offset=bass.IndirectOffsetOnAxis(ap=te_i[0:RB, b:b + 1], axis=0)
                                         ).then_inc(s_R, 16)

            @block.tensor
            def _(pe):
                pe.wait_ge(s_cnt, 1)
                pe.matmul(ps[:, 7, 0:26], ones[0:125, :], cnt[0:125, :], start=True, stop=True).then_inc(s_F, 1)
                pe.wait_ge(s_id, 1)
                pe.wait_ge(s_row, 1)
                for q, Q in enumerate(QUANT):
                    for b in range(NB):
                        pe.transpose(ps[:, q, b * RB:(b + 1) * RB], Q[0:RB, b, :], ident[0:RB, 0:RB])
                for b in range(NB):
                    last = pe.transpose(ps[0:1, 5, b * RB:(b + 1) * RB], tnc[0:RB, b:b + 1], ident[0:RB, 0:RB])
                last.then_inc(s_tr, 1)
                pe.wait_ge(s_kk, 1)
                for a in range(2):
                    for b in range(NB):
                        last = pe.transpose(ps[0:H, 6 + a, b * RB:(b + 1) * RB], KK[0:RB, a, b, :], ident[0:RB, 0:RB])
                last.then_inc(s_kt, 1)
                pe.wait_ge(s_sh, 1)
                for b in range(NB):
                    pe.transpose(ps[0:RB, 0, b * H:(b + 1) * H], KL[0:H, b * RB:(b + 1) * RB], ident[0:H, 0:H])
                for b in range(NB):
                    last = pe.transpose(ps[0:RB, 0, 16 + b * H:16 + (b + 1) * H],
                                        KF[0:H, 1 + b * RB:1 + (b + 1) * RB], ident[0:H, 0:H])
                last.then_inc(s_sht, 1)

            @block.vector
            def _(v):
                do = Chain(v, s_c)
                do(v.memset(ones[:, :], 1.0))
                do(v.memset(zeros[:, :], 0.0))
                v.memset(pad_i[:, 0:48], 8192).then_inc(s_pad, 1)
                v.memset(pad_i[:, 48:96], 0).then_inc(s_pad, 1)
                for t in (i0, i1, i3):
                    v.memset(t[:, NS:NS + 2 * G], 0)
                v.memset(x[:, FULL, :], 0.0).then_inc(s_pad, 1)
                do(v.memset(cnt, 0.0))
                do(v.memset(cnt[:, 25:26], E / 125))
                v.wait_ge(s_dst, 16)
                do(v.tensor_copy(dst_f[0:125, :], dst_i[0:125, :]))
                for j in range(1, NT):
                    ins = v.tensor_scalar(cnt_cmp[0:125, j - 1, :], dst_f[0:125, :], float(P * j), None, ALU.is_lt)
                do(ins)
                do(v.tensor_reduce(cnt[0:125, 1:NT], cnt_cmp[0:125], AX, ALU.add))
                v.nop().then_inc(s_cnt, 1)
                v.wait_ge(s_F, 1)
                do(v.tensor_copy(Fv, ps[:, 7, 0:26]))
                do(v.tensor_copy(Fi, Fv))
                do(v.tensor_scalar(Fi, Fi, 7, None, ALU.arith_shift_right))
                do(v.tensor_copy(af, Fi))
                do(v.tensor_scalar(lf, Fv, -1.0, None, ALU.add))
                do(v.tensor_copy(Li, lf))
                do(v.tensor_scalar(Li, Li, 7, None, ALU.arith_shift_right))
                do(v.tensor_copy(lf, Li))
                do(v.tensor_tensor(nn, lf[:, 1:26], af[:, 0:25], ALU.subtract))
                do(v.tensor_scalar(nn, nn, 1.0, None, ALU.add))
                do(v.tensor_tensor(dl_, Fv[:, 1:26], Fv[:, 0:25], ALU.is_gt))
                do(v.tensor_tensor(nn, nn, dl_, ALU.mult))
                do(v.tensor_tensor_scan(Oc, ones[:, 0:25], nn, 0.0, ALU.mult, ALU.add))
                do(v.tensor_tensor(dl_, nn, Oc, ALU.subtract))
                do(v.tensor_tensor(dl_, dl_, af[:, 0:25], ALU.add))
                v.wait_ge(s_io, 4)
                do(v.tensor_tensor(TJ, bc(Oc.unsqueeze(1), [P, NB, NT]), bc(sval.unsqueeze(2), [P, NB, NT]), ALU.is_le))
                do(v.tensor_reduce(tn, TJ, AX, ALU.add))
                do(v.tensor_tensor(TJ, bc(iota_row[:, 0:NT].unsqueeze(1), [P, NB, NT]),
                                   bc(tn.unsqueeze(2), [P, NB, NT]), ALU.is_equal))
                do(v.tensor_tensor(TJ, TJ, bc(dl_.unsqueeze(1), [P, NB, NT]), ALU.mult))
                do(v.tensor_reduce(te, TJ, AX, ALU.add))
                do(v.tensor_tensor(te, te, sval, ALU.add))
                do(v.tensor_scalar(te, te, float(ET - 1), 0.0, ALU.min, ALU.max))
                do(v.tensor_copy(te_i, te))
                v.nop().then_inc(s_te, 1)
                do(v.tensor_scalar(tnc, tn, float(NT - 1), None, ALU.min))
                do(v.tensor_scalar(tn128, tn, float(P), None, ALU.mult))
                v.wait_ge(s_R, 16 * NB)
                do(v.tensor_copy(A1[0:RB, 4096:4096 + NB * 512], A1[0:RB, 1024:1024 + NB * 512].bitcast(I32)))
                dstf, srcf, t3f, t5f = (Rf[0:RB, :, q, :] for q in range(4))
                do(v.tensor_tensor(DL[0:RB], dstf, bc(tn128[0:RB].unsqueeze(2), [RB, NB, P]), ALU.subtract))
                do(v.tensor_scalar(VAL[0:RB], DL[0:RB], 0.0, None, ALU.is_ge))
                do(v.tensor_scalar(TMP[0:RB], DL[0:RB], float(P), None, ALU.is_lt))
                do(v.tensor_tensor(VAL[0:RB], VAL[0:RB], TMP[0:RB], ALU.mult))
                do(v.tensor_scalar(Kr[:, :, :], dstf, 1.0, None, ALU.add))
                do(v.tensor_tensor(Kr[:, :, :], Kr[:, :, :], VAL[0:RB], ALU.mult))
                do(v.tensor_scalar(Kr[:, :, :], Kr[:, :, :], -1.0, None, ALU.add))
                do(v.scalar_tensor_tensor(I0f[0:RB], t3f, float(NP), srcf, ALU.mult, ALU.add))
                do(v.scalar_tensor_tensor(I1f[0:RB], t5f, float(NP), srcf, ALU.mult, ALU.add))
                do(v.tensor_copy(DLB[0:RB], DL[0:RB]))
                v.nop().then_inc(s_row, 1)
                do(v.tensor_copy(KK[0:RB, 0], bc(Kr[:, :, P - 1:P], [RB, NB, H])))
                do(v.tensor_copy(KK[0:RB, 1], bc(Kr[:, :, 0:1], [RB, NB, H])))
                v.nop().then_inc(s_kk, 1)
                v.wait_ge(s_tr, 1)
                do(v.tensor_copy(dlT[:, :], ps[:, 0, 0:NS]))
                do(v.tensor_copy(dl16[:, :], ps[:, 0, 0:NS]))
                v.wait_ge(s_io, 2)
                do(v.tensor_copy(iota16[:, :], iota_row[:, :]))
                do(v.tensor_copy(srcT[:, :], ps[:, 1, 0:NS]))
                do(v.tensor_copy(i3[:, 0:NS], ps[:, 1, 0:NS]))
                do(v.tensor_copy(i0[:, 0:NS], ps[:, 2, 0:NS]))
                do(v.tensor_copy(i1[:, 0:NS], ps[:, 3, 0:NS]))
                do(v.tensor_copy(t3T[:, :], ps[:, 4, 0:NS]))
                do(v.tensor_scalar(tnI[:, :], ps[0:1, 5, 0:NS], float(P), None, ALU.mult))
                do(v.tensor_scalar(LO, i3[:, 0:NS], P - 1, None, ALU.bitwise_and))
                do(v.tensor_copy(loT[:, :], LO))
                do(v.tensor_scalar(HI, i3[:, 0:NS], 7, None, ALU.arith_shift_right))
                do(v.tensor_copy(HIf, HI))
                do(v.tensor_scalar(VT, dlT[:, :], 0.0, None, ALU.is_ge))
                do(v.scalar_tensor_tensor(VT, dlT[:, :], float(P), VT, ALU.is_lt, ALU.mult))
                do(v.scalar_tensor_tensor(HIf, HIf, 1.0, VT, ALU.add, ALU.mult))
                do(v.tensor_scalar(hiT[:, :], HIf, -1.0, None, ALU.add))
                v.wait_ge(s_kt, 1)
                do(v.memset(KL[0:H, 0:1], -5.0))
                do(v.memset(KF[0:H, NS:NS + 1], -6.0))
                do(v.tensor_copy(KL[0:H, 1:NS + 1], ps[0:H, 6, 0:NS]))
                do(v.tensor_copy(KF[0:H, 0:NS], ps[0:H, 7, 0:NS]))
                v.nop().then_inc(s_sh, 1)
                do(v.tensor_tensor(chain_f[:, :], KL[0:H, 1:NS + 1], KL[0:H, 0:NS], ALU.is_equal))
                do(v.tensor_tensor(chain_b[:, :], KF[0:H, 1:NS + 1], KF[0:H, 0:NS], ALU.is_equal))
                v.wait_ge(s_sht, 1)
                do(v.tensor_copy(PL[0:RB].rearrange("p a b h -> p (a b h)"), ps[0:RB, 0, 0:32]))
                do(v.tensor_tensor(carry_f[:, :, :], Kr[:, :, 0:1], PL[0:RB, 0, :, 0:1], ALU.is_equal))
                do(v.tensor_tensor(carry_b[:, :, :], Kr[:, :, P - 1:P], PL[0:RB, 1, :, 0:1], ALU.is_equal))
                do(v.tensor_tensor(is_last[:, :, 0:P - 1], Kr[:, :, 1:P], Kr[:, :, 0:P - 1], ALU.not_equal))
                do(v.tensor_scalar(is_last[:, :, P - 1:P], carry_b[:, :, :], -1.0, 1.0, ALU.mult, ALU.add))
                do(v.tensor_tensor(is_last[:, :, :], is_last[:, :, :], VAL[0:RB], ALU.mult))

        def scan_masks(v, do, part):
            if part == 0:
                v.memset(same_f[:, :, :, 0:1], 0.0)
                v.memset(same_b[:, :, :, P - 1:P], 0.0)
            if part < H:
                h = part
                v.tensor_tensor(same_f[:, :, h, 1:P], Kr[:, :, 1:P], Kr[:, :, 0:P - 1], ALU.is_equal)
                do(v.tensor_tensor(same_b[:, :, h, 0:P - 1], Kr[:, :, 1:P], Kr[:, :, 0:P - 1], ALU.is_equal))
            if part == H:
                for pen, mask in ((pen_f, same_f), (pen_b, same_b)):
                    ins = v.tensor_scalar(pen[:, :, :, :], mask[:, :, :, :], -1.0, BIG, ALU.add, ALU.mult)
                do(ins)
            if part == H + 1:
                for pen, mask in ((pcar_f, carry_f), (pcar_b, carry_b)):
                    v.tensor_scalar(pen[:, :, :], mask[:, :, :], -1.0, BIG, ALU.add, ALU.mult)
                for pen, mask in ((pch_f, chain_f), (pch_b, chain_b)):
                    ins = v.tensor_scalar(pen[:, :], mask[:, :], -1.0, BIG, ALU.add, ALU.mult)
                do(ins)
        hT = A3[:, 0:NT * P].rearrange("p (t n) -> p t n", t=NT)
        xf = x[:, :, :].rearrange("p t d -> p (t d)")
        hf = hid[:, :, :].rearrange("p t d -> p (t d)")
        stats = SM[:, 0:NT * 6].rearrange("p (t w) -> p t w", t=NT)
        mean, var, std, rstd, nmr, dm = (SM[:, 160 + 32 * k:160 + 32 * k + NT] for k in range(6))
        RUNS = ((0, 3), (3, 5), (5, 7))
        QUADS = [range(4 * q, min(4 * q + 4, NT)) for q in range(-(-NT // 4))]

        def norm_stats_v(v, do, s_var, s_std, scale=None):
            for t in range(NT):
                ins = v.bn_stats(stats[:, t, :], x[:, t, :])
            do(ins)
            do(v.tensor_tensor(mean, stats[:, :, 1], stats[:, :, 4], ALU.add))
            do(v.tensor_tensor(dm, stats[:, :, 1], stats[:, :, 4], ALU.subtract))
            do(v.tensor_tensor(dm, dm, dm, ALU.mult))
            do(v.tensor_tensor(var, stats[:, :, 2], stats[:, :, 5], ALU.add))
            do(v.tensor_scalar(var, var, 1.0 / D, EPS, ALU.mult, ALU.add))
            do(v.scalar_tensor_tensor(var, dm, 0.25, var, ALU.mult, ALU.add))
            v.nop().then_inc(s_var, 1)
            v.wait_ge(s_std, 1)
            do(v.reciprocal(rstd, std))
            if scale is not None:
                do(v.tensor_tensor(rstd, rstd, scale, ALU.mult))
            do(v.scalar_tensor_tensor(nmr, mean, -0.5, rstd, ALU.mult, ALU.mult))
            v.nop().then_inc(s_var, 1)

        def norm_relu_a(a, t):
            return a.activation(hid[:, t, :], x[:, t, :], ACT.Relu, bias=nmr[:, t:t + 1], scale=rstd[:, t:t + 1])

        def node_stage(tag, prods, norm=True, prep_v=None, prep_pe=None, prep_sp=None, table_sp=None,
                       between_v=None, after_v=None):
            s_c, s_var, s_std, s_h, s_ht, s_htc, s_w, s_wd, s_mm, s_st, s_pw, s_pwc = (
                sem(f"{tag}_{n}") for n in ("c", "var", "std", "h", "ht", "htc", "w", "wd", "mm", "st", "pw", "pwc"))
            s_out = {"v": sem(f"{tag}_ov"), "a": sem(f"{tag}_oa")}
            BANKS = (0, 1, 2, 3, 7)
            flat, total, after = [], {"v": 0, "a": 0}, []
            for q in QUADS:
                for t in q:
                    for w, n, e, put in prods[t]:
                        total[e] += 1
                        flat.append((t, w, n, e, put, total[e]))
                after.append((len(flat), dict(total)))
            quad_prods = [range(a, b) for a, b in zip([0] + [x_[0] for x_ in after], [x_[0] for x_ in after])]

            def evacuate(eng, e, q):
                for j in quad_prods[q]:
                    t, w, n, ee, put, _ = flat[j]
                    if ee == e:
                        eng.wait_ge(s_mm, j + 1)
                        put(eng, ps[:, BANKS[j % 5], 0:n]).then_inc(s_out[e], 1)

            with nc.Block() as block:
                @block.sync
                def _(sp):
                    if prep_sp:
                        prep_sp(sp, s_wd)
                    if table_sp:
                        for q0, q1 in RUNS:
                            for e in "va":
                                if after[q1 - 1][1][e]:
                                    sp.wait_ge(s_out[e], after[q1 - 1][1][e])
                            table_sp(sp, s_st, range(QUADS[q0][0], QUADS[q1 - 1][-1] + 1))

                @block.vector
                def _(v):
                    do = Chain(v, s_c)
                    if norm:
                        norm_stats_v(v, do, s_var, s_std)
                    if not norm:
                        v.nop().then_inc(s_h, len(QUADS))
                    if prep_v:
                        prep_v(v, do, s_wd, s_pw, s_pwc)
                    v.nop().then_inc(s_w, 1)
                    for q, tiles in enumerate(QUADS):
                        v.wait_ge(s_ht, q + 1)
                        v.tensor_copy(A3[:, 512 * q:512 * q + P * len(tiles)], ps[:, 4 + q % 3, 0:P * len(tiles)]).then_inc(s_htc, 1)
                        if q:
                            evacuate(v, "v", q - 1)
                            if between_v:
                                between_v(v, do, q - 1)
                    evacuate(v, "v", len(QUADS) - 1)
                    if after_v:
                        for e in "va":
                            v.wait_ge(s_out[e], total[e])
                        after_v(v, do)

                @block.scalar
                def _(a):
                    if norm:
                        a.wait_ge(s_var, 1)
                        a.activation(std, var, ACT.Sqrt).then_inc(s_std, 1)
                        a.wait_ge(s_var, 2)
                    for q in range(len(QUADS) + 2):
                        if norm and q < len(QUADS):
                            for t in QUADS[q]:
                                ins = norm_relu_a(a, t)
                            ins.then_inc(s_h, 1)
                        if q >= 2:
                            evacuate(a, "a", q - 2)

                @block.tensor
                def _(pe):
                    if prep_pe:
                        prep_pe(pe, s_wd, s_pw)
                        pe.wait_ge(s_pwc, 1)

                    def products(q):
                        for j in quad_prods[q]:
                            t, w, n, e, put, _ = flat[j]
                            if j >= 5:
                                pe.wait_ge(s_out[flat[j - 5][3]], flat[j - 5][5])
                            pe.matmul(ps[:, BANKS[j % 5], 0:n], hT[:, t, :], w, start=True, stop=True).then_inc(s_mm, 1)

                    for q, tiles in enumerate(QUADS):
                        pe.wait_ge(s_h, q + 1)
                        if q >= 3:
                            pe.wait_ge(s_htc, q - 2)
                        for k, t in enumerate(tiles):
                            last = pe.transpose(ps[:, 4 + q % 3, k * P:(k + 1) * P], hid[:, t, :], ident[:, :])
                        last.then_inc(s_ht, 1)
                        if q == 0:
                            pe.wait_ge(s_w, 1)
                        if q:
                            pe.wait_ge(s_htc, q)
                            products(q - 1)
                    pe.wait_ge(s_htc, len(QUADS))
                    products(len(QUADS) - 1)

        def copy_to(dst):
            def put(eng, src):
                if eng.engine == mybir.EngineType.Activation:
                    return eng.activation(dst, src, ACT.Copy)
                return eng.tensor_copy(dst, src)
            return put

        def gather_loop(g, table, rows, s_rows, ready):
            with g.Fori(0, NI) as i:
                for h in range(2):
                    ready(i, h)
                    for k in range(G):
                        g.indirect_dma_start(out=rows(h, k), out_offset=None, in_=table,
                                             in_offset=bass.IndirectOffsetOnAxis(ap=idx[:, h, k:k + 1], axis=0)
                                             ).then_inc(s_rows[h], 16)

        def broadcast_loop(eng, dst, src, s_in, s_free):
            with eng.Fori(0, NI) as i:
                for h in range(2):
                    hold(eng, s_free[h], i + 1)
                    eng.dma_start(dst(h), src[ds(i * (2 * G * P) + h * (G * P), G * P)].partition_broadcast(P)
                                  ).then_inc(s_in[h], 16)

        def onehot_in(rows8):
            return bc(iota_row[:, :].unsqueeze(1), [P, G, P]), bc(rows8.unsqueeze(2), [P, G, P])

        def clear_acc(pe, banks):
            for b in range(banks):
                pe.matmul(ps[:, b, :], zeros[:, 0:P], zeros[:, :], start=True, stop=False, skip_group_check=True)

        NBUF = 4
        tile_regs = [nc.tensor.alloc_register(f"tile{k}") for k in range(NBUF * G)]

        def load_tiles(pe, s0, n):
            pe.load(tile_regs[0:n], tnI[0:1, ds(s0, n)])
            return [pe.snap(r, min_val=0, max_val=(NT - 1) * P) for r in tile_regs[0:n]]

        def lookup_stage(tag, table, idx_src, width, vcol, rhs, ncol, use):
            s_oht, s_g, s_c = (sem(f"{tag}_{n}") for n in ("oht", "g", "c"))
            s_rows, s_used, s_sp, s_spf, s_dl, s_dlf = ([sem(f"{tag}_{n}{h}") for h in range(2)]
                                                        for n in ("rows", "used", "sp", "spf", "dl", "dlf"))
            rows = A1[:, 0:2 * G * width].rearrange("p (h k w) -> p h k w", h=2, k=G)
            o = 4096
            OHT = A1[:, o:o + 2048].rearrange("p (h k n) -> p h k n", h=2, k=G)
            dlb = A1[:, o + 2048:o + 3072].bitcast(BF16).rearrange("p (h n) -> p h n", h=2)
            prod = A1[:, o + 3072:o + 5120]
            look = [ps[:, 2 * h:2 * h + 2, :].rearrange("p a (k n) -> p (a k) n", n=P)[:, :, 0:ncol] for h in range(2)]
            with nc.Block() as block:
                @block.gpsimd
                def _(g):
                    def ready(i, h):
                        hold(g, s_used[h], i + 1)
                        hold(g, s_spf[h], i + 1)

                    gather_loop(g, table, lambda h, k: rows[:, h, k, :], s_rows, ready)

                @block.scalar
                def _(a):
                    broadcast_loop(a, lambda h: dlb[:, h, :], dl_dram, s_dl, s_dlf)

                @block.sync
                def _(sp):
                    for h in range(2):
                        sp.sem_inc(s_spf[h], 1)
                    with sp.Fori(0, NI) as i:
                        for h in range(2):
                            hold(sp, s_rows[h], i * (16 * G) + 16 * G)
                            sp.dma_start(spill[:, ds(i * (2 * G * P) + h * (G * P), G * P)].rearrange("p (k d) -> p k d", k=G),
                                         rows[:, h, :, vcol:vcol + D]).then_inc(s_sp[h], 16)
                            hold(sp, s_sp[h], 16 * i + 16)
                            sp.sem_inc(s_spf[h], 1)

                @block.vector
                def _(v):
                    for h in range(2):
                        v.tensor_copy(idx[:, h, :], idx_src[:, h * G:(h + 1) * G]).then_inc(s_used[h], 1)
                        v.sem_inc(s_dlf[h], 1)
                    with v.Fori(0, NI) as i:
                        for h in range(2):
                            hold(v, s_dl[h], 16 * i + 16)
                            v.tensor_scalar(OHT[:, h].rearrange("p k n -> p (k n)"), dlb[:, h, :], iota_p[:, 0:1], None,
                                            ALU.is_equal).then_inc(s_oht, 1)
                            hold(v, s_oht, 2 * i + (h + 1))
                            v.sem_inc(s_dlf[h], 1)
                            hold(v, s_g, 2 * i + (h + 1))
                            hold(v, s_rows[h], i * (16 * G) + 16 * G)
                            use(v, i, h, rows, look[h], prod, s_c)
                            v.tensor_copy(idx[:, h, :], idx_src[:, ds(i * (2 * G) + (2 + h) * G, G)]).then_inc(s_used[h], 1)

                @block.tensor
                def _(pe):
                    with pe.Fori(0, NI) as i:
                        tiles = load_tiles(pe, i * (2 * G), 2 * G)
                        for h in range(2):
                            hold(pe, s_oht, 2 * i + (h + 1))
                            hold(pe, s_used[h], i + 1)
                            for k in range(G):
                                last = pe.matmul(look[h][:, k, :], OHT[:, h, k, :], rhs(tiles[h * G + k]), start=True, stop=True)
                            last.then_inc(s_g, 1)

        NIB = NS // (NBUF * G)
        assert NIB * NBUF * G == NS

        PARTS = 2.0 ** 11
        EXO, EXW = NT * P, 32

        psx = psf[:, EXO:EXO + NT * EXW]

        def sum_stage(tag, wts, table, w, combine, combine_sp=None):
            s_oh, s_ohb, s_ex, s_ec, s_c, s_all, s_e = (
                sem(f"{tag}_{n}") for n in ("oh", "ohb", "ex", "ec", "c", "all", "e"))
            s_v, s_mf = ([sem(f"{tag}_{n}{h}") for h in range(NBUF)] for n in ("v", "mf"))
            val = A1[:, 0:NBUF * 1024].rearrange("p (h n) -> p h n", h=NBUF)
            OH = A1[:, NBUF * 1024:2 * NBUF * 1024].rearrange("p (h k n) -> p h k n", h=NBUF, k=G)
            OHB = A1[:, 2 * NBUF * 1024:5 * NBUF * 512].bitcast(F16).rearrange("p (h k n) -> p h k n", h=NBUF, k=G)
            EX = SM[:, 128:128 + NBUF * G * w].bitcast(F16).rearrange("p (h k w) -> p h k w", h=NBUF, k=G)
            RES = SM[:, 560:560 + G * w].rearrange("p (k w) -> p k w", k=G)
            with nc.Block() as block:
                @block.sync
                def _(sp):
                    with sp.Fori(0, NIB) as i:
                        for h in range(NBUF):
                            hold(sp, s_mf[h], i + 1)
                            sp.dma_start(val[:, h, :], spill[:, ds(i * (NBUF * G * P) + h * (G * P), G * P)]).then_inc(s_v[h], 16)
                    if combine_sp:
                        combine_sp(sp, s_e)

                @block.scalar
                def _(a):
                    with a.Fori(0, NIB) as i:
                        for h in range(NBUF):
                            hold(a, s_ohb, NBUF * i + (h + 1))
                            hold(a, s_ex, NBUF * i + (h + 1))
                            a.activation(OH[:, h].rearrange("p k n -> p (k n)"), OHB[:, h].rearrange("p k n -> p (k n)"),
                                         ACT.Copy).then_inc(s_oh, 1)

                @block.gpsimd
                def _(g):
                    with g.Fori(0, NIB) as i:
                        for h in range(NBUF):
                            n0 = i * (2 * NBUF) + 2 * h
                            src = table[:, ds(i * (NBUF * G * w) + h * (G * w), G * w)].rearrange("p (k w) -> p k w", k=G)
                            hold(g, s_mf[h], i + 1)
                            g.tensor_copy(EX[:, h, :, 0:w], src).then_inc(s_ec, 1)
                            hold(g, s_ec, n0 + 1)
                            g.tensor_tensor(RES, src, EX[:, h, :, 0:w], ALU.subtract).then_inc(s_ec, 1)
                            hold(g, s_ec, n0 + 2)
                            g.tensor_scalar(EX[:, h, :, w:2 * w], RES, PARTS, None, ALU.mult).then_inc(s_ex, 1)
                            hold(g, s_ex, NBUF * i + (h + 1))

                @block.vector
                def _(v):
                    with v.Fori(0, NIB) as i:
                        for h in range(NBUF):
                            hold(v, s_v[h], 16 * i + 16)
                            wt = wts[:, ds(i * (NBUF * G * H) + h * (G * H), G * H)]
                            vq = val[:, h, :].rearrange("p (q c) -> p q c", c=C)
                            v.tensor_tensor(vq, vq, bc(wt.unsqueeze(2), [P, G * H, C]), ALU.mult)
                            v.tensor_tensor(OHB[:, h], bc(iota16[:, :].unsqueeze(1), [P, G, P]),
                                            bc(dl16[:, ds(i * (NBUF * G) + h * G, G)].unsqueeze(2), [P, G, P]),
                                            ALU.is_equal).then_inc(s_ohb, 1)
                    v.wait_ge(s_all, 1)
                    combine(v, Chain(v, s_c), s_e)

                @block.tensor
                def _(pe):
                    for h in range(NBUF):
                        pe.sem_inc(s_mf[h], 1)
                    clear_acc(pe, 8)
                    with pe.Fori(0, NIB) as i:
                        tiles = load_tiles(pe, i * (NBUF * G), NBUF * G)
                        for h in range(NBUF):
                            hold(pe, s_oh, NBUF * i + (h + 1))
                            for k in range(G):
                                pe.matmul(psf[:, ds(tiles[h * G + k], P)], OH[:, h, k, :], val[:, h, k * P:(k + 1) * P],
                                          start=False, stop=False, skip_group_check=True)
                            for k in range(G):
                                last = pe.matmul(psx[:, ds(tiles[h * G + k] >> 2, 2 * w)], OHB[:, h, k, :], EX[:, h, k, :],
                                                 start=False, stop=False, skip_group_check=True)
                            last.then_inc(s_mf[h], 1)
                    for h in range(NBUF):
                        pe.wait_ge(s_mf[h], NIB + 1)
                    pe.nop().then_inc(s_all, 1)

        def small_sums(v, dst, w):
            ex = psx.rearrange("p (t w) -> p t w", w=EXW)
            v_low = SM[:, 128:128 + NT * w].rearrange("p (t w) -> p t w", w=w)
            return [lambda: v.tensor_scalar(v_low, ex[:, :, w:2 * w], 1.0 / PARTS, None, ALU.mult),
                    lambda: v.tensor_tensor(dst, v_low, ex[:, :, 0:w], ALU.add)]

        XN = NREL * H
        XC = XN + 1
        XP = 16

        def row4(ap):
            return ap.rearrange("p (b h e) -> p b h e", b=NB, h=H)

        CC = SM[0:H, 0:NS + 1]
        CI = SM[0:RB, 424:440].rearrange("p (b h) -> p b h", b=NB)
        EDGE = SM[0:RB, 440:456].rearrange("p (b h) -> p b h", b=NB)

        def scan_v(v, do, to_pe, from_pe, Xin, Y, kind, back):
            is_max = kind == "max"
            if is_max:
                same, carry, chain = (pen_b, pcar_b, pch_b) if back else (pen_f, pcar_f, pch_f)
            else:
                same, carry, chain = (same_b, carry_b, chain_b) if back else (same_f, carry_f, chain_f)
            keep = ALU.add if is_max else ALU.mult
            join = ALU.max if is_max or back else ALU.add
            samef = same[:, :, :, :].rearrange("p b h e -> p (b h e)")
            st = -1 if back else 1
            ini = -BIG if is_max else 0.0
            def scan():
                do(v.tensor_tensor_scan(Y[:, ::st], samef[:, ::st], Xin[:, ::st], ini, keep, join))

            v.memset(CC[:, NS:NS + 1] if back else CC[:, 0:1], ini)
            scan()
            to_pe.give(v.nop())
            e = P - 1 if back else 0
            edge = row4(Xin)[:, :, :, e]
            if not back:
                do(v.tensor_copy(EDGE, edge))
            o = 0 if back else 1
            from_pe.take(v)
            do(v.tensor_tensor_scan(CC[:, o:o + NS][:, ::st], chain[:, ::st], ps[0:H, 0, 0:NS][:, ::st], ini, keep, join))
            to_pe.give(v.nop())
            from_pe.take(v)
            do(v.tensor_tensor(CI, bc(carry[:, :, :], [RB, NB, H]),
                               ps[0:RB, 1, 0:NB * H].rearrange("p (b h) -> p b h", b=NB), keep))
            do(v.tensor_tensor(edge, edge, CI, join))
            scan()
            if not back:
                do(v.tensor_copy(edge, EDGE))

        def scan_pe(pe, from_v, to_v, Y, back):
            from_v.take(pe)
            e = 0 if back else P - 1
            for b in range(NB):
                last = pe.transpose(ps[0:H, 0, b * RB:(b + 1) * RB], row4(Y)[:, b, :, e], ident[0:RB, 0:RB])
            to_v.give(last)
            from_v.take(pe)
            o = 1 if back else 0
            for b in range(NB):
                last = pe.transpose(ps[0:RB, 1, b * H:(b + 1) * H], CC[:, o + b * RB:o + (b + 1) * RB], ident[0:H, 0:H])
            to_v.give(last)

        def total_v(v, do, to_pe, from_pe, Xin, Y, M, kind):
            scan_v(v, do, to_pe, from_pe, Xin, Y, kind, False)
            scan_v(v, do, to_pe, from_pe, Y, M, kind, True)

        def total_pe(pe, from_v, to_v, Y, M):
            scan_pe(pe, from_v, to_v, Y, False)
            scan_pe(pe, from_v, to_v, M, True)

        def to_rows_pe(pe, src, bank):
            for b in range(NB):
                for h in range(H):
                    last = pe.transpose(ps[0:RB, bank + b, h * P:(h + 1) * P], src[:, b * RB:(b + 1) * RB, h], ident[:, :])
            return last

        def to_edges_pe(pe, X, bank):
            for h in range(H):
                for b in range(NB):
                    last = pe.transpose(ps[:, bank + h, b * RB:(b + 1) * RB], row4(X)[:, b, h, :], ident[0:RB, 0:RB])
            return last

        NC0 = NREL * WN0
        HN = A1[:, 0:NT * NC0].rearrange("p (t r w) -> p t r w", t=NT, r=NREL)
        HNf = A1[:, 0:NT * NC0].rearrange("p (t w) -> p t w", t=NT)
        W0c = A2[:, 0:NC0].rearrange("p (r w) -> p r w", r=NREL)
        ATT = A2[:, 512:512 + 2 * NREL * P].rearrange("p (a r w) -> p a r w", a=2, r=NREL)
        WAT = A2[:, 1536:1536 + NREL * P].rearrange("p (r w) -> p r w", r=NREL)
        wrel = sb("wrel", [P, NREL])
        rl = SM[:, 384:384 + NREL]
        rmax, rsum = SM[:, 390:391], SM[:, 391:392]
        NDA = sb("NDA", [P, NT * 32])
        nda = NDA[:, :].rearrange("p (t w) -> p t w", t=NT)

        def l0_prep_sp(sp, s_wd):
            sp.dma_start(W0c[:, :, 0:D], W_in.rearrange("r i o -> i r o")).then_inc(s_wd, 16)
            sp.dma_start(ATT[:, 0].rearrange("p r w -> p (r w)"),
                         as_in.rearrange("r h c -> (r h c)").partition_broadcast(P)).then_inc(s_wd, 16)
            sp.dma_start(ATT[:, 1].rearrange("p r w -> p (r w)"),
                         ad_in.rearrange("r h c -> (r h c)").partition_broadcast(P)).then_inc(s_wd, 16)
            sp.dma_start(rl, relw_in.partition_broadcast(P)).then_inc(s_wd, 16)

        def l0_prep_v(v, do, s_wd, s_pw, s_pwc):
            v.wait_ge(s_wd, 64)
            for a in range(2):
                do(v.tensor_tensor(WAT, W0c[:, :, 0:D], ATT[:, a], ALU.mult))
                for r in range(NREL):
                    ins = v.tensor_reduce(W0c[:, r, D + a * H:D + (a + 1) * H],
                                          WAT[:, r].rearrange("p (h c) -> p h c", h=H), AX, ALU.add)
                do(ins)
            do(v.tensor_reduce(rmax, rl, AX, ALU.max))
            do(v.tensor_scalar(wrel[:, :], rl, rmax, None, ALU.subtract))

        def l0_after_v(v, do):
            a_s = HN[:, :, :, D:D + H]
            a_d = HN[:, :, :, D + H:D + 2 * H]
            od = nda[:, :, 0:NREL * H]
            os_ = nda[:, :, NREL * H:2 * NREL * H]
            for r in range(NREL):
                v.tensor_copy(od[:, :, r * H:(r + 1) * H], a_d[:, :, r, :])
                ins = v.tensor_tensor(os_[:, :, r * H:(r + 1) * H], a_s[:, :, r, :], a_d[:, :, r, :], ALU.add)
            do(ins)
            do(v.scalar_tensor_tensor(os_, os_, 0.2, os_, ALU.mult, ALU.max))
            for r in range(NREL):
                ins = v.tensor_scalar(LIM[:, :, r], t3T[:, :], float(r), None, ALU.is_equal)
            do(ins)
            do(v.tensor_scalar(A3[:, 0:NS * NREL], A3[:, 0:NS * NREL], 1e30, -NEG, ALU.mult, ALU.add))

        def store_rows(sp, s_st, table, src, tiles, width):
            a, b = tiles[0], tiles[-1] + 1
            sp.dma_start(table[a * P:b * P, :].rearrange("(t p) w -> p t w", p=P), src[:, a:b, 0:width]).then_inc(s_st, 16)

        def l0_table_sp(sp, s_st, tiles):
            for r in range(NREL):
                store_rows(sp, s_st, tab0[r * NP:(r + 1) * NP, :], HN[:, :, r, :], tiles, WA0)
            if tiles[-1] == NT - 1:
                sp.wait_ge(s_st, 16 * len(RUNS) * NREL)

        AS = A3[:, 0:NS * H].rearrange("p (s h) -> p s h", h=H)
        LIM = A3[:, 0:NS * NREL].rearrange("p (s r) -> p s r", r=NREL)
        SC8 = SM[:, 0:G * NREL * H].rearrange("p (k r h) -> p k r h", k=G, r=NREL)
        ADS = A2[:, 0:NS * 24].rearrange("p (s w) -> p s w", w=24)
        CS = A2[:, NS * 24:NS * 24 + NS * XC].rearrange("p (s w) -> p s w", w=XC)
        CSf = A2[:, NS * 24:NS * 24 + NS * XC]
        WT = A3[:, 3328:4992]
        WTv = WT.rearrange("p (s h) -> p s h", h=H)
        R_ = [A1[0:RB, 2048 * k:2048 * (k + 1)] for k in range(5)]
        ACC = hf[0:RB, 0:2048]
        ADS_N = 24

        def l0_use(v, i, h, rows, look, prod, s_c):
            s0, n0 = i * (2 * G) + h * G, i * 6 + 3 * h
            out = ADS[:, ds(s0, G), :]
            v.tensor_copy(out[:, :, NREL * H:], look[:, :, NREL * H:])
            v.tensor_tensor(SC8, look[:, :, 0:NREL * H].rearrange("p k (r h) -> p k r h", r=NREL),
                            bc(rows[:, h, :, D:D + H].unsqueeze(2), [P, G, NREL, H]), ALU.add).then_inc(s_c, 1)
            hold(v, s_c, n0 + 1)
            v.scalar_tensor_tensor(SC8, SC8, 0.2, SC8, ALU.mult, ALU.max).then_inc(s_c, 1)
            hold(v, s_c, n0 + 2)
            v.tensor_tensor(out[:, :, 0:NREL * H].rearrange("p k (r h) -> p k r h", r=NREL), SC8,
                            bc(LIM[:, ds(s0, G), :].unsqueeze(3), [P, G, NREL, H]), ALU.min).then_inc(s_c, 1)
            hold(v, s_c, n0 + 3)

        def l0_softmax():
            s_c, s_x1, s_e1 = sem("l0s_c"), sem("l0s_x1"), sem("l0s_e1")
            s_vp, s_pv, s_w, s_zd = sem("l0s_vp"), sem("l0s_pv"), sem("l0s_w"), sem("l0s_zd")
            s_in, s_cp = sem("l0s_in"), sem("l0s_cp")
            S, Y, M = R_[1:4]
            XS = (R_[0], R_[4], R_[0])
            fills = ["X0"] + [f"{n}{q}" for r in range(NREL) for n, q in (("S", r), ("X", r + 1), ("O", r)) if (n, q) != ("X", NREL)]
            nth = {name: k + 1 for k, name in enumerate(fills)}
            with nc.Block() as block:
                @block.sync
                def _(sp):
                    for k in range(G):
                        sp.dma_start(scat[k][0:NP, :].rearrange("(p a) d -> p a d", p=P),
                                     bc(zeros[:, 0:D].unsqueeze(1), [P, NT, D])).then_inc(s_zd, 16)
                    sp.wait_ge(s_zd, 16 * G)

                @block.scalar
                def _(a):
                    a.wait_ge(s_w, 1)
                    a.activation(wrel[:, :], wrel[:, :], ACT.Exp, accum_out=rsum).then_inc(s_w, 1)

                    def rows_in(name, dst):
                        a.wait_ge(s_in, nth[name])
                        a.activation(dst, psf[0:RB, 2048:4096], ACT.Copy).then_inc(s_cp, 1)

                    rows_in("X0", XS[0])
                    for r in range(NREL):
                        rows_in(f"S{r}", S)
                        a.wait_ge(s_x1, 2 * r + 1)
                        a.activation(XS[r], XS[r], ACT.Exp).then_inc(s_e1, 1)
                        a.wait_ge(s_x1, 2 * r + 2)
                        a.activation(S, S, ACT.Exp).then_inc(s_e1, 1)
                        if r + 1 < NREL:
                            rows_in(f"X{r + 1}", XS[r + 1])
                        a.wait_ge(s_in, nth[f"O{r}"])
                        for h in range(H):
                            ins = a.activation(CS[:, :, r * H + h], ps[:, 4 + h, 0:NS], ACT.Copy)
                        ins.then_inc(s_cp, 1)

                @block.tensor
                def _(pe):
                    vp, pv = Hand(s_vp), Hand(s_pv)

                    def rows_out(name, col):
                        if nth[name] > 1:
                            pe.wait_ge(s_cp, nth[name] - 1)
                        to_rows_pe(pe, ADS[:, :, col:col + H], 4).then_inc(s_in, 1)

                    rows_out("X0", 0)
                    for r in range(NREL):
                        rows_out(f"S{r}", NREL * H + r * H)
                        total_pe(pe, vp, pv, Y, M)
                        if r + 1 < NREL:
                            rows_out(f"X{r + 1}", (r + 1) * H)
                        total_pe(pe, vp, pv, Y, M)
                        vp.take(pe)
                        pe.wait_ge(s_cp, nth[f"O{r}"] - 1)
                        to_edges_pe(pe, S, 4).then_inc(s_in, 1)
                    vp.take(pe)
                    pe.wait_ge(s_cp, len(fills))
                    to_edges_pe(pe, ACC, 0)
                    for b in range(NB):
                        last = pe.transpose(ps[:, 4, b * RB:(b + 1) * RB], is_last[:, b, :], ident[0:RB, 0:RB])
                    pv.give(last)

                @block.vector
                def _(v):
                    do = Chain(v, s_c)
                    vp, pv = Hand(s_vp), Hand(s_pv)
                    v.nop().then_inc(s_w, 1)
                    v.wait_ge(s_w, 2)
                    do(v.reciprocal(rmax, rsum))
                    do(v.tensor_scalar(wrel[:, :], wrel[:, :], rmax, None, ALU.mult))
                    for r in range(NREL):
                        X = XS[r]
                        v.wait_ge(s_cp, nth[f"X{r}"])
                        total_v(v, do, vp, pv, X, Y, M, "max")
                        v.wait_ge(s_cp, nth[f"S{r}"])
                        do(v.tensor_tensor(M, M, S, ALU.max))
                        v.tensor_tensor(X, X, M, ALU.subtract).then_inc(s_x1, 1)
                        v.tensor_tensor(S, S, M, ALU.subtract).then_inc(s_x1, 1)
                        v.wait_ge(s_x1, 2 * r + 2)
                        v.wait_ge(s_e1, 2 * r + 1)
                        total_v(v, do, vp, pv, X, Y, M, "sum")
                        v.wait_ge(s_e1, 2 * r + 2)
                        do(v.tensor_tensor(M, M, S, ALU.add))
                        do(v.reciprocal(M, M))
                        do(v.scalar_tensor_tensor(S, S, wrel[0:RB, r:r + 1], M, ALU.mult, ALU.mult))
                        do(v.tensor_tensor(row4(S), row4(S), bc(is_last[:, :, :].unsqueeze(2), [RB, NB, H, P]), ALU.mult))
                        vp.give(v.nop())
                        if r:
                            do(v.scalar_tensor_tensor(X, X, wrel[0:RB, r:r + 1], M, ALU.mult, ALU.mult))
                            do(v.tensor_tensor(ACC, ACC, X, ALU.add))
                        else:
                            do(v.scalar_tensor_tensor(ACC, X, wrel[0:RB, r:r + 1], M, ALU.mult, ALU.mult))
                    vp.give(v.nop())
                    pv.take(v)
                    for h in range(H):
                        ins = v.tensor_copy(WTv[:, :, h], ps[:, h, 0:NS])
                    do(ins)
                    do(v.tensor_copy(CS[:, :, XN], ps[:, 4, 0:NS]))

        CO = A3[:, 0:NT * XP].rearrange("p (t w) -> p t w", w=XP)
        HB = [A2[:, 3200 * k:3200 * (k + 1)].rearrange("p (t d) -> p t d", t=NT) for k in range(4)]
        BIA = A3[:, 512:512 + NREL * D].rearrange("p (r d) -> p r d", r=NREL)
        CF = A3[:, 1024:1024 + NT * H].rearrange("p (t h) -> p t h", h=H)
        ABS = A3[:, 1152:1152 + NT]

        def l0_combine_sp(sp, s_e):
            sp.wait_ge(s_e, 1)
            for r in range(NREL):
                sp.dma_start(HB[r], tab0[r * NP:(r + 1) * NP, 0:D].rearrange("(t p) w -> p t w", p=P)).then_inc(s_e, 16)
            sp.dma_start(BIA.rearrange("p r d -> p (r d)"), bias_in.rearrange("r d -> (r d)").partition_broadcast(P)).then_inc(s_e, 16)
            sp.wait_ge(s_e, 65)

        def l0_combine(v, do, s_e):
            v.nop().then_inc(s_e, 1)
            do(v.tensor_tensor(xf, xf, psf[:, 0:NT * P], ALU.add))
            for step in small_sums(v, CO[:, :, 0:XC], XC):
                do(step())
            do(v.tensor_scalar(ABS, CO[:, :, XN], -1.0, 1.0, ALU.mult, ALU.add))
            v.wait_ge(s_e, 65)
            for r in range(NREL):
                do(v.tensor_scalar(CF, bc(ABS.unsqueeze(2), [P, NT, H]), wrel[:, r:r + 1], None, ALU.mult))
                do(v.tensor_tensor(CF, CF, CO[:, :, r * H:(r + 1) * H], ALU.add))
                t4 = HB[3].rearrange("p t (h c) -> p t h c", h=H)
                do(v.tensor_tensor(t4, HB[r].rearrange("p t (h c) -> p t h c", h=H),
                                   bc(CF.unsqueeze(3), [P, NT, H, C]), ALU.mult))
                do(v.tensor_tensor(x[:, :, :], x[:, :, :], HB[3], ALU.add))
                b0, br = BIA[:, 0, :], BIA[:, r, :]
                do(v.scalar_tensor_tensor(b0, br, wrel[:, r:r + 1], b0, ALU.mult, ALU.add) if r
                   else v.tensor_scalar(b0, b0, wrel[:, 0:1], None, ALU.mult))
            do(v.tensor_tensor(x[:, :, :], x[:, :, :], bc(BIA[:, 0:1, :], [P, NT, D]), ALU.add))

        node_stage("n0", [[(W0c.rearrange("p r w -> p (r w)"), NC0, "va"[t % 2], copy_to(HNf[:, t, :]))] for t in range(NT)],
                   prep_v=l0_prep_v, prep_sp=l0_prep_sp, table_sp=l0_table_sp, between_v=scan_masks, after_v=l0_after_v)
        lookup_stage("k0", tab0, i0, WA0, 0, lambda r: NDA[:, ds(r >> 2, ADS_N)], ADS_N, l0_use)
        l0_softmax()
        sum_stage("m0", WT, CSf, XC, l0_combine, combine_sp=l0_combine_sp)

        def finish():
            s_fin = sem("s_fin")
            with nc.Block() as block:
                @block.sync
                def _(sp):
                    sp.dma_start(out[0:FULL * P, :].rearrange("(t p) d -> p t d", p=P), x[:, 0:FULL, :]).then_inc(s_fin, 16)
                    sp.dma_start(out[FULL * P:N, :], x[0:REST, FULL, :]).then_inc(s_fin, 16)
                    sp.wait_ge(s_fin, 32)

        end_layer()

        Bo = A1[:, 6400:6912].rearrange("p (k d) -> p k d", k=NBASE)
        BT = A1[:, 6912:7424].rearrange("p (k d) -> p k d", k=NBASE)
        W0o = A1[:, 7424:7552]
        WT1 = A1[:, 7552:7552 + (NRAT + 1) * D]
        Abc = A1[:, 8320:8320 + NRAT * NBASE]
        T1 = A2[:, 0:NT * NRAT * D].rearrange("p (t w) -> p t w", t=NT)
        dinv = sb("dinv", [P, NT])

        def l1_prep_sp(sp, s_wd):
            sp.dma_start(Bo, B_in.rearrange("k o i -> o k i")).then_inc(s_wd, 16)
            sp.dma_start(W0o, W0_in).then_inc(s_wd, 16)
            sp.dma_start(Abc, A_in.rearrange("r k -> (r k)").partition_broadcast(P)).then_inc(s_wd, 16)

        def l1_prep_pe(pe, s_wd, s_pw):
            pe.wait_ge(s_wd, 48)
            for k in range(NBASE):
                pe.transpose(ps[:, 7, k * P:(k + 1) * P], Bo[:, k, :], ident[:, :])
            pe.transpose(ps[:, 6, 0:P], W0o, ident[:, :]).then_inc(s_pw, 1)

        def l1_prep_v(v, do, s_wd, s_pw, s_pwc):
            v.wait_ge(s_wd, 48)
            v.wait_ge(s_pw, 1)
            do(v.tensor_copy(BT.rearrange("p k d -> p (k d)"), ps[:, 7, :]))
            do(v.tensor_copy(WT1[:, NRAT * D:], ps[:, 6, 0:P]))
            v.nop().then_inc(s_pwc, 1)
            for k in range(NBASE):
                for r in range(NRAT):
                    w, a = WT1[:, r * D:(r + 1) * D], Abc[:, r * NBASE + k:r * NBASE + k + 1]
                    ins = (v.scalar_tensor_tensor(w, BT[:, k, :], a, w, ALU.mult, ALU.add) if k
                           else v.tensor_scalar(w, BT[:, k, :], a, None, ALU.mult))
                do(ins)

        def l1_table_sp(sp, s_st, tiles):
            for r in range(NRAT):
                store_rows(sp, s_st, tab1[r * NP:(r + 1) * NP, :], T1[:, :, r * D:(r + 1) * D], tiles, D)
            if tiles[-1] == NT - 1:
                sp.wait_ge(s_st, 16 * len(RUNS) * NRAT)

        def add_to_x(t):
            return lambda eng, src: eng.tensor_tensor(x[:, t, :], x[:, t, :], src, ALU.add)

        node_stage("n1", [[(WT1[:, 0:512], 512, "a", copy_to(T1[:, t, 0:512])),
                           (WT1[:, 512:640], 128, "v", copy_to(T1[:, t, 512:640])),
                           (WT1[:, 640:768], 128, "v", add_to_x(t))] for t in range(NT)],
                   prep_v=l1_prep_v, prep_pe=l1_prep_pe, prep_sp=l1_prep_sp, table_sp=l1_table_sp)

        def l1_edges():
            s_oh, s_c, s_all, s_v, s_sq = (sem(f"e1_{n}") for n in ("oh", "c", "all", "v", "sq"))
            s_rows, s_mf, s_idx = ([sem(f"e1_{n}{h}") for h in range(2)] for n in ("rows", "mf", "idx"))
            rows = A1[:, 0:2048].rearrange("p (h k w) -> p h k w", h=2, k=G)
            OH = A1[:, 2048:4096].rearrange("p (h k n) -> p h k n", h=2, k=G)
            LO_ = A1[:, 4096:5120].bitcast(BF16).rearrange("p (h k n) -> p h k n", h=2, k=G)
            HI_ = A1[:, 5120:5120 + G * NT].bitcast(BF16).rearrange("p (h k n) -> p h k n", h=2, k=G)
            deg = SM[:, 0:NT]
            with nc.Block() as block:
                @block.gpsimd
                def _(g):
                    def ready(i, h):
                        hold(g, s_mf[h], i + 1)
                        hold(g, s_idx[h], i + 1)

                    gather_loop(g, tab1, lambda h, k: rows[:, h, k, :], s_rows, ready)

                @block.scalar
                def _(a):
                    a.wait_ge(s_v, 1)
                    a.activation(deg, deg, ACT.Sqrt).then_inc(s_sq, 1)

                @block.vector
                def _(v):
                    do = Chain(v, s_c)
                    for h in range(2):
                        v.tensor_copy(idx[:, h, :], i1[:, h * G:(h + 1) * G]).then_inc(s_idx[h], 1)
                    with v.Fori(0, NI) as i:
                        for h in range(2):
                            s0 = i * (2 * G) + h * G
                            hold(v, s_mf[h], i + 1)
                            a, b = onehot_in(dlT[:, ds(s0, G)])
                            v.tensor_tensor(OH[:, h], a, b, ALU.is_equal)
                            a, b = onehot_in(loT[:, ds(s0, G)])
                            v.tensor_tensor(LO_[:, h], a, b, ALU.is_equal)
                            v.tensor_tensor(HI_[:, h], bc(iota_row[:, 0:NT].unsqueeze(1), [P, G, NT]),
                                            bc(hiT[:, ds(s0, G)].unsqueeze(2), [P, G, NT]), ALU.is_equal).then_inc(s_oh, 1)
                            hold(v, s_rows[h], i * (16 * G) + 16 * G)
                            v.tensor_copy(idx[:, h, :], i1[:, ds(i * (2 * G) + (2 + h) * G, G)]).then_inc(s_idx[h], 1)
                    v.wait_ge(s_all, 1)
                    do(v.tensor_tensor(xf, xf, psf[:, 0:NT * P], ALU.add))
                    do(v.tensor_copy(deg, ps[:, 7, 0:NT]))
                    do(v.scalar_tensor_tensor(deg[:, FULL:NT], iota_p[:, :], float(REST), deg[:, FULL:NT], ALU.is_ge, ALU.add))
                    v.nop().then_inc(s_v, 1)
                    v.wait_ge(s_sq, 1)
                    do(v.reciprocal(dinv[:, :], deg))

                @block.tensor
                def _(pe):
                    for h in range(2):
                        pe.sem_inc(s_mf[h], 1)
                    clear_acc(pe, 8)
                    with pe.Fori(0, NI) as i:
                        tiles = load_tiles(pe, i * (2 * G), 2 * G)
                        for h in range(2):
                            hold(pe, s_oh, 2 * i + (h + 1))
                            hold(pe, s_rows[h], i * (16 * G) + 16 * G)
                            for k in range(G):
                                pe.matmul(psf[:, ds(tiles[h * G + k], P)], OH[:, h, k, :], rows[:, h, k, :],
                                          start=False, stop=False, skip_group_check=True)
                            for k in range(G):
                                last = pe.matmul(ps[:, 7, 0:NT], LO_[:, h, k, :], HI_[:, h, k, :],
                                                 start=False, stop=False, skip_group_check=True)
                            last.then_inc(s_mf[h], 1)
                    for h in range(2):
                        pe.wait_ge(s_mf[h], NI + 1)
                    pe.nop().then_inc(s_all, 1)

        l1_edges()
        end_layer()

        def l2_edges():
            s_c, s_var, s_std = sem("e2_c"), sem("e2_var"), sem("e2_std")
            s_oht, s_seq, s_g, s_val, s_sum, s_gs, s_ix, s_prev, s_cc = (
                sem(f"e2_{n}") for n in ("oht", "seq", "g", "val", "sum", "gs", "ix", "prev", "cc"))
            s_dl, s_dlf, s_sr = ([sem(f"e2_{n}{h}") for h in range(2)] for n in ("dl", "dlf", "sr"))
            s_t = [sem(f"e2_t{k}") for k in range(G)]
            s_in = sem("e2_in")
            OHT = A1[:, 0:2048].rearrange("p (h k n) -> p h k n", h=2, k=G)
            dlb = A1[:, 2048:3072].bitcast(BF16).rearrange("p (h n) -> p h n", h=2)
            srcb = A1[:, 3072:5120].rearrange("p (h n) -> p h n", h=2)
            SEQ = A1[:, 5120:7168].rearrange("p (h k n) -> p h k n", h=2, k=G)
            val = A1[:, 7168:9216].rearrange("p (h k n) -> p h k n", h=2, k=G)
            gs = A3[:, 0:2048].rearrange("p (h k n) -> p h k n", h=2, k=G)
            tmp = A3[:, 2048:3072].rearrange("p (k n) -> p k n", k=G)
            LOW = A3[:, 3072:3200]
            spare = SM[:, 512:513]
            cnt8, first8, d8 = SM[:, 520:528], SM[:, 528:536], SM[:, 536:544]
            SIX = SMI[:, 0:2 * G].rearrange("p (h k) -> p h k", h=2)
            look = [ps[:, 2 * h:2 * h + 2, :].rearrange("p a n -> p (a n)") for h in range(2)]
            tot = [ps[:, 4 + 2 * h:6 + 2 * h, :].rearrange("p a n -> p (a n)") for h in range(2)]
            with nc.Block() as block:
                @block.vector
                def _(v):
                    do = Chain(v, s_c)
                    norm_stats_v(v, do, s_var, s_std, scale=dinv[:, :])
                    do(v.tensor_scalar(LOW, iota_row[:, :], iota_p[:, 0:1], None, ALU.is_lt))
                    do(v.tensor_scalar(spare, iota_p[:, 0:1], float(NP), None, ALU.add))

                @block.scalar
                def _(a):
                    a.wait_ge(s_var, 1)
                    a.activation(std, var, ACT.Sqrt).then_inc(s_std, 1)
                    a.wait_ge(s_var, 2)
                    for t in range(NT):
                        norm_relu_a(a, t)

            with nc.Block() as block:
                @block.sync
                def _(sp):
                    with sp.Fori(0, NI) as i:
                        for h in range(2):
                            hold(sp, s_dlf[h], i + 1)
                            c0 = i * (2 * G * P) + h * (G * P)
                            sp.dma_start(dlb[:, h, :], dl_dram[ds(c0, G * P)].partition_broadcast(P)).then_inc(s_dl[h], 16)
                            sp.dma_start(srcb[:, h, :], srcrow_dram[ds(c0, G * P)].partition_broadcast(P)).then_inc(s_sr[h], 16)

                @block.vector
                def _(v):
                    for h in range(2):
                        v.sem_inc(s_dlf[h], 1)
                    with v.Fori(0, NI) as i:
                        for h in range(2):
                            s0 = i * (2 * G) + h * G
                            hold(v, s_dl[h], 16 * i + 16)
                            hold(v, s_g, 2 * i + (h + 1))
                            v.tensor_scalar(OHT[:, h].rearrange("p k n -> p (k n)"), dlb[:, h, :], iota_p[:, 0:1], None,
                                            ALU.is_equal).then_inc(s_oht, 1)
                            hold(v, s_sr[h], 16 * i + 16)
                            hold(v, s_sum, 2 * i + (h + 1))
                            v.tensor_tensor(SEQ[:, h], srcb[:, h, :].rearrange("p (k n) -> p k n", k=G),
                                            bc(srcT[:, ds(s0, G)].unsqueeze(2), [P, G, P]), ALU.is_equal).then_inc(s_seq, 1)
                            hold(v, s_seq, 2 * i + (h + 1))
                            hold(v, s_oht, 2 * i + (h + 1))
                            v.sem_inc(s_dlf[h], 1)
                            n0 = i * 8 + 4 * h

                            def step(ins, k):
                                ins.then_inc(s_cc, 1)
                                hold(v, s_cc, i * 10 + (5 * h + k))
                            step(v.tensor_tensor(tmp, SEQ[:, h], bc(LOW.unsqueeze(1), [P, G, P]), ALU.mult), 1)
                            step(v.tensor_reduce(cnt8, tmp, AX, ALU.add), 2)
                            step(v.tensor_scalar(d8, srcT[:, ds(s0, G)], spare, None, ALU.subtract), 3)
                            step(v.scalar_tensor_tensor(first8, cnt8, 0.0, d8, ALU.is_equal, ALU.mult), 4)
                            step(v.tensor_scalar(first8, first8, spare, None, ALU.add), 5)
                            hold(v, s_prev, 2 * i + (h + 1))
                            v.tensor_copy(SIX[:, h, :], first8).then_inc(s_ix, 1)
                            hold(v, s_ix, 2 * i + (h + 1))

                @block.tensor
                def _(pe):
                    pe.sem_inc(s_g, 2)
                    pe.sem_inc(s_sum, 2)
                    with pe.Fori(0, NI) as i:
                        tiles = load_tiles(pe, i * (2 * G), 2 * G)
                        for h in range(2):
                            hold(pe, s_oht, 2 * i + (h + 1))
                            hold(pe, s_val, 2 * i + (h + 1))
                            for k in range(G):
                                last = pe.matmul(look[h][:, k * P:(k + 1) * P], OHT[:, h, k, :], hf[:, ds(tiles[h * G + k], P)],
                                                 start=True, stop=True)
                            last.then_inc(s_g, 1)
                            hold(pe, s_seq, 2 * i + (h + 1))
                            hold(pe, s_val, 2 * i + (h + 3))
                            hold(pe, s_gs, 2 * i + (h + 1))
                            for k in range(G):
                                last = pe.matmul(tot[h][:, k * P:(k + 1) * P], SEQ[:, h, k, :], val[:, h, k, :],
                                                 start=True, stop=True)
                            last.then_inc(s_sum, 1)

                @block.scalar
                def _(a):
                    a.sem_inc(s_val, 2)
                    a.sem_inc(s_gs, 2)
                    with a.Fori(0, NI) as i:
                        for h in range(2):
                            hold(a, s_g, 2 * i + (h + 3))
                            hold(a, s_sum, 2 * i + (h + 1))
                            a.activation(val[:, h].rearrange("p k n -> p (k n)"), look[h], ACT.Copy).then_inc(s_val, 1)
                            hold(a, s_sum, 2 * i + (h + 3))
                            hold(a, s_prev, 2 * i + (h + 1))
                            a.activation(gs[:, h].rearrange("p k n -> p (k n)"), tot[h], ACT.Copy).then_inc(s_gs, 1)

                @block.gpsimd
                def _(g):
                    g.sem_inc(s_prev, 1)
                    for k in range(G):
                        g.dma_start(scat[k][NP:NDUMP, :], zeros[:, 0:D]).then_inc(s_t[k], 16)
                    with g.Fori(0, NI) as i:
                        for h in range(2):
                            hold(g, s_gs, 2 * i + (h + 3))
                            hold(g, s_ix, 2 * i + (h + 1))
                            for k in range(G):
                                hold(g, s_t[k], i * 32 + (16 * h + 16))
                                g.indirect_dma_start(out=scat[k], out_offset=bass.IndirectOffsetOnAxis(ap=SIX[:, h, k:k + 1], axis=0),
                                                     in_=gs[:, h, k, :], in_offset=None,
                                                     compute_op=ALU.add).then_inc(s_t[k], 16)
                            g.sem_inc(s_prev, 1)
                    for k in range(G):
                        g.wait_ge(s_t[k], 16 + 32 * NI)

            TB = [A2[:, 3200 * k:3200 * (k + 1)] for k in range(5)] + [A1[:, 3200 * k:3200 * (k + 1)] for k in range(3)]
            with nc.Block() as block:
                @block.sync
                def _(sp):
                    for k in range(G):
                        sp.dma_start(TB[k].rearrange("p (t d) -> p t d", t=NT),
                                     scat[k][0:NP, :].rearrange("(t p) d -> p t d", p=P)).then_inc(s_t2[k], 16)
                    for k in range(G):
                        sp.wait_ge(s_t2[k], 16)

                @block.vector
                def _(v):
                    do = Chain(v, s_in)
                    v.wait_ge(s_t2[0], 16)
                    for k in range(1, G):
                        v.wait_ge(s_t2[k], 16)
                        do(v.tensor_tensor(TB[0], TB[0], TB[k], ALU.add))
                    do(v.tensor_tensor(hid[:, :, :], TB[0].rearrange("p (t d) -> p t d", t=NT),
                                       bc(dinv[:, :].unsqueeze(2), [P, NT, D]), ALU.mult))

        s_t2 = [sem(f"e2_l{k}") for k in range(G)]
        l2_edges()
        W2o, W2T = A1[:, 0:P], A1[:, P:2 * P]

        def l2_prep_sp(sp, s_wd):
            sp.dma_start(W2o, W2_in).then_inc(s_wd, 16)

        def l2_prep_pe(pe, s_wd, s_pw):
            pe.wait_ge(s_wd, 16)
            pe.transpose(ps[:, 7, 0:P], W2o, ident[:, :]).then_inc(s_pw, 1)

        def l2_prep_v(v, do, s_wd, s_pw, s_pwc):
            v.wait_ge(s_pw, 1)
            do(v.tensor_copy(W2T, ps[:, 7, 0:P]))
            v.nop().then_inc(s_pwc, 1)

        def add_relu(t):
            return lambda eng, src: eng.scalar_tensor_tensor(x[:, t, :], src, 0.0, x[:, t, :], ALU.max, ALU.add)

        node_stage("n2", [[(W2T, D, "v", add_relu(t))] for t in range(NT)], norm=False,
                   prep_v=l2_prep_v, prep_pe=l2_prep_pe, prep_sp=l2_prep_sp)
        end_layer()

        KV = A2[:, 0:NT * 4 * D].rearrange("p (t w) -> p t w", t=NT)
        WALL = A2[:, 12800:13312]
        BALL = A2[:, 13312:13824]
        ALf = A3[:, 0:NS * H]

        def l3_layer(l):
            Wq, Wk, Wv, Ws, bq, bk, bv, bs = l3[8 * l:8 * l + 8]
            tag = f"t{l}"

            def prep_sp(sp, s_wd):
                for k, (w, b) in enumerate(((Wk, bk), (Wv, bv), (Wq, bq), (Ws, bs))):
                    sp.dma_start(WALL[:, k * D:(k + 1) * D], w).then_inc(s_wd, 16)
                    sp.dma_start(BALL[:, k * D:(k + 1) * D], b.partition_broadcast(P)).then_inc(s_wd, 16)

            def prep_v(v, do, s_wd, s_pw, s_pwc):
                v.wait_ge(s_wd, 128)

            def put(t):
                return lambda eng, src: eng.tensor_tensor(KV[:, t, :], src, BALL, ALU.add)

            def table_sp(sp, s_st, tiles):
                store_rows(sp, s_st, tab3, KV, tiles, 2 * D)
                if tiles[-1] == NT - 1:
                    sp.wait_ge(s_st, 16 * len(RUNS))

            node_stage(tag + "n", [[(WALL, 4 * D, "v", put(t))] for t in range(NT)], norm=(l == 0),
                       prep_v=prep_v, prep_sp=prep_sp, table_sp=table_sp)

            def use(v, i, h, rows, look, prod, s_c):
                pk = prod[:, h * 1024:(h + 1) * 1024]
                v.tensor_tensor(pk.rearrange("p (k d) -> p k d", k=G), rows[:, h, :, 0:D], look, ALU.mult).then_inc(s_c, 1)
                hold(v, s_c, 4 * i + (2 * h + 1))
                v.tensor_reduce(ALf[:, ds(i * (2 * G * H) + h * (G * H), G * H)],
                                pk.rearrange("p (q c) -> p q c", c=C), AX, ALU.add).then_inc(s_c, 1)
                hold(v, s_c, 4 * i + (2 * h + 2))

            lookup_stage(tag + "k", tab3, i3, 2 * D, D, lambda r: A2[:, ds(r * 4 + 2 * D, D)], D, use)

            s_c, s_x1, s_e1, s_vp, s_pv = (sem(f"{tag}s_{n}") for n in ("c", "x1", "e1", "vp", "pv"))
            X, Y, M = R_[0:3]
            with nc.Block() as block:
                @block.scalar
                def _(a):
                    a.wait_ge(s_x1, 1)
                    a.activation(X, X, ACT.Exp, scale=float(C) ** -0.5).then_inc(s_e1, 1)

                @block.tensor
                def _(pe):
                    vp, pv = Hand(s_vp), Hand(s_pv)
                    pv.give(to_rows_pe(pe, AS, 0))
                    total_pe(pe, vp, pv, Y, M)
                    vp.take(pe)
                    pv.give(to_edges_pe(pe, X, 2))

                @block.vector
                def _(v):
                    do = Chain(v, s_c)
                    vp, pv = Hand(s_vp), Hand(s_pv)
                    pv.take(v)
                    do(v.tensor_copy(X, psf[0:RB, 0:2048]))
                    total_v(v, do, vp, pv, X, Y, M, "max")
                    do(v.tensor_tensor(X, X, M, ALU.subtract))
                    v.nop().then_inc(s_x1, 1)
                    v.wait_ge(s_e1, 1)
                    vp.give(v.nop())
                    pv.take(v)
                    for h in range(H):
                        ins = v.tensor_copy(WTv[:, :, h], ps[:, 2 + h, 0:NS])
                    do(ins)

            DEN = SM[:, 0:NT * H]

            def combine(v, do, s_e):
                for step in small_sums(v, DEN.rearrange("p (t h) -> p t h", h=H), H):
                    do(step())
                do(v.tensor_scalar(DEN, DEN, 1e-16, None, ALU.max))
                do(v.reciprocal(DEN, DEN))
                do(v.tensor_tensor(hf.rearrange("p (q c) -> p q c", c=C),
                                   psf[:, 0:NT * P].rearrange("p (q c) -> p q c", c=C),
                                   bc(DEN.unsqueeze(2), [P, NT * H, C]), ALU.mult))
                do(v.tensor_tensor(hid[:, :, :], hid[:, :, :], KV[:, :, 3 * D:4 * D], ALU.add))
                if l == 0:
                    do(v.tensor_scalar(hid[:, :, :], hid[:, :, :], 0.0, None, ALU.max))
                else:
                    do(v.scalar_tensor_tensor(xf, hf, 0.0, xf, ALU.max, ALU.add))

            sum_stage(tag + "m", WT, WT, H, combine)

        l3_layer(0)
        end_layer()
        l3_layer(1)
        finish()


_L3 = [f"L3_gnn_{k}{l}" for l in range(2) for k in ("Wq", "Wk", "Wv", "Ws", "bq", "bk", "bv", "bs")]
_INS = ["x", "src", "dst", "edge_type_3", "edge_type_5", "L0_gnn_W", "L0_gnn_att_src", "L0_gnn_att_dst",
        "L0_gnn_bias", "L0_gnn_rel_w", "L1_gnn_B", "L1_gnn_A", "L1_gnn_W0", "L2_gnn_weight"] + _L3


def kernel(**inputs):
    import numpy as _np
    import concourse.bacc as _bacc
    from concourse import mybir as _mybir
    from concourse.bass_utils import run_bass_kernel_spmd as _run

    nc = _bacc.Bacc("TRN2", target_bir_lowering=False, num_devices=1)
    arrays, args = {}, {}
    for name in _INS:
        a = _np.ascontiguousarray(inputs[name])
        arrays[f"in_{name}_dram"] = a
        args[name] = nc.dram_tensor(f"in_{name}_dram", a.shape, _mybir.dt.from_np(a.dtype), kind="ExternalInput").ap()
    out = nc.dram_tensor("out_0_dram", (N, D), F32, kind="ExternalOutput").ap()
    A = [args[n] for n in _INS]
    build(nc, A[0], A[1], A[2], A[3], A[4], A[5], A[6], A[7], A[8], A[9], A[10], A[11], A[12], A[13], A[14:], out)
    r = _run(nc, [arrays], core_ids=[0])
    return r.results[0]["out_0_dram"]
```
